# Optimizing a Trainium2 kernel written in Bass

```python
import numpy as np
import jax
import jax.numpy as jnp

def _softmax(x, axis=-1):
    return jax.nn.softmax(x, axis=axis)

def _gelu(x):
    return jax.nn.gelu(x, approximate=True)

def _silu(x):
    return jax.nn.silu(x)

def _sigmoid(x):
    return jax.nn.sigmoid(x)

def _layernorm(x, axis=-1, eps=1e-05):
    m = jnp.mean(x, axis=axis, keepdims=True)
    v = jnp.var(x, axis=axis, keepdims=True)
    return (x - m) / jnp.sqrt(v + eps)

def _scatter_add(tgt, idx, src, axis=0):
    return tgt.at[idx].add(src)

def _segment_sum(src, seg, n):
    return jax.ops.segment_sum(src, seg, n)
kernel_name = 'mk_macaron_d4_jaxref_r8_2a4abe'

def setup_inputs(seed: int=0):
    np.random.seed(seed)
    _w = jnp.asarray

    def _L0_attn_setup():
        import jax, jax.numpy as jnp
        import numpy as np

        def _sin_rpe(Lq, d_model, dtype):
            inv_freq = 1.0 / 10000.0 ** (jnp.arange(0, d_model, 2, dtype=jnp.float32) / d_model)
            pos = jnp.arange(-(Lq - 1), Lq, dtype=jnp.float32)
            ang = pos[:, None] * inv_freq[None, :]
            emb = jnp.zeros((2 * Lq - 1, d_model), dtype=jnp.float32)
            emb = emb.at[:, 0::2].set(jnp.sin(ang)).at[:, 1::2].set(jnp.cos(ang))
            return emb.astype(dtype)

        def _rel_shift(x):
            B, H, Lq, Lr = x.shape
            xp = jnp.concatenate([jnp.zeros((B, H, Lq, 1), x.dtype), x], axis=-1)
            xp = xp.reshape(B, H, Lr + 1, Lq)
            return xp[:, :, 1:].reshape(B, H, Lq, Lr)[..., Lr - Lq:]
        key = jax.random.key(seed)
        ks = jax.random.split(key, 7)
        B, Lq, D, H = (1, 256, 128, 16)
        d_head = D // H
        s = 0.02
        return {'w': jax.random.normal(ks[0], (B, Lq, D), jnp.float32), 'Wq': jax.random.normal(ks[1], (D, D), jnp.float32) * s, 'Wk': jax.random.normal(ks[2], (D, D), jnp.float32) * s, 'Wv': jax.random.normal(ks[3], (D, D), jnp.float32) * s, 'Wr': jax.random.normal(ks[4], (D, D), jnp.float32) * s, 'u_bias': jax.random.normal(ks[5], (H, d_head), jnp.float32) * 0.02, 'v_bias': jax.random.normal(ks[6], (H, d_head), jnp.float32) * 0.02}
    _L0_attn_in = _L0_attn_setup()

    def _L0_ffn_setup():
        import jax, jax.numpy as jnp
        import numpy as np
        B, S, H = (2, 128, 128)
        KD, NH, K = (128, 8, 8)
        NE = 8192
        NK = 32
        EPS = 1e-05
        key = jax.random.key(seed)
        ks = jax.random.split(key, 5)
        inputs = jax.random.normal(ks[0], (B, S, H), jnp.float32)
        bn_gamma = jnp.ones((H,), jnp.float32)
        bn_beta = jnp.zeros((H,), jnp.float32)
        w_q = jax.random.normal(ks[1], (2 * NH * KD, H), jnp.float32) * (1.0 / np.sqrt(H))
        keys_p = jax.random.normal(ks[2], (NH, NK, 2, KD), jnp.float32) * 0.02
        lim = float(np.sqrt(6.0 / (NE + H)))
        down = jax.random.uniform(ks[3], (NE, H), jnp.float32, -lim, lim)
        up = jax.random.uniform(ks[4], (NE, H), jnp.float32, -lim, lim)
        return {'inputs': inputs, 'bn_gamma': bn_gamma, 'bn_beta': bn_beta, 'w_q': w_q, 'keys_p': keys_p, 'down': down, 'up': up}
    _L0_ffn_in = _L0_ffn_setup()

    def _L1_attn_setup():
        import jax, jax.numpy as jnp
        import numpy as np
        D_MODEL = 128
        NUM_HEADS = 16
        HEAD_DIM = D_MODEL // NUM_HEADS
        ROPE_THETA = 10000.0

        def apply_rope(x):
            S, d_k = (x.shape[-2], x.shape[-1])
            inv_freq = ROPE_THETA ** (jnp.arange(0, d_k, 2, dtype=jnp.float32) / d_k)
            ang = jnp.arange(S, dtype=jnp.float32)[:, None] / inv_freq[None, :]
            cos, sin = (jnp.cos(ang), jnp.sin(ang))
            xp = x.reshape(x.shape[:-1] + (d_k // 2, 2))
            x0, x1 = (xp[..., 0], xp[..., 1])
            out = jnp.stack([x0 * cos - x1 * sin, x0 * sin + x1 * cos], axis=-1)
            return out.reshape(x.shape)
        key = jax.random.key(seed)
        k1, k2, k3 = jax.random.split(key, 3)
        B, S = (2, 256)
        std = 2.0 / (D_MODEL + 3 * D_MODEL)
        std_o = 2.0 / (D_MODEL + D_MODEL)
        return {'x': jax.random.normal(k1, (B, S, D_MODEL), dtype=jnp.float32), 'W_qkv': jax.random.normal(k2, (3 * D_MODEL, D_MODEL), dtype=jnp.float32) * std, 'W_o': jax.random.normal(k3, (D_MODEL, D_MODEL), dtype=jnp.float32) * std_o}
    _L1_attn_in = _L1_attn_setup()

    def _L1_ffn_setup():
        import jax, jax.numpy as jnp
        import numpy as np
        DIM = 128
        DEPTH = 2
        HEADS = 8
        DIM_HEAD = 64
        WINDOW = 64
        INNER = HEADS * DIM_HEAD
        HID = int(DIM * 4 * 2 / 3)
        B, N = (2, 1024)
        QK_SCALE = 8.0

        def shift_token(t):
            t1, t2 = jnp.split(t, 2, axis=-1)
            t2 = jnp.pad(t2, ((0, 0), (1, 0), (0, 0)))[:, :-1]
            return jnp.concatenate([t1, t2], axis=-1)

        def l2norm(t):
            return t / jnp.clip(jnp.linalg.norm(t, axis=-1, keepdims=True), 1e-12)

        def rotate_half(x):
            x1, x2 = jnp.split(x, 2, axis=-1)
            return jnp.concatenate([-x2, x1], axis=-1)

        def rotary_xpos(q, k):
            n = q.shape[-2]
            half_idx = jnp.arange(0, DIM_HEAD, 2, dtype=jnp.float32)
            inv_freq = 1.0 / 10000.0 ** (half_idx / DIM_HEAD)
            t = jnp.arange(n, dtype=jnp.float32)
            freqs = t[:, None] * inv_freq[None, :]
            freqs = jnp.concatenate([freqs, freqs], axis=-1)
            base = (half_idx + 0.4 * DIM_HEAD) / (1.4 * DIM_HEAD)
            power = (t - n // 2) / float(WINDOW // 2)
            scale = base[None, :] ** power[:, None]
            scale = jnp.concatenate([scale, scale], axis=-1)
            cos, sin = (jnp.cos(freqs), jnp.sin(freqs))
            q = q * cos * scale + rotate_half(q) * sin * scale
            k = k * cos / scale + rotate_half(k) * sin / scale
            return (q, k)

        def local_attention(q, k, v):
            b, h, n, d = q.shape
            w = n // WINDOW
            bq = q.reshape(b, h, w, WINDOW, d) * QK_SCALE
            bk = k.reshape(b, h, w, WINDOW, d)
            bv = v.reshape(b, h, w, WINDOW, d)

            def look_around(t):
                p = jnp.pad(t, ((0, 0), (0, 0), (1, 0), (0, 0), (0, 0)))
                return jnp.concatenate([p[:, :, :w], p[:, :, 1:]], axis=3)
            bk, bv = (look_around(bk), look_around(bv))
            bt = jnp.arange(n).reshape(w, WINDOW)
            btp = jnp.pad(bt, ((1, 0), (0, 0)), constant_values=-1)
            btk = jnp.concatenate([btp[:w], btp[1:]], axis=1)
            sim = jnp.einsum('bhwid,bhwjd->bhwij', bq, bk)
            i = bt[:, :, None]
            j = btk[:, None, :]
            mask = (i < j) | (i > j + WINDOW) | (j == -1)
            sim = jnp.where(mask, -jnp.finfo(sim.dtype).max, sim)
            attn = jax.nn.softmax(sim, axis=-1)
            out = jnp.einsum('bhwij,bhwjd->bhwid', attn, bv)
            return out.reshape(b, h, n, d)

        def _layer(x, wqkv, qs, ksc, wo, lg, lb, w1, b1, w2, b2):
            b, n, _ = x.shape
            h = shift_token(x)
            qkv = h @ wqkv
            q, k, v = jnp.split(qkv, 3, axis=-1)
            to_heads = lambda t: t.reshape(b, n, HEADS, DIM_HEAD).transpose(0, 2, 1, 3)
            q, k, v = (to_heads(q), to_heads(k), to_heads(v))
            q = l2norm(q) * qs
            k = l2norm(k) * ksc
            q, k = rotary_xpos(q, k)
            o = local_attention(q, k, v)
            o = o.transpose(0, 2, 1, 3).reshape(b, n, INNER)
            x = x + o @ wo
            h = shift_token(x)
            mu = h.mean(-1, keepdims=True)
            var = h.var(-1, keepdims=True)
            h = (h - mu) / jnp.sqrt(var + 1e-05) * lg + lb
            h = h @ w1 + b1
            a, g = jnp.split(h, 2, axis=-1)
            h = a * jax.nn.gelu(g, approximate=False)
            x = x + h @ w2 + b2
            return x
        key = jax.random.key(seed)
        ks = jax.random.split(key, 6)
        return {'x': jax.random.normal(ks[0], (B, N, DIM), jnp.float32), 'wqkv': jax.random.normal(ks[1], (DEPTH, DIM, 3 * INNER), jnp.float32) * 0.02, 'q_scale': jnp.ones((DEPTH, DIM_HEAD), jnp.float32), 'k_scale': jnp.ones((DEPTH, DIM_HEAD), jnp.float32), 'wo': jax.random.normal(ks[2], (DEPTH, INNER, DIM), jnp.float32) * 0.02, 'ln_g': jnp.ones((DEPTH, DIM), jnp.float32), 'ln_b': jnp.zeros((DEPTH, DIM), jnp.float32), 'w1': jax.random.normal(ks[3], (DEPTH, DIM, 2 * HID), jnp.float32) * 0.02, 'b1': jnp.zeros((DEPTH, 2 * HID), jnp.float32), 'w2': jax.random.normal(ks[4], (DEPTH, HID, DIM), jnp.float32) * 0.02, 'b2': jnp.zeros((DEPTH, DIM), jnp.float32)}
    _L1_ffn_in = _L1_ffn_setup()

    def _L2_attn_setup():
        import math
        import jax, jax.numpy as jnp
        import numpy as np
        D, DK, DV = (128, 128, 128)
        B, S = (4, 256)
        key = jax.random.key(seed)
        ks = jax.random.split(key, 4)
        std_qk = math.sqrt(2.0 / (D + DK))
        std_v = math.sqrt(2.0 / (D + DV))
        return {'X': jax.random.normal(ks[0], (B, S, D), dtype=jnp.float32), 'W_q': jax.random.normal(ks[1], (D, DK), dtype=jnp.float32) * std_qk, 'W_k': jax.random.normal(ks[2], (D, DK), dtype=jnp.float32) * std_qk, 'W_v': jax.random.normal(ks[3], (D, DV), dtype=jnp.float32) * std_v, 'b_q': jnp.zeros((DK,), dtype=jnp.float32), 'b_k': jnp.zeros((DK,), dtype=jnp.float32), 'b_v': jnp.zeros((DV,), dtype=jnp.float32)}
    _L2_attn_in = _L2_attn_setup()

    def _L2_ffn_setup():
        import jax, jax.numpy as jnp
        import numpy as np
        B, S, H = (2, 64, 128)
        E, I = (64, 64)
        K = 8
        G, TG = (8, 4)
        SCALE = 2.5
        T = B * S
        CAP = 64

        def _moe_forward(x, router_w, gate_w, up_w, down_w, shared_gate_w, shared_up_w, shared_down_w):
            b, s, h = x.shape
            tokens = x.reshape(-1, h)
            t = tokens.shape[0]
            logits = tokens @ router_w
            scores = jax.nn.sigmoid(logits)
            eg = E // G
            group_scores = scores.reshape(t, G, eg).max(axis=-1)
            _, sel_groups = jax.lax.top_k(group_scores, TG)
            group_mask = jnp.zeros((t, G), bool).at[jnp.arange(t)[:, None], sel_groups].set(True)
            expert_mask = jnp.repeat(group_mask, eg, axis=1)
            masked_scores = jnp.where(expert_mask, scores, 0.0)
            topk_w, topk_idx = jax.lax.top_k(masked_scores, K)
            topk_w = topk_w / jnp.clip(topk_w.sum(-1, keepdims=True), 1e-09)
            topk_w = topk_w * SCALE
            flat_e = topk_idx.reshape(-1)
            onehot = jax.nn.one_hot(flat_e, E, dtype=jnp.int32)
            prior = jnp.cumsum(onehot, axis=0) - onehot
            pos = jnp.take_along_axis(prior, flat_e[:, None], axis=1)[:, 0]
            valid = (pos < CAP).astype(tokens.dtype)
            pos_c = jnp.minimum(pos, CAP - 1)
            tidx = jnp.repeat(jnp.arange(t), K)
            dispatch = jnp.zeros((E, CAP, h), tokens.dtype)
            dispatch = dispatch.at[flat_e, pos_c].add(tokens[tidx] * valid[:, None])
            g = jnp.einsum('ech,ehi->eci', dispatch, gate_w)
            u = jnp.einsum('ech,ehi->eci', dispatch, up_w)
            expert_out = jnp.einsum('eci,eih->ech', jax.nn.silu(g) * u, down_w)
            gathered = expert_out[flat_e, pos_c]
            contrib = gathered * (topk_w.reshape(-1) * valid)[:, None]
            output = jnp.zeros((t, h), tokens.dtype).at[tidx].add(contrib)
            sg = jax.nn.silu(tokens @ shared_gate_w) * (tokens @ shared_up_w)
            output = output + sg @ shared_down_w
            return output.reshape(b, s, h)
        key = jax.random.key(seed)
        ks = jax.random.split(key, 9)
        s_h = 1.0 / np.sqrt(H)
        s_i = 1.0 / np.sqrt(I)
        return {'x': jax.random.normal(ks[0], (B, S, H), jnp.float32), 'router_w': jax.random.normal(ks[1], (H, E), jnp.float32) * s_h, 'gate_w': jax.random.normal(ks[2], (E, H, I), jnp.float32) * s_h, 'up_w': jax.random.normal(ks[3], (E, H, I), jnp.float32) * s_h, 'down_w': jax.random.normal(ks[4], (E, I, H), jnp.float32) * s_i, 'shared_gate_w': jax.random.normal(ks[5], (H, I), jnp.float32) * s_h, 'shared_up_w': jax.random.normal(ks[6], (H, I), jnp.float32) * s_h, 'shared_down_w': jax.random.normal(ks[7], (I, H), jnp.float32) * s_i}
    _L2_ffn_in = _L2_ffn_setup()

    def _L3_attn_setup():
        import jax, jax.numpy as jnp
        import numpy as np
        import math
        N_HEAD = 16
        N_LATENTS = 64
        CHUNK = 128
        ROPE_THETA = 10000.0

        def _rope_cos_sin(T, D, theta):
            inv = 1.0 / theta ** (jnp.arange(0, D, 2, dtype=jnp.float32) / D)
            ang = jnp.arange(T, dtype=jnp.float32)[:, None] * inv[None, :]
            return (jnp.cos(ang), jnp.sin(ang))

        def _apply_rope(k, cos, sin):
            B, T, H, D = k.shape
            kr = k.reshape(B, T, H, D // 2, 2)
            a, b = (kr[..., 0], kr[..., 1])
            c = cos[None, :, None, :]
            s = sin[None, :, None, :]
            out = jnp.stack([a * c - b * s, a * s + b * c], axis=-1)
            return out.reshape(B, T, H, D).astype(k.dtype)
        key = jax.random.key(seed)
        ks = jax.random.split(key, 6)
        B, T, C = (8, 512, 128)
        H, L = (N_HEAD, N_LATENTS)
        D = C // H
        std_in = 1.0 / math.sqrt(C)
        return {'x': jax.random.normal(ks[0], (B, T, C), jnp.float32), 'latent_queries': jax.random.normal(ks[1], (1, L, H, D), jnp.float32) * (1.0 / math.sqrt(D)), 'W_k': jax.random.normal(ks[2], (C, C), jnp.float32) * std_in, 'W_v': jax.random.normal(ks[3], (C, C), jnp.float32) * std_in, 'W_g': jax.random.normal(ks[4], (H * L, C), jnp.float32) * std_in, 'W_p': jax.random.normal(ks[5], (C, C), jnp.float32) * std_in}
    _L3_attn_in = _L3_attn_setup()

    def _L3_ffn_setup():
        import jax, jax.numpy as jnp
        import numpy as np
        DIM = 128
        HIDDEN = 384
        SCALE = 1.0 / 127.0

        def _dequant(w_int, dtype):
            return w_int.astype(dtype) * jnp.asarray(SCALE, dtype)
        key = jax.random.key(seed)
        k_x, k_g, k_u, k_d = jax.random.split(key, 4)
        x = jax.random.normal(k_x, (4, 256, DIM), dtype=jnp.float32)
        w_gate = jax.random.randint(k_g, (HIDDEN, DIM), -127, 128, dtype=jnp.int32)
        w_up = jax.random.randint(k_u, (HIDDEN, DIM), -127, 128, dtype=jnp.int32)
        w_down = jax.random.randint(k_d, (DIM, HIDDEN), -127, 128, dtype=jnp.int32)
        return {'x': x, 'w_gate': w_gate, 'w_up': w_up, 'w_down': w_down}
    _L3_ffn_in = _L3_ffn_setup()
    _d = {'L0_attn_w': _L0_attn_in['w'], 'L0_attn_Wq': _L0_attn_in['Wq'], 'L0_attn_Wk': _L0_attn_in['Wk'], 'L0_attn_Wv': _L0_attn_in['Wv'], 'L0_attn_Wr': _L0_attn_in['Wr'], 'L0_attn_u_bias': _L0_attn_in['u_bias'], 'L0_attn_v_bias': _L0_attn_in['v_bias'], 'L0_ffn_bn_gamma': _L0_ffn_in['bn_gamma'], 'L0_ffn_bn_beta': _L0_ffn_in['bn_beta'], 'L0_ffn_w_q': _L0_ffn_in['w_q'], 'L0_ffn_keys_p': _L0_ffn_in['keys_p'], 'L0_ffn_down': _L0_ffn_in['down'], 'L0_ffn_up': _L0_ffn_in['up'], 'L1_attn_W_qkv': _L1_attn_in['W_qkv'], 'L1_attn_W_o': _L1_attn_in['W_o'], 'L1_ffn_wqkv': _L1_ffn_in['wqkv'], 'L1_ffn_q_scale': _L1_ffn_in['q_scale'], 'L1_ffn_k_scale': _L1_ffn_in['k_scale'], 'L1_ffn_wo': _L1_ffn_in['wo'], 'L1_ffn_ln_g': _L1_ffn_in['ln_g'], 'L1_ffn_ln_b': _L1_ffn_in['ln_b'], 'L1_ffn_w1': _L1_ffn_in['w1'], 'L1_ffn_b1': _L1_ffn_in['b1'], 'L1_ffn_w2': _L1_ffn_in['w2'], 'L1_ffn_b2': _L1_ffn_in['b2'], 'L2_attn_W_q': _L2_attn_in['W_q'], 'L2_attn_W_k': _L2_attn_in['W_k'], 'L2_attn_W_v': _L2_attn_in['W_v'], 'L2_attn_b_q': _L2_attn_in['b_q'], 'L2_attn_b_k': _L2_attn_in['b_k'], 'L2_attn_b_v': _L2_attn_in['b_v'], 'L2_ffn_router_w': _L2_ffn_in['router_w'], 'L2_ffn_gate_w': _L2_ffn_in['gate_w'], 'L2_ffn_up_w': _L2_ffn_in['up_w'], 'L2_ffn_down_w': _L2_ffn_in['down_w'], 'L2_ffn_shared_gate_w': _L2_ffn_in['shared_gate_w'], 'L2_ffn_shared_up_w': _L2_ffn_in['shared_up_w'], 'L2_ffn_shared_down_w': _L2_ffn_in['shared_down_w'], 'L3_attn_latent_queries': _L3_attn_in['latent_queries'], 'L3_attn_W_k': _L3_attn_in['W_k'], 'L3_attn_W_v': _L3_attn_in['W_v'], 'L3_attn_W_g': _L3_attn_in['W_g'], 'L3_attn_W_p': _L3_attn_in['W_p'], 'L3_ffn_w_gate': _L3_ffn_in['w_gate'], 'L3_ffn_w_up': _L3_ffn_in['w_up'], 'L3_ffn_w_down': _L3_ffn_in['w_down']}
    _x0 = _d['L0_attn_w']
    _d['L0_attn_w'] = jax.random.normal(jax.random.fold_in(jax.random.key(seed), 1), (16, 256, 128), dtype=_x0.dtype)
    del _x0
    return _d

def reference(L0_attn_w, L0_attn_Wq, L0_attn_Wk, L0_attn_Wv, L0_attn_Wr, L0_attn_u_bias, L0_attn_v_bias, L0_ffn_bn_gamma, L0_ffn_bn_beta, L0_ffn_w_q, L0_ffn_keys_p, L0_ffn_down, L0_ffn_up, L1_attn_W_qkv, L1_attn_W_o, L1_ffn_wqkv, L1_ffn_q_scale, L1_ffn_k_scale, L1_ffn_wo, L1_ffn_ln_g, L1_ffn_ln_b, L1_ffn_w1, L1_ffn_b1, L1_ffn_w2, L1_ffn_b2, L2_attn_W_q, L2_attn_W_k, L2_attn_W_v, L2_attn_b_q, L2_attn_b_k, L2_attn_b_v, L2_ffn_router_w, L2_ffn_gate_w, L2_ffn_up_w, L2_ffn_down_w, L2_ffn_shared_gate_w, L2_ffn_shared_up_w, L2_ffn_shared_down_w, L3_attn_latent_queries, L3_attn_W_k, L3_attn_W_v, L3_attn_W_g, L3_attn_W_p, L3_ffn_w_gate, L3_ffn_w_up, L3_ffn_w_down):

    def _L0_attn_ref(w, Wq, Wk, Wv, Wr, u_bias, v_bias):
        import jax, jax.numpy as jnp
        import numpy as np

        def _sin_rpe(Lq, d_model, dtype):
            inv_freq = 1.0 / 10000.0 ** (jnp.arange(0, d_model, 2, dtype=jnp.float32) / d_model)
            pos = jnp.arange(-(Lq - 1), Lq, dtype=jnp.float32)
            ang = pos[:, None] * inv_freq[None, :]
            emb = jnp.zeros((2 * Lq - 1, d_model), dtype=jnp.float32)
            emb = emb.at[:, 0::2].set(jnp.sin(ang)).at[:, 1::2].set(jnp.cos(ang))
            return emb.astype(dtype)

        def _rel_shift(x):
            B, H, Lq, Lr = x.shape
            xp = jnp.concatenate([jnp.zeros((B, H, Lq, 1), x.dtype), x], axis=-1)
            xp = xp.reshape(B, H, Lr + 1, Lq)
            return xp[:, :, 1:].reshape(B, H, Lq, Lr)[..., Lr - Lq:]
        B, Lq, D = w.shape
        H, d_head = u_bias.shape
        scale = 1.0 / np.sqrt(d_head).astype(np.float32)
        r = _sin_rpe(Lq, D, w.dtype)
        q = (w @ Wq.T).reshape(B, Lq, H, d_head).transpose(0, 2, 1, 3)
        k = (w @ Wk.T).reshape(B, Lq, H, d_head).transpose(0, 2, 1, 3)
        v = (w @ Wv.T).reshape(B, Lq, H, d_head).transpose(0, 2, 1, 3)
        rp = (r @ Wr.T).reshape(2 * Lq - 1, H, d_head).transpose(1, 0, 2)
        AC = jnp.einsum('bhid,bhjd->bhij', q + u_bias[None, :, None, :], k)
        BD = jnp.einsum('bhid,hjd->bhij', q + v_bias[None, :, None, :], rp)
        BD = _rel_shift(BD)
        attn = jax.nn.softmax((AC + BD) * scale, axis=-1)
        out = jnp.einsum('bhij,bhjd->bhid', attn, v)
        return out.transpose(0, 2, 1, 3).reshape(B, Lq, D)

    def _L0_ffn_ref(inputs, bn_gamma, bn_beta, w_q, keys_p, down, up):
        import jax, jax.numpy as jnp
        import numpy as np
        B, S, H = (2, 128, 128)
        KD, NH, K = (128, 8, 8)
        NE = 8192
        NK = 32
        EPS = 1e-05
        b, s, d = inputs.shape
        x = inputs.reshape(b * s, d)
        mean = x.mean(axis=0)
        var = x.var(axis=0)
        xn = (x - mean) * jax.lax.rsqrt(var + EPS) * bn_gamma + bn_beta
        xn = xn.reshape(b, s, d)
        q = (xn @ w_q.T).reshape(b, s, 2, NH, KD).transpose(2, 0, 1, 3, 4)
        sim = jnp.einsum('pbnhd,hkpd->pbnhk', q, keys_p)
        scores, idx = jax.lax.top_k(sim, K)
        all_scores = (scores[0][..., :, None] + scores[1][..., None, :]).reshape(b, s, NH, K * K)
        all_idx = (idx[0][..., :, None] * NK + idx[1][..., None, :]).reshape(b, s, NH, K * K)
        sc, pk = jax.lax.top_k(all_scores, K)
        indices = jnp.take_along_axis(all_idx, pk, axis=-1)
        wd = down[indices]
        hmid = jnp.einsum('bnd,bnhkd->bnhk', inputs, wd)
        hmid = jax.nn.sigmoid(sc) * jax.nn.gelu(hmid, approximate=False)
        wu = up[indices]
        return jnp.einsum('bnhk,bnhkd->bnd', hmid, wu)

    def _L1_attn_ref(x, W_qkv, W_o):
        import jax, jax.numpy as jnp
        import numpy as np
        D_MODEL = 128
        NUM_HEADS = 16
        HEAD_DIM = D_MODEL // NUM_HEADS
        ROPE_THETA = 10000.0

        def apply_rope(x):
            S, d_k = (x.shape[-2], x.shape[-1])
            inv_freq = ROPE_THETA ** (jnp.arange(0, d_k, 2, dtype=jnp.float32) / d_k)
            ang = jnp.arange(S, dtype=jnp.float32)[:, None] / inv_freq[None, :]
            cos, sin = (jnp.cos(ang), jnp.sin(ang))
            xp = x.reshape(x.shape[:-1] + (d_k // 2, 2))
            x0, x1 = (xp[..., 0], xp[..., 1])
            out = jnp.stack([x0 * cos - x1 * sin, x0 * sin + x1 * cos], axis=-1)
            return out.reshape(x.shape)
        B, S, d_model = x.shape
        H, d_k = (NUM_HEADS, HEAD_DIM)
        qkv = jnp.einsum('bsi,oi->bso', x, W_qkv)
        Q, K, V = jnp.split(qkv, 3, axis=-1)

        def to_heads(t):
            return t.reshape(B, S, H, d_k).transpose(0, 2, 1, 3)
        Q, K, V = (to_heads(Q), to_heads(K), to_heads(V))
        Q, K = (apply_rope(Q), apply_rope(K))
        scores = jnp.einsum('bhqd,bhkd->bhqk', Q, K) / jnp.sqrt(jnp.float32(d_k))
        causal = jnp.tril(jnp.ones((S, S), dtype=bool))
        scores = jnp.where(causal, scores, -jnp.inf)
        attn = jax.nn.softmax(scores, axis=-1)
        out = jnp.einsum('bhqk,bhkd->bhqd', attn, V)
        out = out.transpose(0, 2, 1, 3).reshape(B, S, d_model)
        return jnp.einsum('bsi,oi->bso', out, W_o)

    def _L1_ffn_ref(x, wqkv, q_scale, k_scale, wo, ln_g, ln_b, w1, b1, w2, b2):
        import jax, jax.numpy as jnp
        import numpy as np
        DIM = 128
        DEPTH = 2
        HEADS = 8
        DIM_HEAD = 64
        WINDOW = 64
        INNER = HEADS * DIM_HEAD
        HID = int(DIM * 4 * 2 / 3)
        B, N = (2, 1024)
        QK_SCALE = 8.0

        def shift_token(t):
            t1, t2 = jnp.split(t, 2, axis=-1)
            t2 = jnp.pad(t2, ((0, 0), (1, 0), (0, 0)))[:, :-1]
            return jnp.concatenate([t1, t2], axis=-1)

        def l2norm(t):
            return t / jnp.clip(jnp.linalg.norm(t, axis=-1, keepdims=True), 1e-12)

        def rotate_half(x):
            x1, x2 = jnp.split(x, 2, axis=-1)
            return jnp.concatenate([-x2, x1], axis=-1)

        def rotary_xpos(q, k):
            n = q.shape[-2]
            half_idx = jnp.arange(0, DIM_HEAD, 2, dtype=jnp.float32)
            inv_freq = 1.0 / 10000.0 ** (half_idx / DIM_HEAD)
            t = jnp.arange(n, dtype=jnp.float32)
            freqs = t[:, None] * inv_freq[None, :]
            freqs = jnp.concatenate([freqs, freqs], axis=-1)
            base = (half_idx + 0.4 * DIM_HEAD) / (1.4 * DIM_HEAD)
            power = (t - n // 2) / float(WINDOW // 2)
            scale = base[None, :] ** power[:, None]
            scale = jnp.concatenate([scale, scale], axis=-1)
            cos, sin = (jnp.cos(freqs), jnp.sin(freqs))
            q = q * cos * scale + rotate_half(q) * sin * scale
            k = k * cos / scale + rotate_half(k) * sin / scale
            return (q, k)

        def local_attention(q, k, v):
            b, h, n, d = q.shape
            w = n // WINDOW
            bq = q.reshape(b, h, w, WINDOW, d) * QK_SCALE
            bk = k.reshape(b, h, w, WINDOW, d)
            bv = v.reshape(b, h, w, WINDOW, d)

            def look_around(t):
                p = jnp.pad(t, ((0, 0), (0, 0), (1, 0), (0, 0), (0, 0)))
                return jnp.concatenate([p[:, :, :w], p[:, :, 1:]], axis=3)
            bk, bv = (look_around(bk), look_around(bv))
            bt = jnp.arange(n).reshape(w, WINDOW)
            btp = jnp.pad(bt, ((1, 0), (0, 0)), constant_values=-1)
            btk = jnp.concatenate([btp[:w], btp[1:]], axis=1)
            sim = jnp.einsum('bhwid,bhwjd->bhwij', bq, bk)
            i = bt[:, :, None]
            j = btk[:, None, :]
            mask = (i < j) | (i > j + WINDOW) | (j == -1)
            sim = jnp.where(mask, -jnp.finfo(sim.dtype).max, sim)
            attn = jax.nn.softmax(sim, axis=-1)
            out = jnp.einsum('bhwij,bhwjd->bhwid', attn, bv)
            return out.reshape(b, h, n, d)

        def _layer(x, wqkv, qs, ksc, wo, lg, lb, w1, b1, w2, b2):
            b, n, _ = x.shape
            h = shift_token(x)
            qkv = h @ wqkv
            q, k, v = jnp.split(qkv, 3, axis=-1)
            to_heads = lambda t: t.reshape(b, n, HEADS, DIM_HEAD).transpose(0, 2, 1, 3)
            q, k, v = (to_heads(q), to_heads(k), to_heads(v))
            q = l2norm(q) * qs
            k = l2norm(k) * ksc
            q, k = rotary_xpos(q, k)
            o = local_attention(q, k, v)
            o = o.transpose(0, 2, 1, 3).reshape(b, n, INNER)
            x = x + o @ wo
            h = shift_token(x)
            mu = h.mean(-1, keepdims=True)
            var = h.var(-1, keepdims=True)
            h = (h - mu) / jnp.sqrt(var + 1e-05) * lg + lb
            h = h @ w1 + b1
            a, g = jnp.split(h, 2, axis=-1)
            h = a * jax.nn.gelu(g, approximate=False)
            x = x + h @ w2 + b2
            return x
        for l in range(DEPTH):
            x = _layer(x, wqkv[l], q_scale[l], k_scale[l], wo[l], ln_g[l], ln_b[l], w1[l], b1[l], w2[l], b2[l])
        return x

    def _L2_attn_ref(X, W_q, W_k, W_v, b_q, b_k, b_v):
        import math
        import jax, jax.numpy as jnp
        import numpy as np
        D, DK, DV = (128, 128, 128)
        B, S = (4, 256)
        scale = 1.0 / math.sqrt(DK)
        Q = X @ W_q + b_q
        K = X @ W_k + b_k
        V = X @ W_v + b_v
        A = jnp.einsum('bsd,btd->bst', Q, K) * scale
        A = jax.nn.softmax(A, axis=2)
        return jnp.einsum('bst,btv->bsv', A, V)

    def _L2_ffn_ref(x, router_w, gate_w, up_w, down_w, shared_gate_w, shared_up_w, shared_down_w):
        import jax, jax.numpy as jnp
        import numpy as np
        B, S, H = (2, 64, 128)
        E, I = (64, 64)
        K = 8
        G, TG = (8, 4)
        SCALE = 2.5
        T = B * S
        CAP = 64

        def _moe_forward(x, router_w, gate_w, up_w, down_w, shared_gate_w, shared_up_w, shared_down_w):
            b, s, h = x.shape
            tokens = x.reshape(-1, h)
            t = tokens.shape[0]
            logits = tokens @ router_w
            scores = jax.nn.sigmoid(logits)
            eg = E // G
            group_scores = scores.reshape(t, G, eg).max(axis=-1)
            _, sel_groups = jax.lax.top_k(group_scores, TG)
            group_mask = jnp.zeros((t, G), bool).at[jnp.arange(t)[:, None], sel_groups].set(True)
            expert_mask = jnp.repeat(group_mask, eg, axis=1)
            masked_scores = jnp.where(expert_mask, scores, 0.0)
            topk_w, topk_idx = jax.lax.top_k(masked_scores, K)
            topk_w = topk_w / jnp.clip(topk_w.sum(-1, keepdims=True), 1e-09)
            topk_w = topk_w * SCALE
            flat_e = topk_idx.reshape(-1)
            onehot = jax.nn.one_hot(flat_e, E, dtype=jnp.int32)
            prior = jnp.cumsum(onehot, axis=0) - onehot
            pos = jnp.take_along_axis(prior, flat_e[:, None], axis=1)[:, 0]
            valid = (pos < CAP).astype(tokens.dtype)
            pos_c = jnp.minimum(pos, CAP - 1)
            tidx = jnp.repeat(jnp.arange(t), K)
            dispatch = jnp.zeros((E, CAP, h), tokens.dtype)
            dispatch = dispatch.at[flat_e, pos_c].add(tokens[tidx] * valid[:, None])
            g = jnp.einsum('ech,ehi->eci', dispatch, gate_w)
            u = jnp.einsum('ech,ehi->eci', dispatch, up_w)
            expert_out = jnp.einsum('eci,eih->ech', jax.nn.silu(g) * u, down_w)
            gathered = expert_out[flat_e, pos_c]
            contrib = gathered * (topk_w.reshape(-1) * valid)[:, None]
            output = jnp.zeros((t, h), tokens.dtype).at[tidx].add(contrib)
            sg = jax.nn.silu(tokens @ shared_gate_w) * (tokens @ shared_up_w)
            output = output + sg @ shared_down_w
            return output.reshape(b, s, h)
        return _moe_forward(x, router_w, gate_w, up_w, down_w, shared_gate_w, shared_up_w, shared_down_w)

    def _L3_attn_ref(x, latent_queries, W_k, W_v, W_g, W_p):
        import jax, jax.numpy as jnp
        import numpy as np
        import math
        N_HEAD = 16
        N_LATENTS = 64
        CHUNK = 128
        ROPE_THETA = 10000.0

        def _rope_cos_sin(T, D, theta):
            inv = 1.0 / theta ** (jnp.arange(0, D, 2, dtype=jnp.float32) / D)
            ang = jnp.arange(T, dtype=jnp.float32)[:, None] * inv[None, :]
            return (jnp.cos(ang), jnp.sin(ang))

        def _apply_rope(k, cos, sin):
            B, T, H, D = k.shape
            kr = k.reshape(B, T, H, D // 2, 2)
            a, b = (kr[..., 0], kr[..., 1])
            c = cos[None, :, None, :]
            s = sin[None, :, None, :]
            out = jnp.stack([a * c - b * s, a * s + b * c], axis=-1)
            return out.reshape(B, T, H, D).astype(k.dtype)
        B, T, C = x.shape
        H, L, cs = (N_HEAD, N_LATENTS, CHUNK)
        D = C // H
        scale = 1.0 / math.sqrt(D)
        k = (x @ W_k.T).reshape(B, T, H, D)
        v = (x @ W_v.T).reshape(B, T, H, D)
        cos, sin = _rope_cos_sin(T, D, ROPE_THETA)
        k = _apply_rope(k, cos, sin)
        gates = jax.nn.softmax((x @ W_g.T).reshape(B, T, H, L) * scale, axis=-1)
        q = jnp.transpose(latent_queries, (0, 2, 1, 3))
        nc = T // cs
        kc = jnp.transpose(k, (0, 2, 1, 3)).reshape(B, H, nc, cs, D)
        vc = jnp.transpose(v, (0, 2, 1, 3)).reshape(B, H, nc, cs, D)
        scores = jnp.einsum('zhld,bhncd->bhnlc', q, kc) * scale
        causal = jnp.arange(cs)[None, :] <= jnp.arange(L)[:, None]
        scores = jnp.where(causal[None, None, None], scores, -jnp.inf)
        probs = jax.nn.softmax(scores, axis=-1)
        attn = jnp.einsum('bhnlc,bhncd->bhld', probs, vc)
        weighted = jnp.einsum('bhld,bthl->bthd', attn, gates)
        out = weighted.reshape(B, T, C) @ W_p.T
        return out

    def _L3_ffn_ref(x, w_gate, w_up, w_down):
        import jax, jax.numpy as jnp
        import numpy as np
        DIM = 128
        HIDDEN = 384
        SCALE = 1.0 / 127.0

        def _dequant(w_int, dtype):
            return w_int.astype(dtype) * jnp.asarray(SCALE, dtype)
        wg = _dequant(w_gate, x.dtype)
        wu = _dequant(w_up, x.dtype)
        wd = _dequant(w_down, x.dtype)
        gate = jnp.einsum('bsd,hd->bsh', x, wg)
        up = jnp.einsum('bsd,hd->bsh', x, wu)
        h = jax.nn.silu(gate) * up
        return jnp.einsum('bsh,dh->bsd', h, wd)
    x = L0_attn_w
    x = x + 0.5 * _L0_ffn_ref(_layernorm(x, axis=-1), L0_ffn_bn_gamma, L0_ffn_bn_beta, L0_ffn_w_q, L0_ffn_keys_p, L0_ffn_down, L0_ffn_up)
    x = x + _L0_attn_ref(_layernorm(x, axis=-1), L0_attn_Wq, L0_attn_Wk, L0_attn_Wv, L0_attn_Wr, L0_attn_u_bias, L0_attn_v_bias)
    x = x + 0.5 * _L0_ffn_ref(_layernorm(x, axis=-1), L0_ffn_bn_gamma, L0_ffn_bn_beta, L0_ffn_w_q, L0_ffn_keys_p, L0_ffn_down, L0_ffn_up)
    x = x + 0.5 * _L1_ffn_ref(_layernorm(x, axis=-1), L1_ffn_wqkv, L1_ffn_q_scale, L1_ffn_k_scale, L1_ffn_wo, L1_ffn_ln_g, L1_ffn_ln_b, L1_ffn_w1, L1_ffn_b1, L1_ffn_w2, L1_ffn_b2)
    x = x + _L1_attn_ref(_layernorm(x, axis=-1), L1_attn_W_qkv, L1_attn_W_o)
    x = x + 0.5 * _L1_ffn_ref(_layernorm(x, axis=-1), L1_ffn_wqkv, L1_ffn_q_scale, L1_ffn_k_scale, L1_ffn_wo, L1_ffn_ln_g, L1_ffn_ln_b, L1_ffn_w1, L1_ffn_b1, L1_ffn_w2, L1_ffn_b2)
    x = x + 0.5 * _L2_ffn_ref(_layernorm(x, axis=-1), L2_ffn_router_w, L2_ffn_gate_w, L2_ffn_up_w, L2_ffn_down_w, L2_ffn_shared_gate_w, L2_ffn_shared_up_w, L2_ffn_shared_down_w)
    x = x + _L2_attn_ref(_layernorm(x, axis=-1), L2_attn_W_q, L2_attn_W_k, L2_attn_W_v, L2_attn_b_q, L2_attn_b_k, L2_attn_b_v)
    x = x + 0.5 * _L2_ffn_ref(_layernorm(x, axis=-1), L2_ffn_router_w, L2_ffn_gate_w, L2_ffn_up_w, L2_ffn_down_w, L2_ffn_shared_gate_w, L2_ffn_shared_up_w, L2_ffn_shared_down_w)
    x = x + 0.5 * _L3_ffn_ref(_layernorm(x, axis=-1), L3_ffn_w_gate, L3_ffn_w_up, L3_ffn_w_down)
    x = x + _L3_attn_ref(_layernorm(x, axis=-1), L3_attn_latent_queries, L3_attn_W_k, L3_attn_W_v, L3_attn_W_g, L3_attn_W_p)
    x = x + 0.5 * _L3_ffn_ref(_layernorm(x, axis=-1), L3_ffn_w_gate, L3_ffn_w_up, L3_ffn_w_down)
    return x

_drawn_inputs = setup_inputs


def setup_inputs(seed=0):
    import zlib

    import numpy as np

    out = dict(_drawn_inputs(seed))
    spreads = {'L0_ffn_bn_gamma': (1.0, 0.6),
     'L0_ffn_bn_beta': (0.0, 0.506),
     'L1_ffn_q_scale': (1.0, 0.6),
     'L1_ffn_k_scale': (1.0, 0.6),
     'L1_ffn_ln_g': (1.0, 0.6),
     'L1_ffn_ln_b': (0.0, 0.8),
     'L1_ffn_b1': (0.0, 0.369),
     'L1_ffn_b2': (0.0, 0.1),
     'L2_attn_b_q': (0.0, 0.563),
     'L2_attn_b_k': (0.0, 0.8),
     'L2_attn_b_v': (0.0, 0.1)}
    factors = {'L0_attn_Wq': 5.991,
     'L0_attn_Wk': 5.899,
     'L0_attn_Wr': 8.0,
     'L0_attn_u_bias': 8.0,
     'L0_attn_v_bias': 8.0,
     'L1_attn_W_qkv': 8.0,
     'L1_attn_W_o': 8.0,
     'L3_attn_latent_queries': 8.0,
     'L3_attn_W_k': 8.0,
     'L3_attn_W_v': 8.0,
     'L3_attn_W_g': 8.0,
     'L3_attn_W_p': 8.0}
    for name, (base, spread) in spreads.items():
        noise = np.random.default_rng([zlib.crc32(name.encode()), seed]).standard_normal(out[name].shape)
        drawn = base * np.exp(spread * noise) if base else spread * noise
        out[name] = jnp.asarray(drawn.astype(out[name].dtype))
    for name, factor in factors.items():
        out[name] = (out[name] * factor).astype(out[name].dtype)
    return out
```

```python
from contextlib import ExitStack

import numpy as np

import concourse.bass as bass
from concourse import mybir

F32 = mybir.dt.float32
I32 = mybir.dt.int32
U32 = mybir.dt.uint32
ALU = mybir.AluOpType
ACT = mybir.ActivationFunctionType
AX = mybir.AxisListType.X
ds = bass.ds

P = 128
D = 128
NB = 16
L = 256
T = NB * L
NT = T // P
BLK = 512
NBLK = T // BLK
LN_EPS = 1e-5


class Phase:

    def __init__(self, nc, tag):
        self.nc, self.tag, self.sems, self.ctx = nc, tag, [], ExitStack()

    def __enter__(self):
        return self

    def sb(self, name, shape, dt=F32):
        return self.ctx.enter_context(self.nc.sbuf_tensor(f"{self.tag}_{name}", shape, dt))

    def ps(self, name, shape, dt=F32):
        return self.ctx.enter_context(self.nc.psum_tensor(f"{self.tag}_{name}", shape, dt))

    def sem(self, name):
        s = self.nc.alloc_semaphore(f"{self.tag}_{name}")
        self.sems.append(s)
        return s

    def __exit__(self, *exc):
        if exc[0] is None:
            self.nc.clear_and_free_semaphores(self.sems)
            self.nc.all_engine_barrier()
            self.ctx.close()
        return False


def constants():
    f = np.float32
    out = {}
    out["ones_mean"] = np.full((P, P), 1.0 / D, f)
    out["eye"] = np.eye(P, dtype=f)
    freq = (1.0 / 10000.0 ** (np.arange(0, D, 2, dtype=f) / f(D))).astype(f).astype(np.float64)
    j = np.arange(L, dtype=np.float64)

    def table(pos):
        a = freq[:, None] * pos[None, :]
        t = np.zeros((D, len(pos)))
        t[0::2], t[1::2] = np.sin(a), np.cos(a)
        return t.astype(f)

    out["rel_low"] = table(L - 1 + j)
    out["rel_up"] = table(j - L)
    a = freq[:, None] * j[None, :]
    turn = np.zeros((D, 2, L))
    turn[0::2, 0], turn[1::2, 0] = np.cos(a), np.cos(a)
    turn[0::2, 1], turn[1::2, 1] = np.sin(a), -np.sin(a)
    out["rel_turn"] = turn.astype(f)
    i, k = np.arange(P)[:, None], np.arange(P)[None, :]
    mask = np.zeros((P, 2, 2, P), f)
    mask[:, 0, 0], mask[:, 1, 0] = k <= i, k <= i
    mask[:, 0, 1] = (k + 1) >= i + 2
    mask[:, 1, 1] = k >= i + 2
    out["rel_mask"] = mask
    q = np.arange(P)[:, None, None] + P * np.arange(2)[None, :, None]
    kk = np.arange(L)[None, None, :]
    out["causal"] = np.where(kk <= q, 0.0, -1e30).astype(f)
    out["band"] = np.where((kk <= q) & (kk >= q - 64), 0.0, -1e30).astype(f)
    out["open"] = np.zeros((P, 2, L), f)

    def rope8(inv):
        ang = j[None, :] * inv[:, None]
        t = np.zeros((P, 2, L))
        for c in range(P):
            m = (c % 8) // 2
            t[c, 0] = np.cos(ang[m])
            t[c, 1] = np.sin(ang[m]) * (1 if c % 2 else -1)
        return t.astype(f)

    theta = (f(10000.0) ** (np.arange(0, 8, 2, dtype=f) / f(8))).astype(f)
    out["rope8"] = rope8(1.0 / theta.astype(np.float64))
    half = np.arange(0, 64, 2, dtype=f)
    inv = (1.0 / 10000.0 ** (half / f(64))).astype(f).astype(np.float64)
    base = ((half + 0.4 * 64) / (1.4 * 64)).astype(np.float64)
    power = (j - L // 2) / 32.0
    t = np.zeros((P, 2, 2, L))
    for c in range(P):
        m = (c % 64) % 32
        sign = -1 if (c % 64) < 32 else 1
        sc = base[m] ** power
        t[c, 0, 0], t[c, 0, 1] = np.cos(j * inv[m]) * sc, np.cos(j * inv[m]) / sc
        t[c, 1, 0], t[c, 1, 1] = sign * np.sin(j * inv[m]) * sc, sign * np.sin(j * inv[m]) / sc
    out["xpos"] = t.astype(f)
    out["block64"] = np.kron(np.eye(2), np.ones((64, 64))).astype(f)
    out["tri"] = (np.arange(P)[:, None] < np.arange(P)[None, :]).astype(f)
    out["ones"] = np.ones((P, P), f)
    out["slot"] = np.tile(np.arange(64, dtype=f), (P, 1))
    out["token"] = (np.arange(P, dtype=f)[:, None] + P * np.arange(NT, dtype=f)[None, :]).astype(f)
    out["lane"] = np.tile(np.arange(P, dtype=f), (P, 1))
    lat = np.arange(64)
    m = np.where(lat[None, :] <= lat[:, None], 0.0, -1e30)
    out["latent_mask"] = np.concatenate([m, m], 0).astype(f)
    own = np.zeros((P, 8, P), f)
    for pair in range(8):
        for s in range(2):
            own[64 * s:64 * s + 64, pair, (2 * pair + s) * 8:(2 * pair + s) * 8 + 8] = 1
    out["own_head"] = own
    return out


def load(eng, dst, src, sem):
    return eng.dma_start(dst, src, allow_slow_non_contiguous=True).then_inc(sem, 16)


def enter_stream(nc, x, X, ident):
    U = 4
    with Phase(nc, "enter") as ph:
        raw = ph.sb("raw", [P, NT, D])
        turned = ph.ps("turned", [P, U, 512])
        loaded, turned_up, stored = ph.sem("loaded"), ph.sem("turned_up"), ph.sem("stored")
        tile = ph.sb("tile", [P, U, D])
        staged = ph.sem("staged")
        with nc.Block() as block:
            @block.sync
            def _(sp):
                load(sp, raw[:, :, :], x.rearrange("b (u p) c -> p (b u) c", p=P), loaded)

            @block.gpsimd
            def _(pool):
                pool.wait_ge(loaded, 16)
                with pool.Fori(0, NT // U) as g:
                    pool.wait_ge(stored, g + 1)
                    pool.tensor_copy(tile[:, :, :], raw[:, ds(g * U, U), :]).then_inc(staged, 1)

            @block.tensor
            def _(pe):
                with pe.Fori(0, NT // U) as g:
                    pe.wait_ge(staged, g + 1)
                    for s in range(U):
                        pe.transpose(turned[:, s, 0:P], tile[:, s, :], ident[:, :]).then_inc(turned_up, 1)

            @block.vector
            def _(dve):
                dve.sem_inc(stored, 1)
                with dve.Fori(0, NT // U) as g:
                    dve.wait_ge(turned_up, (g + 1) * U)
                    dve.tensor_copy(X[:, ds(g * U * P, U * P)].rearrange("p (s c) -> p s c", s=U),
                                    turned[:, :, 0:P]).then_inc(stored, 1)


def leave_stream(nc, X, out, ident):
    U = 4
    with Phase(nc, "leave") as ph:
        rows = ph.sb("rows", [P, NT, D])
        tile = ph.sb("tile", [P, U, D])
        turned = ph.ps("turned", [P, U, 512])
        staged, turned_up, stored, written = (ph.sem(n) for n in ("staged", "turned_up", "stored", "written"))
        with nc.Block() as block:
            @block.gpsimd
            def _(pool):
                with pool.Fori(0, NT // U) as g:
                    pool.wait_ge(stored, g + 1)
                    pool.tensor_copy(tile[:, :, :],
                                     X[:, ds(g * U * P, U * P)].rearrange("p (s c) -> p s c", s=U)).then_inc(staged, 1)

            @block.tensor
            def _(pe):
                with pe.Fori(0, NT // U) as g:
                    pe.wait_ge(staged, g + 1)
                    for s in range(U):
                        pe.transpose(turned[:, s, 0:P], tile[:, s, :], ident[:, :]).then_inc(turned_up, 1)

            @block.vector
            def _(dve):
                dve.sem_inc(stored, 1)
                with dve.Fori(0, NT // U) as g:
                    dve.wait_ge(turned_up, (g + 1) * U)
                    dve.tensor_copy(rows[:, ds(g * U, U), :], turned[:, :, 0:P]).then_inc(stored, 1)

            @block.sync
            def _(sp):
                sp.wait_ge(stored, NT // U + 1)
                sp.dma_start(out.rearrange("b (u p) c -> p (b u) c", p=P), rows[:, :, :]).then_inc(written, 16)
                sp.wait_ge(written, 16)


def layer_norm(nc, tag, X, XN, ones_mean, eps):
    U = 4
    with Phase(nc, tag) as ph:
        mean, var = ph.ps("mean", [P, U, BLK]), ph.ps("var", [P, U, BLK])
        dev, sq, log, inv = (ph.sb(n, [P, U, BLK]) for n in ("dev", "sq", "log", "inv"))
        means, devs, squares, vars_, logs, invs, trip_done = (
            ph.sem(n) for n in ("means", "devs", "squares", "vars", "logs", "invs", "trip_done"))
        with nc.Block() as block:
            @block.tensor
            def _(pe):
                with pe.Fori(0, NBLK // U) as g:
                    pe.wait_ge(trip_done, g + 1)
                    for s in range(U):
                        pe.matmul(mean[:, s, :], ones_mean[:, :], X[:, ds((g * U + s) * BLK, BLK)],
                                  start=True, stop=True).then_inc(means, 1)
                    for s in range(U):
                        pe.wait_ge(squares, g * U + s + 1)
                        pe.matmul(var[:, s, :], ones_mean[:, :], sq[:, s, :], start=True, stop=True).then_inc(vars_, 1)

            @block.vector
            def _(dve):
                dve.sem_inc(trip_done, 1)
                with dve.Fori(0, NBLK // U) as g:
                    for s in range(U):
                        dve.wait_ge(means, g * U + s + 1)
                        dve.wait_ge(trip_done, g + 1)
                        dve.tensor_tensor(dev[:, s, :], X[:, ds((g * U + s) * BLK, BLK)], mean[:, s, :],
                                          ALU.subtract).then_inc(devs, 1)
                    for s in range(U):
                        dve.wait_ge(invs, g * U + s + 1)
                        o = dve.tensor_tensor(XN[:, ds((g * U + s) * BLK, BLK)], dev[:, s, :], inv[:, s, :], ALU.mult)
                    o.then_inc(trip_done, 1)

            @block.gpsimd
            def _(pool):
                with pool.Fori(0, NBLK // U) as g:
                    for s in range(U):
                        pool.wait_ge(devs, g * U + s + 1)
                        pool.tensor_tensor(sq[:, s, :], dev[:, s, :], dev[:, s, :], ALU.mult).then_inc(squares, 1)

            @block.scalar
            def _(act):
                with act.Fori(0, NBLK // U) as g:
                    for s in range(U):
                        act.wait_ge(vars_, g * U + s + 1)
                        act.activation(log[:, s, :], var[:, s, :], ACT.Ln, bias=eps[:, 0:1]).then_inc(logs, 1)
                        act.wait_ge(logs, g * U + s + 1)
                        act.activation(inv[:, s, :], log[:, s, :], ACT.Exp, scale=-0.5).then_inc(invs, 1)


HEADS = {"rel": 16, "rope": 16, "full": 1, "win": 8}
STRIP = {"rel": 32, "rope": 32, "full": 128, "win": 64}
SCALE = {"rel": 8 ** -0.5, "rope": 8 ** -0.5, "full": 128 ** -0.5, "win": 8.0}


def attention(nc, tag, kind, R, XN, A, W, ident):
    nh, strip, scale = HEADS[kind], STRIP[kind], SCALE[kind]
    G = nh * strip // P
    small = strip == 32
    NU = 2 * nh
    keys = (lambda t: L) if kind in ("rel", "full") else (lambda t: P * (t + 1))
    VW = G * P
    RS, RE, RT = 3, 6, 3
    TURN_LAG, VALUE_LAG, SHARE_LAG = 4, 6, 2
    with Phase(nc, tag) as ph:
        xs = ph.sb("xs", [P, L])
        qT, kT = ph.sb("qT", [P, G, L]), ph.sb("kT", [P, G, L])
        V = ph.sb("V", [P, 2, VW])
        S, E = ph.sb("S", [P, RS, L]), ph.sb("E", [P, RE, L])
        ET = ph.sb("ET", [P, RT, 2, P])
        least, total, share = ph.sb("least", [P, NU]), ph.sb("total", [P, NU]), ph.sb("share", [P, NU])
        mask = ph.sb("mask", [P, 2, L])
        PJ = ph.ps("PJ", [P, 2, 512])
        SC = ph.ps("SC", [P, 2, 512])
        TU = ph.ps("TU", [P, 2, 512])
        OT = ph.ps("OT", [P, 2, 512])
        wq = ph.sb("wq", [P, G * P if kind == "win" else P])
        wk = ph.sb("wk", [P, G * P if kind == "win" else P])
        wv = ph.sb("wv", [P, VW])
        if kind in ("rope", "win"):
            wqx, wkx = ph.sb("wqx", [P, wq.shape[1]]), ph.sb("wkx", [P, wk.shape[1]])
        if small:
            wv_raw = ph.sb("wv_raw", [P, P])
            spread = ph.sb("spread", [P, G, 4, 32])
            qk = ph.sb("qk", [P, 2, L])
        if kind == "rope":
            rt = ph.sb("rt", [P, 2, L])
            parts = ph.sb("parts", [P, 2, 2, L])
        if kind == "rel":
            qv = ph.sb("qv", [P, L])
            ub, vb = ph.sb("ub", [P, 1]), ph.sb("vb", [P, 1])
            wr = ph.sb("wr", [P, 16, 2, P])
            wr_raw = ph.sb("wr_raw", [P, P])
            turn = ph.sb("turn", [P, 2, L])
            low, up = ph.sb("low", [P, L]), ph.sb("up", [P, L])
            rmask = ph.sb("rmask", [P, 2, 2, P])
            tparts = ph.sb("tparts", [P, 2, 2, L])
            Ah = ph.sb("Ah", [P, 2, L + 1])
            lowm, upm, bd = ph.sb("lowm", [P, 2, L]), ph.sb("upm", [P, 2, L]), ph.sb("bd", [P, 2, L])
        if kind in ("rel", "rope", "win"):
            wo = ph.sb("wo", [P, G, D])
            oT = ph.sb("oT", [P, G, L])
        if kind == "full":
            bias = ph.sb("bias", [P, 3])
        if kind == "win":
            tab = ph.sb("tab", [P, 2, 2, L])
            qs = ph.sb("qs", [P, 2, 2])
            b64 = ph.sb("b64", [P, P])
            sq, clipped, log, inv = (ph.sb(n, [P, 2 * L]) for n in ("sq", "clipped", "log", "inv"))
            back = ph.sb("back", [P, 1])
            m1, m2, m3 = (ph.sb(n, [P, 2 * L]) for n in ("m1", "m2", "m3"))

        names = ("loaded cleared prepared staged projected v_made v_copied spread_made strips_copied scored "
                 "shifted exped summed shared turned turned_copied valued o_copied final trip_done "
                 "qk_ready parts_made a_made a_parts a_ready masked bd_ready squares norms logs clips invs "
                 "m1_made m2_made m3_made passed back_set").split()
        sm = {n: ph.sem(n) for n in names}
        n_loads = [0]

        def ld(eng, dst, src):
            n_loads[0] += 1
            load(eng, dst, src, sm["loaded"])

        half = (lambda ap: ap.rearrange("p (n two) -> p n two", two=2))

        with nc.Block() as block:
            @block.sync
            def _(sp):
                ld(sp, wq[:, :], W["q"])
                ld(sp, wk[:, :], W["k"])
                if kind == "rel":
                    ld(sp, ub[:, :], W["u"])
                    ld(sp, vb[:, :], W["v_bias"])
                    ld(sp, turn[:, :, :], A["rel_turn"])
                    ld(sp, low[:, :], A["rel_low"])
                    ld(sp, up[:, :], A["rel_up"])
                    ld(sp, rmask[:, :, :, :], A["rel_mask"])
                    sp.wait_ge(sm["cleared"], 1)
                    for h in range(16):
                        ld(sp, wr[8 * h:8 * h + 8, h, 0, :], W["r"][8 * h:8 * h + 8, :])
                        ld(sp, wr[8 * h:8 * h + 8, h, 1, :], W["r_crossed"][8 * h:8 * h + 8, :])
                if kind in ("rope", "win"):
                    ld(sp, wqx[:, :], W["q_crossed"])
                    ld(sp, wkx[:, :], W["k_crossed"])
                if kind == "rope":
                    ld(sp, rt[:, :, :], A["rope8"])
                if small:
                    ld(sp, wv_raw[:, :], W["v"])
                    sp.wait_ge(sm["cleared"], 2 if kind == "rel" else 1)
                    for s in range(4):
                        for g in range(4):
                            ld(sp, wo[32 * s:32 * s + 8, g, :], W["o"][(4 * g + s) * 8:(4 * g + s) * 8 + 8, :])
                if kind == "full":
                    ld(sp, wv[:, :], W["v"])
                    ld(sp, bias[:, :], W["bias"])
                if kind == "win":
                    ld(sp, wv[:, :], W["v"])
                    ld(sp, wo[:, :, :], W["o"])
                    ld(sp, qs[:, :, :], W["qk_scale"])
                    ld(sp, tab[:, :, :, :], A["xpos"])
                    ld(sp, b64[:, :], A["block64"])
                if kind != "rel":
                    ld(sp, mask[:, :, :], A[{"rope": "causal", "win": "band", "full": "open"}[kind]])

            loads = 16 * n_loads[0]

            @block.gpsimd
            def _(pool):
                if kind == "rel":
                    pool.memset(wr[:, :, :, :], 0.0).then_inc(sm["cleared"], 1)
                if small:
                    pool.memset(wo[:, :, :], 0.0).then_inc(sm["cleared"], 1)
                    pool.memset(spread[:, :, :, :], 0.0).then_inc(sm["prepared"], 1)
                    pool.memset(wv[:, :], 0.0).then_inc(sm["prepared"], 1)
                    pool.wait_ge(sm["loaded"], loads)
                    pool.wait_ge(sm["prepared"], 2)
                    pool.tensor_copy(spread[:, :, :, 0:8],
                                     ident[:, :].rearrange("p (g s d) -> p g s d", g=4, s=4)).then_inc(sm["prepared"], 1)
                    pool.tensor_copy(wv[:, :].rearrange("p (h w) -> p h w", w=32)[:, :, 0:8],
                                     wv_raw[:, :].rearrange("p (h d) -> p h d", d=8)).then_inc(sm["prepared"], 1)
                if kind == "rel":
                    pool.memset(lowm[:, :, :], 0.0).then_inc(sm["prepared"], 1)
                    pool.memset(upm[:, :, :], 0.0).then_inc(sm["prepared"], 1)
                    pool.memset(Ah[:, :, :], 0.0).then_inc(sm["prepared"], 1)
                    pool.wait_ge(sm["prepared"], 7)
                if kind == "win":
                    pool.memset(back[:, :], 10.0 * float(np.log(2.0))).then_inc(sm["back_set"], 1)
                    pool.wait_ge(sm["loaded"], loads)
                    for d in range(2):
                        for w in range(2):
                            pool.tensor_scalar(tab[:, d, w, :], tab[:, d, w, :], qs[:, d, w:w + 1], None,
                                               ALU.mult).then_inc(sm["prepared"], 1)
                with pool.Fori(0, NB) as b:
                    if kind == "rope":
                        pool.wait_ge(sm["parts_made"], 2 * b + 2)
                        pool.tensor_tensor(qk[:, :, :], parts[:, 0, :, :], parts[:, 1, :, :], ALU.add).then_inc(sm["qk_ready"], 1)
                    if kind == "rel":
                        for step in range(nh + 1):
                            if step < nh:
                                h = step
                                pool.wait_ge(sm["a_parts"], nh * b + h + 1)
                                if h >= 2:
                                    pool.wait_ge(sm["scored"], NU * b + 2 * (h - 2) + 2)
                                else:
                                    pool.wait_ge(sm["trip_done"], b + 1)
                                pool.tensor_tensor(Ah[:, h % 2, 0:L], tparts[:, h % 2, 0, :], tparts[:, h % 2, 1, :],
                                                   ALU.add).then_inc(sm["a_ready"], 1)
                            if step >= 1:
                                for u in (2 * step - 2, 2 * step - 1):
                                    pool.wait_ge(sm["masked"], 2 * (NU * b + u) + 2)
                                    if u >= 2:
                                        pool.wait_ge(sm["shifted"], NU * b + u - 1)
                                    pool.tensor_tensor(bd[:, u % 2, :], lowm[:, u % 2, :], upm[:, u % 2, :],
                                                       ALU.add).then_inc(sm["bd_ready"], 1)
                    if kind == "win":
                        for c in range(G):
                            pool.wait_ge(sm["m2_made"], G * b + c + 1)
                            if c >= 1:
                                pool.wait_ge(sm["strips_copied"], G * b + c)
                            pool.tensor_tensor(m3[:, :], m1[:, :], m2[:, :], ALU.add).then_inc(sm["m3_made"], 1)
                            pool.wait_ge(sm["m3_made"], G * b + c + 1)
                            pool.wait_ge(sm["invs"], G * b + c + 1)
                            pool.tensor_tensor(qT[:, c, :], m3[:, 0:L], inv[:, 0:L], ALU.mult)
                            pool.tensor_tensor(kT[:, c, :], m3[:, L:2 * L], inv[:, L:2 * L],
                                               ALU.mult).then_inc(sm["strips_copied"], 1)
                    if kind == "full":
                        pool.wait_ge(sm["trip_done"], b + 1)

            @block.tensor
            def _(pe):
                pe.wait_ge(sm["loaded"], loads)
                if small:
                    pe.wait_ge(sm["prepared"], 7 if kind == "rel" else 4)
                with pe.Fori(0, NB) as b:
                    pe.wait_ge(sm["trip_done"], b + 1)
                    pe.wait_ge(sm["staged"], b + 1)
                    if kind != "win":
                        pe.matmul(PJ[:, 0, 0:L], wq[:, :], xs[:, :], start=True, stop=True)
                        last = pe.matmul(PJ[:, 0, L:2 * L], wk[:, :], xs[:, :], start=True, stop=True)
                        if kind == "rope":
                            pe.matmul(PJ[:, 1, 0:L], wqx[:, :], xs[:, :], start=True, stop=True)
                            last = pe.matmul(PJ[:, 1, L:2 * L], wkx[:, :], xs[:, :], start=True, stop=True)
                        last.then_inc(sm["projected"], 1)
                    for t in range(2):
                        pe.matmul(SC[:, t, 0:VW], xs[:, t * P:(t + 1) * P], wv[:, :], start=True,
                                  stop=True).then_inc(sm["v_made"], 1)
                    if small:
                        pe.wait_ge(sm["qk_ready"], b + 1)
                        for g in range(G):
                            bank = TU[:, g, :] if g < 2 else OT[:, g - 2, :]
                            pe.matmul(bank, spread[:, g, :, :], qk[:, :, :], start=True, stop=True).then_inc(sm["spread_made"], 1)
                    if kind == "win":
                        for c in range(G):
                            cols = slice(c * P, (c + 1) * P)
                            if c >= 1:
                                pe.wait_ge(sm["m2_made"], G * b + c)
                                pe.wait_ge(sm["squares"], G * b + c)
                            pe.matmul(PJ[:, 0, 0:L], wq[:, cols], xs[:, :], start=True, stop=True)
                            pe.matmul(PJ[:, 0, L:2 * L], wk[:, cols], xs[:, :], start=True, stop=True)
                            pe.matmul(PJ[:, 1, 0:L], wqx[:, cols], xs[:, :], start=True, stop=True)
                            pe.matmul(PJ[:, 1, L:2 * L], wkx[:, cols], xs[:, :], start=True,
                                      stop=True).then_inc(sm["projected"], 1)
                            pe.wait_ge(sm["squares"], G * b + c + 1)
                            if c >= 1:
                                pe.wait_ge(sm["clips"], G * b + c)
                            pe.matmul(TU[:, 0, :], b64[:, :], sq[:, :], start=True, stop=True).then_inc(sm["norms"], 1)

                    def make_a(h):
                        if h >= 2:
                            pe.wait_ge(sm["a_parts"], nh * b + h - 1)
                        for x in range(2):
                            last = pe.matmul(PJ[:, h % 2, x * L:(x + 1) * L], wr[:, h, x, :], qv[:, :], start=True, stop=True)
                        last.then_inc(sm["a_made"], 1)

                    def score(u):
                        h, t = u // 2, u % 2
                        g, s = h * strip // P, (h * strip % P)
                        rows = slice(s, s + strip)
                        if u >= 2:
                            pe.wait_ge(sm["shifted"], NU * b + u - 1)
                        n = keys(t)
                        sc = SC[:, u % 2, :]
                        last = pe.matmul(sc[:, 0:n], qT[rows, g, t * P:(t + 1) * P], kT[rows, g, 0:n],
                                         start=True, stop=kind != "rel", skip_group_check=kind == "rel")
                        if kind == "rel":
                            pe.wait_ge(sm["a_ready"], nh * b + h + 1)
                            a0 = Ah[:, h % 2, t * P:(t + 1) * P]
                            a1 = Ah[:, h % 2, t * P + 1:(t + 1) * P + 1]
                            if t == 0:
                                pe.matmul(sc[:, P + 1:L], a1, up[:, P + 1:L], start=False, stop=True, skip_group_check=True)
                                pe.matmul(sc[:, L:L + P], a0, low[:, 0:P], start=False, stop=True, skip_group_check=True)
                                last = pe.matmul(sc[:, L + P:2 * L], a1, up[:, 1:P + 1], start=False, stop=True,
                                                 skip_group_check=True)
                            else:
                                pe.matmul(sc[:, 0:P], a0, low[:, 0:P], start=False, stop=True, skip_group_check=True)
                                pe.matmul(sc[:, L:L + P], a0, low[:, P:L], start=False, stop=True, skip_group_check=True)
                                last = pe.matmul(sc[:, L + P:2 * L], a1, up[:, P:L], start=False, stop=True,
                                                 skip_group_check=True)
                        last.then_inc(sm["scored"], 1)

                    def turn_up(u):
                        pe.wait_ge(sm["shared"], NU * b + u + 1)
                        if u >= 2:
                            pe.wait_ge(sm["turned_copied"], NU * b + u - 1)
                        for c in range(keys(u % 2) // P):
                            last = pe.transpose(TU[:, u % 2, c * P:(c + 1) * P], E[:, u % RE, c * P:(c + 1) * P], ident[:, :])
                        last.then_inc(sm["turned"], 1)

                    def value(u):
                        h, t = u // 2, u % 2
                        g, s = h * strip // P, h * strip % P
                        pe.wait_ge(sm["turned_copied"], NU * b + u + 1)
                        nk = keys(t) // P
                        col = (g % 2) * L + t * P
                        for c in range(nk):
                            last = pe.matmul(OT[s:s + strip, g // 2, col:col + P], V[:, c, h * strip:(h + 1) * strip],
                                             ET[:, u % RT, c, :], start=c == 0, stop=c == nk - 1)
                        last.then_inc(sm["valued"], 1)

                    pe.wait_ge(sm["v_copied"], 2 * b + 2)
                    pe.wait_ge(sm["strips_copied"], (G if G > 1 else 2) * (b + 1))
                    if kind == "rel":
                        make_a(0)
                    for step in range(NU + VALUE_LAG):
                        if kind == "rel" and step % 2 == 0 and step // 2 + 1 < nh:
                            make_a(step // 2 + 1)
                        if step < NU:
                            score(step)
                        if 0 <= step - TURN_LAG < NU:
                            turn_up(step - TURN_LAG)
                        if step >= VALUE_LAG:
                            value(step - VALUE_LAG)
                    if kind != "full":
                        pe.wait_ge(sm["o_copied"], 2 * b + 2)
                        for g in range(G):
                            last = pe.matmul(PJ[:, 0, 0:L], wo[:, g, :], oT[:, g, :], start=g == 0, stop=g == G - 1)
                        last.then_inc(sm["final"], 1)

            @block.scalar
            def _(act):
                act.wait_ge(sm["loaded"], loads)
                if kind == "win":
                    act.wait_ge(sm["back_set"], 1)
                with act.Fori(0, NB) as b:
                    act.wait_ge(sm["trip_done"], b + 1)
                    if kind == "full":
                        act.wait_ge(sm["projected"], b + 1)
                        act.activation(qT[:, 0, :], PJ[:, 0, 0:L], ACT.Identity, bias=bias[:, 0:1]).then_inc(sm["strips_copied"], 1)
                        act.activation(kT[:, 0, :], PJ[:, 0, L:2 * L], ACT.Identity, bias=bias[:, 1:2]).then_inc(sm["strips_copied"], 1)
                    for t in range(2):
                        act.wait_ge(sm["v_made"], 2 * b + t + 1)
                        act.activation(V[:, t, :], SC[:, t, 0:VW], ACT.Copy).then_inc(sm["v_copied"], 1)
                    if small:
                        for g in range(G):
                            bank = TU[:, g, :] if g < 2 else OT[:, g - 2, :]
                            act.wait_ge(sm["spread_made"], G * b + g + 1)
                            act.activation(qT[:, g, :], bank[:, 0:L], ACT.Copy)
                            act.activation(kT[:, g, :], bank[:, L:2 * L], ACT.Copy).then_inc(sm["strips_copied"], 1)
                    if kind == "win":
                        for c in range(G):
                            act.wait_ge(sm["projected"], G * b + c + 1)
                            act.activation(sq[:, :], PJ[:, 0, :], ACT.Square).then_inc(sm["squares"], 1)
                            act.wait_ge(sm["clips"], G * b + c + 1)
                            if c >= 1:
                                act.wait_ge(sm["invs"], G * b + c)
                                act.wait_ge(sm["strips_copied"], G * b + c)
                            act.activation(log[:, :], clipped[:, :], ACT.Ln, scale=2.0 ** 20).then_inc(sm["logs"], 1)
                            act.wait_ge(sm["logs"], G * b + c + 1)
                            act.activation(inv[:, :], log[:, :], ACT.Exp, scale=-0.5, bias=back[:, 0:1]).then_inc(sm["invs"], 1)
                    for step in range(NU + TURN_LAG):
                        u = step
                        if u < NU:
                            n = keys(u % 2)
                            act.wait_ge(sm["shifted"], NU * b + u + 1)
                            if u >= RE:
                                act.wait_ge(sm["turned"], NU * b + u - RE + 1)
                            act.activation(E[:, u % RE, 0:n], S[:, u % RS, 0:n], ACT.Exp, bias=least[:, u:u + 1], scale=-1.0,
                                           accum_out=total[:, u:u + 1]).then_inc(sm["exped"], 1)
                        u = step - TURN_LAG
                        if u >= 0:
                            act.wait_ge(sm["turned"], NU * b + u + 1)
                            if u >= RT:
                                act.wait_ge(sm["valued"], NU * b + u - RT + 1)
                            n = keys(u % 2)
                            act.activation(ET[:, u % RT, 0:n // P, :], TU[:, u % 2, 0:n].rearrange("p (c q) -> p c q", q=P),
                                           ACT.Copy).then_inc(sm["turned_copied"], 1)
                    if kind != "full":
                        act.wait_ge(sm["valued"], NU * (b + 1))
                        for i in range(2):
                            act.activation(oT[:, 2 * i:2 * i + 2, :], OT[:, i, :].rearrange("p (g q) -> p g q", g=2),
                                           ACT.Copy).then_inc(sm["o_copied"], 1)

            @block.vector
            def _(dve):
                dve.sem_inc(sm["trip_done"], 1)
                dve.wait_ge(sm["loaded"], loads)
                if kind in ("rel", "win"):
                    dve.wait_ge(sm["prepared"], 7 if kind == "rel" else 4)
                with dve.Fori(0, NB) as b:
                    dve.wait_ge(sm["trip_done"], b + 1)
                    seq = ds(b * L, L)
                    if kind == "win":
                        dve.tensor_copy(xs[0:64, :], XN[0:64, seq])
                        dve.memset(xs[64:P, 0:1], 0.0)
                        dve.tensor_copy(xs[64:P, 1:L], XN[64:P, ds(b * L, L - 1)]).then_inc(sm["staged"], 1)
                    else:
                        dve.tensor_copy(xs[:, :], XN[:, seq]).then_inc(sm["staged"], 1)
                    if kind == "rel":
                        dve.wait_ge(sm["projected"], b + 1)
                        dve.tensor_scalar(qv[:, :], PJ[:, 0, 0:L], vb[:, 0:1], None, ALU.add)
                        dve.tensor_scalar(qk[:, 0, :], PJ[:, 0, 0:L], ub[:, 0:1], None, ALU.add)
                        dve.tensor_copy(qk[:, 1, :], PJ[:, 0, L:2 * L]).then_inc(sm["qk_ready"], 1)
                    if kind == "rope":
                        dve.wait_ge(sm["projected"], b + 1)
                        for x in range(2):
                            tb = rt[:, x, :].rearrange("p (o n) -> p o n", o=1).broadcast_to([P, 2, L])
                            dve.tensor_tensor(parts[:, x, :, :], PJ[:, x, :].rearrange("p (w n) -> p w n", w=2), tb,
                                              ALU.mult).then_inc(sm["parts_made"], 1)
                    if kind == "win":
                        for c in range(G):
                            dve.wait_ge(sm["projected"], G * b + c + 1)
                            if c >= 1:
                                dve.wait_ge(sm["m3_made"], G * b + c)
                            dve.wait_ge(sm["squares"], G * b + c + 1)
                            dve.tensor_tensor(m1[:, :], PJ[:, 0, :], tab[:, 0, :, :].rearrange("p w n -> p (w n)"), ALU.mult)
                            dve.tensor_tensor(m2[:, :], PJ[:, 1, :], tab[:, 1, :, :].rearrange("p w n -> p (w n)"),
                                              ALU.mult).then_inc(sm["m2_made"], 1)
                            dve.wait_ge(sm["norms"], G * b + c + 1)
                            if c >= 1:
                                dve.wait_ge(sm["logs"], G * b + c)
                            dve.tensor_scalar(clipped[:, :], TU[:, 0, :], 1e-24, None, ALU.max).then_inc(sm["clips"], 1)

                    def make_parts(h):
                        dve.wait_ge(sm["a_made"], nh * b + h + 1)
                        if h >= 2:
                            dve.wait_ge(sm["a_ready"], nh * b + h - 1)
                        dve.tensor_tensor(tparts[:, h % 2, :, :], PJ[:, h % 2, :].rearrange("p (x n) -> p x n", x=2),
                                          turn[:, :, :], ALU.mult).then_inc(sm["a_parts"], 1)

                    def shift(u):
                        t = u % 2
                        n = keys(t)
                        dve.wait_ge(sm["scored"], NU * b + u + 1)
                        add = mask[:, t, 0:n]
                        if kind == "rel":
                            k0 = 1 if t == 0 else P
                            if u >= 2:
                                dve.wait_ge(sm["bd_ready"], NU * b + u - 1)
                            dve.tensor_tensor(lowm[:, t, t * P:(t + 1) * P], SC[:, u % 2, L:L + P], rmask[:, t, 0, :],
                                              ALU.mult).then_inc(sm["masked"], 1)
                            dve.tensor_tensor(upm[:, t, k0:k0 + P], SC[:, u % 2, L + P:2 * L], rmask[:, t, 1, :],
                                              ALU.mult).then_inc(sm["masked"], 1)
                            dve.wait_ge(sm["bd_ready"], NU * b + u + 1)
                            add = bd[:, t, :]
                        if u >= RS:
                            dve.wait_ge(sm["exped"], NU * b + u - RS + 1)
                        dve.sem_inc(sm["passed"], 1)
                        dve.tensor_tensor_reduce(S[:, u % RS, 0:n], SC[:, u % 2, 0:n], add, -scale, 3e38, ALU.add, ALU.min,
                                                 least[:, u:u + 1]).then_inc(sm["shifted"], 1)

                    def share_out(u):
                        n = keys(u % 2)
                        dve.wait_ge(sm["exped"], NU * b + u + 1)
                        dve.reciprocal(share[:, u:u + 1], total[:, u:u + 1]).then_inc(sm["summed"], 1)
                        dve.wait_ge(sm["summed"], NU * b + u + 1)
                        dve.tensor_scalar(E[:, u % RE, 0:n], E[:, u % RE, 0:n], share[:, u:u + 1], None,
                                          ALU.mult).then_inc(sm["shared"], 1)

                    if kind == "rel":
                        make_parts(0)
                    for step in range(NU + SHARE_LAG):
                        if kind == "rel" and step % 2 == 0 and step // 2 + 1 < nh:
                            make_parts(step // 2 + 1)
                        if step < NU:
                            shift(step)
                        if step >= SHARE_LAG:
                            share_out(step - SHARE_LAG)
                    if kind == "full":
                        dve.wait_ge(sm["valued"], NU * (b + 1))
                        dve.scalar_tensor_tensor(R[:, seq], OT[:, 0, 0:L], bias[:, 2:3], R[:, seq], ALU.add,
                                                 ALU.add).then_inc(sm["trip_done"], 1)
                    else:
                        dve.wait_ge(sm["final"], b + 1)
                        dve.tensor_tensor(R[:, seq], PJ[:, 0, 0:L], R[:, seq], ALU.add).then_inc(sm["trip_done"], 1)


def gated_ffn(nc, tag, kind, R, XN, A, W, om=None, eps=None):
    gelu = kind == "gelu"
    HID = 341 if gelu else 384
    NC = 3
    width = [min(P, HID - c * P) for c in range(NC)]
    U = 2
    with Phase(nc, tag) as ph:
        wg, wu = ph.sb("wg", [P, HID]), ph.sb("wu", [P, HID])
        wd = ph.sb("wd", [P, NC, D])
        gate_on, hid = ph.sb("gate_on", [P, 2, BLK]), ph.sb("hid", [P, U, NC, BLK])
        G, UP = ph.ps("G", [P, 2, BLK]), ph.ps("UP", [P, 2, BLK])
        OUT = ph.ps("OUT", [P, U, BLK])
        names = ("loaded weights_ready shifted means devs squares vars logs invs scaled normed gate_made up_made gated "
                 "hidden out_made trip_done zeroed").split()
        sm = {n: ph.sem(n) for n in names}
        if gelu:
            ba, bg, b2 = ph.sb("ba", [P, NC]), ph.sb("bg", [P, NC]), ph.sb("b2", [P, 1])
            lg, lb = ph.sb("lg", [P, 1]), ph.sb("lb", [P, 1])
            hs, dev, sq, log, inv, hn, hx = (ph.sb(n, [P, U, BLK]) for n in ("hs", "dev", "sq", "log", "inv", "hn", "hx"))
            STAT = ph.ps("STAT", [P, U, BLK])
            loads = 16 * (2 + (2 + 2 * 2 + 1 + 2) + 2)
        else:
            ig, iu, idn = ph.sb("ig", [P, HID], I32), ph.sb("iu", [P, HID], I32), ph.sb("idn", [P, NC, D], I32)
            loads = 16 * 3
        with nc.Block() as block:
            @block.sync
            def _(sp):
                if gelu:
                    load(sp, wu[:, :], W["w1"][:, 0:HID], sm["loaded"])
                    load(sp, wg[:, :], W["w1"][:, HID:2 * HID], sm["loaded"])
                    load(sp, wd[:, 0:2, :], W["w2"][0:2 * P, :].rearrange("(c p) d -> p c d", p=P), sm["loaded"])
                    load(sp, wd[0:width[2], 2, :], W["w2"][2 * P:HID, :], sm["loaded"])
                    for dst, o in ((ba, 0), (bg, HID)):
                        load(sp, dst[:, 0:2], W["b1"][o:o + 2 * P].rearrange("(c p) -> p c", p=P), sm["loaded"])
                        load(sp, dst[0:width[2], 2:3], W["b1"][o + 2 * P:o + HID].rearrange("(p c) -> p c", c=1), sm["loaded"])
                    for dst, n in ((b2, "b2"), (lg, "ln_g"), (lb, "ln_b")):
                        load(sp, dst[:, :], W[n].rearrange("(p c) -> p c", c=1), sm["loaded"])
                else:
                    load(sp, ig[:, :], W["gate"], sm["loaded"])
                    load(sp, iu[:, :], W["up"], sm["loaded"])
                    load(sp, idn[:, :, :], W["down"].rearrange("(c p) d -> p c d", p=P), sm["loaded"])

            @block.gpsimd
            def _(pool):
                if gelu:
                    pool.memset(hs[64:P, :, :], 0.0).then_inc(sm["zeroed"], 1)
                    with pool.Fori(0, NBLK // U) as g:
                        for s in range(U):
                            pool.wait_ge(sm["invs"], U * g + s + 1)
                            pool.wait_ge(sm["trip_done"], g + 1)
                            pool.tensor_tensor(hn[:, s, :], dev[:, s, :], inv[:, s, :], ALU.mult).then_inc(sm["scaled"], 1)

            @block.tensor
            def _(pe):
                pe.wait_ge(sm["loaded"], 16 * 11 if gelu else loads)
                if not gelu:
                    pe.wait_ge(sm["weights_ready"], 3)
                with pe.Fori(0, NBLK // U) as g:
                    pe.wait_ge(sm["trip_done"], g + 1)
                    if gelu:
                        for s in range(U):
                            pe.wait_ge(sm["shifted"], U * g + s + 1)
                            pe.matmul(STAT[:, s, :], om[:, :], hs[:, s, :], start=True, stop=True).then_inc(sm["means"], 1)
                        for s in range(U):
                            pe.wait_ge(sm["squares"], U * g + s + 1)
                            pe.wait_ge(sm["devs"], U * g + s + 1)
                            pe.matmul(STAT[:, s, :], om[:, :], sq[:, s, :], start=True, stop=True).then_inc(sm["vars"], 1)

                    def down(s):
                        pe.wait_ge(sm["hidden"], NC * (U * g + s) + NC)
                        for c in range(NC):
                            last = pe.matmul(OUT[:, s, :], wd[0:width[c], c, :], hid[0:width[c], s, c, :],
                                             start=c == 0, stop=c == NC - 1)
                        last.then_inc(sm["out_made"], 1)

                    for k in range(U * NC):
                        s, c = k // NC, k % NC
                        x = hx[:, s, :] if gelu else XN[:, ds((U * g + s) * BLK, BLK)]
                        if gelu and c == 0:
                            pe.wait_ge(sm["normed"], U * g + s + 1)
                        if k >= 2:
                            pe.wait_ge(sm["hidden"], NC * U * g + k - 1)
                        cols = slice(c * P, c * P + width[c])
                        pe.matmul(G[0:width[c], k % 2, :], wg[:, cols], x, start=True, stop=True).then_inc(sm["gate_made"], 1)
                        pe.matmul(UP[0:width[c], k % 2, :], wu[:, cols], x, start=True, stop=True).then_inc(sm["up_made"], 1)
                        if k == NC + 1:
                            down(0)
                    down(1)

            @block.scalar
            def _(act):
                act.wait_ge(sm["loaded"], 16 * 11 if gelu else loads)
                with act.Fori(0, NBLK // U) as g:
                    act.wait_ge(sm["trip_done"], g + 1)
                    if gelu:
                        for s in range(U):
                            act.wait_ge(sm["devs"], U * g + s + 1)
                            act.activation(sq[:, s, :], dev[:, s, :], ACT.Square).then_inc(sm["squares"], 1)
                        for s in range(U):
                            act.wait_ge(sm["vars"], U * g + s + 1)
                            act.activation(log[:, s, :], STAT[:, s, :], ACT.Ln, bias=eps[:, 0:1]).then_inc(sm["logs"], 1)
                        for s in range(U):
                            act.wait_ge(sm["logs"], U * g + s + 1)
                            act.activation(inv[:, s, :], log[:, s, :], ACT.Exp, scale=-0.5).then_inc(sm["invs"], 1)
                        for s in range(U):
                            act.wait_ge(sm["scaled"], U * g + s + 1)
                            act.activation(hx[:, s, :], hn[:, s, :], ACT.Identity, bias=lb[:, 0:1],
                                           scale=lg[:, 0:1]).then_inc(sm["normed"], 1)
                    for k in range(U * NC):
                        c = k % NC
                        w = width[c]
                        act.wait_ge(sm["gate_made"], NC * U * g + k + 1)
                        if k >= 2:
                            act.wait_ge(sm["hidden"], NC * U * g + k - 1)
                        if gelu:
                            act.activation(gate_on[0:w, k % 2, :], G[0:w, k % 2, :], ACT.Gelu,
                                           bias=bg[0:w, c:c + 1]).then_inc(sm["gated"], 1)
                        else:
                            act.activation(gate_on[0:w, k % 2, :], G[0:w, k % 2, :], ACT.Silu).then_inc(sm["gated"], 1)

            @block.vector
            def _(dve):
                dve.sem_inc(sm["trip_done"], 1)
                dve.wait_ge(sm["loaded"], 16 * 11 if gelu else loads)
                if gelu:
                    dve.wait_ge(sm["zeroed"], 1)
                else:
                    for dst, src in ((wg, ig), (wu, iu)):
                        dve.tensor_scalar(dst[:, :], src[:, :], 1.0 / 127.0, None, ALU.mult).then_inc(sm["weights_ready"], 1)
                    dve.tensor_scalar(wd[:, :, :], idn[:, :, :], 1.0 / 127.0, None, ALU.mult).then_inc(sm["weights_ready"], 1)
                with dve.Fori(0, NBLK // U) as g:
                    if gelu:
                        for s in range(U):
                            dve.wait_ge(sm["trip_done"], g + 1)
                            dve.tensor_copy(hs[0:64, s, :], R[0:64, ds((U * g + s) * BLK, BLK)])
                            for q in range(2):
                                o = dve.tensor_copy(hs[64:P, s, q * L + 1:(q + 1) * L],
                                                    R[64:P, ds((U * g + s) * BLK + q * L, L - 1)])
                            o.then_inc(sm["shifted"], 1)
                        for s in range(U):
                            dve.wait_ge(sm["means"], U * g + s + 1)
                            dve.tensor_tensor(dev[:, s, :], hs[:, s, :], STAT[:, s, :], ALU.subtract).then_inc(sm["devs"], 1)

                    def residual(s):
                        dve.wait_ge(sm["out_made"], U * g + s + 1)
                        at = ds((U * g + s) * BLK, BLK)
                        if gelu:
                            o = dve.scalar_tensor_tensor(R[:, at], OUT[:, s, :], b2[:, 0:1], R[:, at], ALU.add, ALU.add)
                        else:
                            o = dve.scalar_tensor_tensor(R[:, at], OUT[:, s, :], 0.5, R[:, at], ALU.mult, ALU.add)
                        if s == U - 1:
                            o.then_inc(sm["trip_done"], 1)

                    for k in range(U * NC):
                        s, c = k // NC, k % NC
                        w = width[c]
                        dve.wait_ge(sm["gated"], NC * U * g + k + 1)
                        dve.wait_ge(sm["up_made"], NC * U * g + k + 1)
                        if gelu:
                            dve.scalar_tensor_tensor(hid[0:w, s, c, :], UP[0:w, k % 2, :], ba[0:w, c:c + 1],
                                                     gate_on[0:w, k % 2, :], ALU.add, ALU.mult).then_inc(sm["hidden"], 1)
                        else:
                            dve.tensor_tensor(hid[0:w, s, c, :], UP[0:w, k % 2, :], gate_on[0:w, k % 2, :],
                                              ALU.mult).then_inc(sm["hidden"], 1)
                    residual(0)
                    residual(1)


def add_half(nc, tag, X, Y):
    with Phase(nc, tag) as ph:
        with nc.Block() as block:
            @block.vector
            def _(dve):
                dve.scalar_tensor_tensor(X[:, :], Y[:, :], 0.5, X[:, :], ALU.mult, ALU.add)


def latent_attention(nc, tag, X, XN, A, W, ident):
    scale = 8 ** -0.5
    NP_ = 8
    with Phase(nc, tag) as ph:
        xs, xopen = ph.sb("xs", [P, L]), ph.sb("xopen", [P, 2, 64])
        wk, wkx, wv, wp = (ph.sb(n, [P, P]) for n in ("wk", "wkx", "wv", "wp"))
        wg = ph.sb("wg", [P, 1024])
        lat = ph.sb("lat", [P, NP_, P])
        rt = ph.sb("rt", [P, 2, L])
        lmask = ph.sb("lmask", [P, 64])
        own = ph.sb("own", [P, NP_, P])
        parts, kr = ph.sb("parts", [P, 2, L]), ph.sb("kr", [P, L])
        V = ph.sb("V", [P, P])
        s1, s2, pr = ph.sb("s1", [P, 16, 64]), ph.sb("s2", [P, 16, 64]), ph.sb("pr", [P, 16, 64])
        smax, ssum, sinv = (ph.sb(n, [P, 16]) for n in ("smax", "ssum", "sinv"))
        prT, att = ph.sb("prT", [P, NP_, P]), ph.sb("att", [P, NP_, P])
        gmax, gsum, ginv = (ph.sb(n, [P, 2, 16]) for n in ("gmax", "gsum", "ginv"))
        g1, g2, g3 = (ph.sb(n, [P, 2, 16, 64]) for n in ("g1", "g2", "g3"))
        gT = ph.sb("gT", [P, NP_, L])
        wt = ph.sb("wt", [P, L])
        PJ, PV = ph.ps("PJ", [P, 512]), ph.ps("PV", [P, 512])
        SC, GA, TR = ph.ps("SC", [P, 2, 512]), ph.ps("GA", [P, 2, 512]), ph.ps("TR", [P, 2, 512])
        names = ("loaded cleared staged k_made v_made parts_made k_ready v_copied scored s1_made smaxed s2_made s_exped "
                 "ssummed sinverted probs p_turned p_copied att_made att_ready g_made gmaxed g1_made g_exped gsummed "
                 "ginverted gates g_turned g_copied weighted w_copied final trip_done").split()
        sm = {n: ph.sem(n) for n in names}
        loads = 16 * (8 + 16)
        flat = (lambda ap: ap.rearrange("p (h l) -> p h l", l=64))

        def spread(ap, n):
            return ap.rearrange("p (h o) -> p h o", o=1).broadcast_to([P, ap.shape[1], n])

        with nc.Block() as block:
            @block.sync
            def _(sp):
                for dst, n in ((wk, "k"), (wkx, "k_crossed"), (wv, "v"), (wp, "p"), (wg, "g")):
                    load(sp, dst[:, :], W[n], sm["loaded"])
                load(sp, rt[:, :, :], A["rope8"], sm["loaded"])
                load(sp, lmask[:, :], A["latent_mask"], sm["loaded"])
                load(sp, own[:, :, :], A["own_head"], sm["loaded"])
                sp.wait_ge(sm["cleared"], 1)
                for h in range(16):
                    load(sp, lat[8 * h:8 * h + 8, h // 2, (h % 2) * 64:(h % 2) * 64 + 64], W["q"][h, :, :], sm["loaded"])

            @block.gpsimd
            def _(pool):
                pool.memset(lat[:, :, :], 0.0).then_inc(sm["cleared"], 1)
                with pool.Fori(0, NB) as b:
                    pool.wait_ge(sm["parts_made"], b + 1)
                    pool.tensor_tensor(kr[:, :], parts[:, 0, :], parts[:, 1, :], ALU.add).then_inc(sm["k_ready"], 1)
                    for t in range(2):
                        pool.wait_ge(sm["ginverted"], 2 * b + t + 1)
                        pool.tensor_tensor(g3[:, t, :, :], g2[:, t, :, :], spread(ginv[:, t, :], 64), ALU.mult).then_inc(sm["gates"], 1)

            @block.tensor
            def _(pe):
                pe.wait_ge(sm["loaded"], loads)
                with pe.Fori(0, NB) as b:
                    pe.wait_ge(sm["staged"], 2 * b + 2)
                    pe.matmul(PJ[:, 0:L], wk[:, :], xs[:, :], start=True, stop=True)
                    pe.matmul(PJ[:, L:2 * L], wkx[:, :], xs[:, :], start=True, stop=True).then_inc(sm["k_made"], 1)
                    pe.matmul(PV[:, 0:P], xopen[:, :, :], wv[:, :], start=True,
                              stop=True).then_inc(sm["v_made"], 1)
                    for q in range(2):
                        pe.matmul(GA[:, q, :], xs[:, 0:P], wg[:, q * 512:(q + 1) * 512], start=True, stop=True).then_inc(sm["g_made"], 1)
                    pe.wait_ge(sm["k_ready"], b + 1)
                    open_keys = kr[:, :].rearrange("p (n t) -> p n t", n=2)[:, :, 0:64]
                    for i in range(NP_):
                        o = pe.matmul(SC[:, i // 4, (i % 4) * P:(i % 4 + 1) * P], lat[:, i, :], open_keys, start=True, stop=True)
                        if i % 4 == 3:
                            o.then_inc(sm["scored"], 1)
                    for q in range(2):
                        pe.wait_ge(sm["g1_made"], 4 * b + q + 1)
                        pe.matmul(GA[:, q, :], xs[:, P:L], wg[:, q * 512:(q + 1) * 512], start=True, stop=True).then_inc(sm["g_made"], 1)
                    pe.wait_ge(sm["probs"], b + 1)
                    for i in range(NP_):
                        o = pe.transpose(TR[:, i // 4, (i % 4) * P:(i % 4 + 1) * P],
                                         pr[:, 2 * i:2 * i + 2, :], ident[:, :])
                        if i % 4 == 3:
                            o.then_inc(sm["p_turned"], 1)
                    pe.wait_ge(sm["p_copied"], 2 * b + 2)
                    pe.wait_ge(sm["v_copied"], b + 1)
                    pe.wait_ge(sm["s1_made"], 2 * b + 2)
                    for i in range(NP_):
                        o = pe.matmul(SC[:, i // 4, (i % 4) * P:(i % 4 + 1) * P], prT[:, i, :], V[:, :], start=True, stop=True)
                        if i % 4 == 3:
                            o.then_inc(sm["att_made"], 1)
                    for t in range(2):
                        pe.wait_ge(sm["gates"], 2 * b + t + 1)
                        for q in range(2):
                            if t == 1:
                                pe.wait_ge(sm["g_copied"], 4 * b + q + 1)
                            for i in range(4):
                                pair = 4 * q + i
                                o = pe.transpose(TR[:, q, i * P:(i + 1) * P], g3[:, t, 2 * pair:2 * pair + 2, :], ident[:, :])
                            o.then_inc(sm["g_turned"], 1)
                    pe.wait_ge(sm["g_copied"], 4 * b + 4)
                    pe.wait_ge(sm["att_ready"], 2 * b + 2)
                    for i in range(NP_):
                        o = pe.matmul(PV[:, 0:L], att[:, i, :], gT[:, i, :], start=i == 0, stop=i == NP_ - 1)
                    o.then_inc(sm["weighted"], 1)
                    pe.wait_ge(sm["w_copied"], b + 1)
                    pe.matmul(PJ[:, 0:L], wp[:, :], wt[:, :], start=True, stop=True).then_inc(sm["final"], 1)

            @block.scalar
            def _(act):
                with act.Fori(0, NB) as b:
                    act.wait_ge(sm["v_made"], b + 1)
                    act.activation(V[:, :], PV[:, 0:P], ACT.Copy).then_inc(sm["v_copied"], 1)
                    act.wait_ge(sm["g1_made"], 4 * b + 2)
                    act.activation(g2[:, 0, :, :], g1[:, 0, :, :], ACT.Exp, scale=scale).then_inc(sm["g_exped"], 1)
                    act.wait_ge(sm["s2_made"], b + 1)
                    act.activation(pr[:, :, :], s2[:, :, :], ACT.Exp).then_inc(sm["s_exped"], 1)
                    act.wait_ge(sm["g1_made"], 4 * b + 4)
                    act.activation(g2[:, 1, :, :], g1[:, 1, :, :], ACT.Exp, scale=scale).then_inc(sm["g_exped"], 1)
                    for q in range(2):
                        act.wait_ge(sm["p_turned"], 2 * b + q + 1)
                        act.activation(prT[:, 4 * q:4 * q + 4, :], TR[:, q, :].rearrange("p (i c) -> p i c", i=4),
                                       ACT.Copy).then_inc(sm["p_copied"], 1)
                    for t in range(2):
                        for q in range(2):
                            act.wait_ge(sm["g_turned"], 4 * b + 2 * t + q + 1)
                            act.activation(gT[:, 4 * q:4 * q + 4, t * P:(t + 1) * P],
                                           TR[:, q, :].rearrange("p (i c) -> p i c", i=4), ACT.Copy).then_inc(sm["g_copied"], 1)
                    act.wait_ge(sm["weighted"], b + 1)
                    act.activation(wt[:, :], PV[:, 0:L], ACT.Copy).then_inc(sm["w_copied"], 1)

            @block.vector
            def _(dve):
                dve.sem_inc(sm["trip_done"], 1)
                dve.wait_ge(sm["loaded"], loads)
                with dve.Fori(0, NB) as b:
                    dve.wait_ge(sm["trip_done"], b + 1)
                    dve.tensor_copy(xs[:, :], XN[:, ds(b * L, L)]).then_inc(sm["staged"], 1)
                    for n in range(2):
                        o = dve.tensor_copy(xopen[:, n, :], XN[:, ds(b * L + n * P, 64)])
                    o.then_inc(sm["staged"], 1)
                    dve.wait_ge(sm["k_made"], b + 1)
                    dve.tensor_tensor(parts[:, :, :], PJ[:, :].rearrange("p (w n) -> p w n", w=2), rt[:, :, :],
                                      ALU.mult).then_inc(sm["parts_made"], 1)

                    def gate_tile(t):
                        for q in range(2):
                            dve.wait_ge(sm["g_made"], 4 * b + 2 * t + q + 1)
                            dve.tensor_reduce(gmax[:, t, 8 * q:8 * q + 8], flat(GA[:, q, :]), AX, ALU.max).then_inc(sm["gmaxed"], 1)
                        for q in range(2):
                            dve.wait_ge(sm["gmaxed"], 4 * b + 2 * t + q + 1)
                            dve.tensor_tensor(g1[:, t, 8 * q:8 * q + 8, :], flat(GA[:, q, :]),
                                              spread(gmax[:, t, 8 * q:8 * q + 8], 64), ALU.subtract).then_inc(sm["g1_made"], 1)

                    gate_tile(0)
                    for q in range(2):
                        dve.wait_ge(sm["scored"], 2 * b + q + 1)
                        m = lmask[:, :].rearrange("p (o c) -> p o c", o=1).broadcast_to([P, 8, 64])
                        dve.scalar_tensor_tensor(s1[:, 8 * q:8 * q + 8, :], flat(SC[:, q, :]), scale, m, ALU.mult,
                                                 ALU.add).then_inc(sm["s1_made"], 1)
                    dve.wait_ge(sm["s1_made"], 2 * b + 2)
                    dve.tensor_reduce(smax[:, :], s1[:, :, :], AX, ALU.max).then_inc(sm["smaxed"], 1)
                    dve.wait_ge(sm["smaxed"], b + 1)
                    dve.tensor_tensor(s2[:, :, :], s1[:, :, :], spread(smax[:, :], 64), ALU.subtract).then_inc(sm["s2_made"], 1)
                    gate_tile(1)
                    dve.wait_ge(sm["s_exped"], b + 1)
                    dve.tensor_reduce(ssum[:, :], pr[:, :, :], AX, ALU.add).then_inc(sm["ssummed"], 1)
                    dve.wait_ge(sm["ssummed"], b + 1)
                    dve.reciprocal(sinv[:, :], ssum[:, :]).then_inc(sm["sinverted"], 1)
                    dve.wait_ge(sm["sinverted"], b + 1)
                    dve.tensor_tensor(pr[:, :, :], pr[:, :, :], spread(sinv[:, :], 64), ALU.mult).then_inc(sm["probs"], 1)
                    for t in range(2):
                        dve.wait_ge(sm["g_exped"], 2 * b + t + 1)
                        dve.tensor_reduce(gsum[:, t, :], g2[:, t, :, :], AX, ALU.add).then_inc(sm["gsummed"], 1)
                        dve.wait_ge(sm["gsummed"], 2 * b + t + 1)
                        dve.reciprocal(ginv[:, t, :], gsum[:, t, :]).then_inc(sm["ginverted"], 1)
                    for q in range(2):
                        dve.wait_ge(sm["att_made"], 2 * b + q + 1)
                        dve.tensor_tensor(att[:, 4 * q:4 * q + 4, :], SC[:, q, :].rearrange("p (i c) -> p i c", i=4),
                                          own[:, 4 * q:4 * q + 4, :], ALU.mult).then_inc(sm["att_ready"], 1)
                    dve.wait_ge(sm["final"], b + 1)
                    at = ds(b * L, L)
                    dve.tensor_tensor(X[:, at], PJ[:, 0:L], X[:, at], ALU.add).then_inc(sm["trip_done"], 1)


def product_key_experts(nc, tag, X, XN, A, W, ident, eps):
    NH, NK, E = 8, 32, 1024
    U = 2
    NU = U * NH
    with Phase(nc, tag) as ph:
        wq = ph.sb("wq", [P, 16, P])
        keys = ph.sb("keys", [P, 2, NH, NK])
        fused = ph.sb("fused", [P, 2, NH, NK])
        down, up = ph.sb("down", [P, E]), ph.sb("up", [P, 8, P])
        gam, bet = ph.sb("gam", [P, 1]), ph.sb("bet", [P, 1])
        st, mv = ph.sb("st", [P, NBLK, 6]), ph.sb("mv", [P, 2])
        col = ph.sb("col", [P, 4])
        ms = ph.sb("ms", [P, 1])
        xb = ph.sb("xb", [P, U, P])
        sim = ph.sb("sim", [P, U, 2, NH, NK])
        top = ph.sb("top", [P, U, 2, NH, 8])
        cand = ph.sb("cand", [P, U, NH, 64])
        best = ph.sb("best", [P, U, NH, 8])
        S, sg, w = ph.sb("S", [P, 2, E]), ph.sb("sg", [P, 2, E]), ph.sb("w", [P, 2, E])
        act_h = ph.sb("act_h", [P, U, 8, P])
        mix = ph.sb("mix", [P, U, 8, P])
        SIM = ph.ps("SIM", [P, U, 512])
        WT = ph.ps("WT", [P, 2, 512])
        HT = ph.ps("HT", [P, 2, 512])
        OUT = ph.ps("OUT", [P, U, 512])
        names = ("loaded stats moments sds invs scales negs affine fused_made fused_ready normed sim_made sim_copied "
                 "tops cands bests summed sigm weighed w_turned h_made h_on mixed out_made trip_done passed").split()
        sm = {n: ph.sem(n) for n in names}
        loads = 16 * 6
        with nc.Block() as block:
            @block.sync
            def _(sp):
                load(sp, gam[:, :], W["gamma"].rearrange("(p c) -> p c", c=1), sm["loaded"])
                load(sp, bet[:, :], W["beta"].rearrange("(p c) -> p c", c=1), sm["loaded"])
                load(sp, wq[:, :, :], W["w_q"].rearrange("(n k) c -> k n c", k=P), sm["loaded"])
                load(sp, keys[:, :, :, :], W["keys"], sm["loaded"])
                load(sp, down[:, :], W["down"], sm["loaded"])
                load(sp, up[:, :, :], W["up"].rearrange("(n e) c -> e n c", e=P), sm["loaded"])

            @block.gpsimd
            def _(pool):
                with pool.Fori(0, NT // U) as g:
                    for k in range(NU):
                        s, h = k // NH, k % NH
                        if h == 0:
                            pool.wait_ge(sm["sim_copied"], U * g + s + 1)
                        if k >= 2:
                            pool.wait_ge(sm["weighed"], NU * g + k - 1)
                        else:
                            pool.wait_ge(sm["trip_done"], g + 1)
                        a = sim[:, s, 0, h, :].rearrange("p (i o) -> p i o", o=1).broadcast_to([P, NK, NK])
                        c = sim[:, s, 1, h, :].rearrange("p (o i) -> p o i", o=1).broadcast_to([P, NK, NK])
                        pool.tensor_tensor(S[:, k % 2, :].rearrange("p (a c) -> p a c", a=NK), a, c, ALU.add).then_inc(sm["summed"], 1)

            @block.tensor
            def _(pe):
                pe.wait_ge(sm["loaded"], loads)
                for n in range(16):
                    o = pe.matmul(SIM[:, 0, n * NK:(n + 1) * NK], wq[:, n, :], keys[:, n // NH, n % NH, :], start=True, stop=True)
                o.then_inc(sm["fused_made"], 1)
                pe.wait_ge(sm["fused_ready"], 1)
                with pe.Fori(0, NT // U) as g:
                    pe.wait_ge(sm["trip_done"], g + 1)
                    for s in range(U):
                        pe.wait_ge(sm["normed"], U * g + s + 1)
                        pe.matmul(SIM[:, s, :], xb[:, s, :], fused[:, :, :, :], start=True, stop=True).then_inc(sm["sim_made"], 1)
                    for s in range(U):
                        x = XN[:, ds((U * g + s) * P, P)]
                        if s:
                            pe.wait_ge(sm["h_on"], U * 2 * g + 2 * s)
                        for n in range(8):
                            o = pe.matmul(HT[:, n // 4, (n % 4) * P:(n % 4 + 1) * P], down[:, n * P:(n + 1) * P], x,
                                          start=True, stop=True)
                            if n % 4 == 3:
                                o.then_inc(sm["h_made"], 1)
                        if s:
                            pe.wait_ge(sm["mixed"], 2 * U * g + 2 * s)
                        for h in range(NH):
                            k = s * NH + h
                            pe.wait_ge(sm["weighed"], NU * g + k + 1)
                            for n in range(8):
                                o = pe.matmul(WT[:, n // 4, (n % 4) * P:(n % 4 + 1) * P], w[:, k % 2, n * P:(n + 1) * P],
                                              ident[:, :], start=h == 0 and n % 4 == 0, stop=h == NH - 1,
                                              is_transpose=True, skip_group_check=True)
                            o.then_inc(sm["w_turned"], 1)
                        pe.wait_ge(sm["mixed"], 2 * (U * g + s) + 2)
                        for n in range(8):
                            o = pe.matmul(OUT[:, s, 0:P], up[:, n, :], mix[:, s, n, :], start=n == 0, stop=n == 7)
                        o.then_inc(sm["out_made"], 1)

            @block.scalar
            def _(act):
                act.wait_ge(sm["moments"], 1)
                act.activation(col[:, 0:1], mv[:, 1:2], ACT.Sqrt, bias=eps[:, 0:1]).then_inc(sm["sds"], 1)
                act.wait_ge(sm["fused_made"], 1)
                act.activation(fused[:, :, :, :], SIM[:, 0, :].rearrange("p (a b c) -> p a b c", a=2, b=NH), ACT.Copy).then_inc(sm["fused_ready"], 1)
                act.wait_ge(sm["affine"], 1)
                with act.Fori(0, NT // U) as g:
                    act.wait_ge(sm["trip_done"], g + 1)
                    for s in range(U):
                        act.activation(xb[:, s, :], XN[:, ds((U * g + s) * P, P)], ACT.Identity, bias=col[:, 3:4],
                                       scale=col[:, 2:3]).then_inc(sm["normed"], 1)
                    for s in range(U):
                        act.wait_ge(sm["sim_made"], U * g + s + 1)
                        act.activation(sim[:, s, :, :, :], SIM[:, s, :].rearrange("p (a b c) -> p a b c", a=2, b=NH),
                                       ACT.Copy).then_inc(sm["sim_copied"], 1)
                    for s in range(U):
                        for q in range(2):
                            act.wait_ge(sm["h_made"], 2 * (U * g + s) + q + 1)
                            act.activation(act_h[:, s, 4 * q:4 * q + 4, :], HT[:, q, :].rearrange("p (n c) -> p n c", n=4),
                                           ACT.Gelu).then_inc(sm["h_on"], 1)
                        for h in range(NH):
                            k = s * NH + h
                            act.wait_ge(sm["summed"], NU * g + k + 1)
                            if k >= 2:
                                act.wait_ge(sm["weighed"], NU * g + k - 1)
                            act.activation(sg[:, k % 2, :], S[:, k % 2, :], ACT.Sigmoid).then_inc(sm["sigm"], 1)

            @block.vector
            def _(dve):
                dve.sem_inc(sm["trip_done"], 1)
                for j in range(NBLK):
                    dve.bn_stats(st[:, j, :], XN[:, j * BLK:(j + 1) * BLK]).then_inc(sm["stats"], 1)
                dve.wait_ge(sm["stats"], NBLK)
                dve.bn_aggr(mv[:, :], st[:, :, :]).then_inc(sm["moments"], 1)
                dve.wait_ge(sm["sds"], 1)
                dve.reciprocal(col[:, 1:2], col[:, 0:1]).then_inc(sm["invs"], 1)
                dve.wait_ge(sm["invs"], 1)
                dve.wait_ge(sm["loaded"], loads)
                dve.tensor_tensor(col[:, 2:3], col[:, 1:2], gam[:, :], ALU.mult).then_inc(sm["scales"], 1)
                dve.wait_ge(sm["scales"], 1)
                dve.tensor_tensor(ms[:, :], mv[:, 0:1], col[:, 2:3], ALU.mult).then_inc(sm["negs"], 1)
                dve.wait_ge(sm["negs"], 1)
                dve.tensor_tensor(col[:, 3:4], bet[:, :], ms[:, :], ALU.subtract).then_inc(sm["affine"], 1)
                with dve.Fori(0, NT // U) as g:
                    for s in range(U):
                        dve.wait_ge(sm["trip_done"], g + 1)
                        dve.wait_ge(sm["sim_copied"], U * g + s + 1)
                        dve.sem_inc(sm["passed"], 1)
                        for n in range(16):
                            o = dve.max(top[:, s, n // NH, n % NH, :], sim[:, s, n // NH, n % NH, :])
                        o.then_inc(sm["tops"], 1)
                        dve.wait_ge(sm["tops"], U * g + s + 1)
                        a = top[:, s, 0, :, :].rearrange("p h (i o) -> p h i o", o=1).broadcast_to([P, NH, 8, 8])
                        c = top[:, s, 1, :, :].rearrange("p h (o i) -> p h o i", o=1).broadcast_to([P, NH, 8, 8])
                        dve.tensor_tensor(cand[:, s, :, :].rearrange("p h (i j) -> p h i j", i=8), a, c, ALU.add).then_inc(sm["cands"], 1)
                        dve.wait_ge(sm["cands"], U * g + s + 1)
                        dve.sem_inc(sm["passed"], 1)
                        for h in range(NH):
                            o = dve.max(best[:, s, h, :], cand[:, s, h, :])
                        o.then_inc(sm["bests"], 1)
                    for s in range(U):
                        dve.wait_ge(sm["bests"], U * g + s + 1)
                        for h in range(NH):
                            k = s * NH + h
                            dve.wait_ge(sm["sigm"], NU * g + k + 1)
                            if k >= 2:
                                dve.wait_ge(sm["w_turned"], NU * g + k - 1)
                            dve.scalar_tensor_tensor(w[:, k % 2, :], S[:, k % 2, :], best[:, s, h, 7:8], sg[:, k % 2, :],
                                                     ALU.is_ge, ALU.mult).then_inc(sm["weighed"], 1)
                        dve.wait_ge(sm["w_turned"], NU * g + s * NH + NH)
                        dve.wait_ge(sm["h_on"], 2 * (U * g + s) + 2)
                        for q in range(2):
                            dve.tensor_tensor(mix[:, s, 4 * q:4 * q + 4, :], WT[:, q, :].rearrange("p (n c) -> p n c", n=4),
                                              act_h[:, s, 4 * q:4 * q + 4, :], ALU.mult).then_inc(sm["mixed"], 1)
                    for s in range(U):
                        dve.wait_ge(sm["out_made"], U * g + s + 1)
                        at = ds((U * g + s) * P, P)
                        o = dve.scalar_tensor_tensor(X[:, at], OUT[:, s, 0:P], 0.5, X[:, at], ALU.mult, ALU.add)
                    o.then_inc(sm["trip_done"], 1)


NE, CAP = 64, 64
NPAIRS = NE // 2


def routed_experts(nc, tag, X, XN, A, W, ident, rows_dram):
    NPAIR = NE // 2
    with ExitStack() as keep:
        place = keep.enter_context(nc.sbuf_tensor(f"{tag}_place", [P, NT, NE], F32))
        vals = keep.enter_context(nc.sbuf_tensor(f"{tag}_vals", [P, NT, NPAIR, 3], F32))
        info = keep.enter_context(nc.sbuf_tensor(f"{tag}_info", [P, NPAIR, 3], F32))
        Eout = keep.enter_context(nc.sbuf_tensor(f"{tag}_Eout", [P, NPAIR, P], F32))
        route(nc, tag + "r", XN, A, W, ident, rows_dram, place, vals)
        find_slots(nc, tag + "s", A, place, vals, info)
        run_experts(nc, tag + "e", A, W, ident, rows_dram, info, Eout)
        combine(nc, tag + "c", X, XN, W, info, Eout)


def route(nc, tag, XN, A, W, ident, rows_dram, place, vals):
    with Phase(nc, tag) as ph:
        wr = ph.sb("wr", [P, NE])
        tri, ones, token = ph.sb("tri", [P, P]), ph.sb("ones", [P, P]), ph.sb("token", [P, NT])
        U = 2
        xs = ph.sb("xs", [P, U, P])
        rows = ph.sb("rows", [P, U, P])
        sc, masked, left, sel = (ph.sb(n, [P, U, NE]) for n in ("sc", "masked", "left", "sel"))
        gmax, gtop, gopen, top = (ph.sb(n, [P, U, 8]) for n in ("gmax", "gtop", "gopen", "top"))
        tsum, tclip, tinv = (ph.sb(n, [P, U]) for n in ("tsum", "tclip", "tinv"))
        wsel, wall, pos = (ph.sb(n, [P, U, NE]) for n in ("wsel", "wall", "pos"))
        before = ph.sb("before", [P, 2, NE])
        LG, RW, CN = ph.ps("LG", [P, U, 512]), ph.ps("RW", [P, U, 512]), ph.ps("CN", [P, U, 512])
        names = ("loaded staged logits rows_made rows_copied rows_out scored gmaxed gtopped gopened masks topped lefted "
                 "selected tsums tclips tinvs wsels walls vals_made counted before_made poss places zeroed trip_done passed").split()
        sm = {n: ph.sem(n) for n in names}
        with nc.Block() as block:
            @block.sync
            def _(sp):
                for dst, src in ((wr, W["router"]), (tri, A["tri"]), (ones, A["ones"]), (token, A["token"])):
                    load(sp, dst[:, :], src, sm["loaded"])
                sp.sem_inc(sm["rows_out"], 16)
                with sp.Fori(0, NT // U) as g:
                    for s in range(U):
                        sp.wait_ge(sm["rows_copied"], U * g + s + 1)
                        sp.dma_start(rows_dram[ds((U * g + s) * P, P), :], rows[:, s, :]).then_inc(sm["rows_out"], 16)
                sp.wait_ge(sm["rows_out"], 16 * NT + 16)

            @block.tensor
            def _(pe):
                pe.wait_ge(sm["loaded"], 64)
                pe.wait_ge(sm["zeroed"], 1)
                with pe.Fori(0, NT // U) as g:
                    pe.wait_ge(sm["trip_done"], g + 1)
                    for s in range(U):
                        pe.wait_ge(sm["staged"], U * g + s + 1)
                        pe.matmul(LG[:, s, 0:NE], xs[:, s, :], wr[:, :], start=True, stop=True).then_inc(sm["logits"], 1)
                        pe.transpose(RW[:, s, 0:P], xs[:, s, :], ident[:, :]).then_inc(sm["rows_made"], 1)
                    for s in range(U):
                        pe.wait_ge(sm["selected"], U * g + s + 1)
                        pe.matmul(CN[:, s, 0:NE], tri[:, :], sel[:, s, :], start=True, stop=False)
                        pe.wait_ge(sm["before_made"], U * g + s + 1)
                        pe.matmul(CN[:, s, 0:NE], ones[:, :], before[:, s, :], start=False, stop=True).then_inc(sm["counted"], 1)

            @block.scalar
            def _(act):
                with act.Fori(0, NT // U) as g:
                    act.wait_ge(sm["trip_done"], g + 1)
                    act.wait_ge(sm["rows_out"], 16 * U * g + 16)
                    for s in range(U):
                        act.activation(xs[:, s, :], XN[:, ds((U * g + s) * P, P)], ACT.Copy).then_inc(sm["staged"], 1)
                    for s in range(U):
                        act.wait_ge(sm["logits"], U * g + s + 1)
                        act.activation(sc[:, s, :], LG[:, s, 0:NE], ACT.Sigmoid).then_inc(sm["scored"], 1)
                        act.wait_ge(sm["rows_made"], U * g + s + 1)
                        act.activation(rows[:, s, :], RW[:, s, 0:P], ACT.Copy).then_inc(sm["rows_copied"], 1)

            @block.vector
            def _(dve):
                dve.sem_inc(sm["trip_done"], 1)
                dve.sem_inc(sm["before_made"], 1)
                dve.memset(before[:, :, :], 0.0).then_inc(sm["zeroed"], 1)
                dve.wait_ge(sm["zeroed"], 1)
                dve.wait_ge(sm["loaded"], 64)
                with dve.Fori(0, NT // U) as g:
                    at = lambda s: U * g + s + 1
                    grp = lambda ap: ap.rearrange("p (g e) -> p g e", g=8)
                    dve.wait_ge(sm["trip_done"], g + 1)
                    for s in range(U):
                        dve.wait_ge(sm["scored"], at(s))
                        dve.tensor_reduce(gmax[:, s, :], grp(sc[:, s, :]), AX, ALU.max).then_inc(sm["gmaxed"], 1)
                    for s in range(U):
                        dve.wait_ge(sm["gmaxed"], at(s))
                        dve.sem_inc(sm["passed"], 1)
                        dve.max(gtop[:, s, :], gmax[:, s, :]).then_inc(sm["gtopped"], 1)
                    for s in range(U):
                        dve.wait_ge(sm["gtopped"], at(s))
                        dve.tensor_scalar(gopen[:, s, :], gmax[:, s, :], gtop[:, s, 3:4], None, ALU.is_ge).then_inc(sm["gopened"], 1)
                    for s in range(U):
                        dve.wait_ge(sm["gopened"], at(s))
                        dve.tensor_tensor(grp(masked[:, s, :]), grp(sc[:, s, :]),
                                          gopen[:, s, :].rearrange("p (g o) -> p g o", o=1).broadcast_to([P, 8, 8]),
                                          ALU.mult).then_inc(sm["masks"], 1)
                    for s in range(U):
                        dve.wait_ge(sm["masks"], at(s))
                        dve.sem_inc(sm["passed"], 1)
                        dve.max(top[:, s, :], masked[:, s, :]).then_inc(sm["topped"], 1)
                    for s in range(U):
                        dve.wait_ge(sm["topped"], at(s))
                        dve.sem_inc(sm["passed"], 1)
                        dve.match_replace(left[:, s, :], top[:, s, :], masked[:, s, :], -1.0).then_inc(sm["lefted"], 1)
                    for s in range(U):
                        dve.wait_ge(sm["lefted"], at(s))
                        dve.tensor_tensor(sel[:, s, :], left[:, s, :], masked[:, s, :], ALU.not_equal).then_inc(sm["selected"], 1)
                        dve.tensor_reduce(tsum[:, s:s + 1], top[:, s, :], AX, ALU.add).then_inc(sm["tsums"], 1)
                    for s in range(U):
                        dve.wait_ge(sm["tsums"], at(s))
                        dve.tensor_scalar(tclip[:, s:s + 1], tsum[:, s:s + 1], 1e-9, None, ALU.max).then_inc(sm["tclips"], 1)
                    for s in range(U):
                        dve.wait_ge(sm["tclips"], at(s))
                        dve.reciprocal(tinv[:, s:s + 1], tclip[:, s:s + 1]).then_inc(sm["tinvs"], 1)
                    for s in range(U):
                        dve.wait_ge(sm["selected"], at(s))
                        dve.tensor_tensor(wsel[:, s, :], sel[:, s, :], masked[:, s, :], ALU.mult).then_inc(sm["wsels"], 1)
                    for s in range(U):
                        dve.wait_ge(sm["tinvs"], at(s))
                        dve.wait_ge(sm["wsels"], at(s))
                        one = vals[:, ds(U * g + s, 1), :, :].rearrange("p o n c -> p (o n) c")
                        dve.tensor_scalar(one[:, :, 1:3], wsel[:, s, :].rearrange("p (n e) -> p n e", e=2), tinv[:, s:s + 1],
                                          2.5, ALU.mult, ALU.mult).then_inc(sm["walls"], 1)
                        dve.tensor_copy(one[:, :, 0], token[:, ds(U * g + s, 1)].broadcast_to([P, NE // 2])).then_inc(sm["vals_made"], 1)
                    for s in range(U):
                        dve.wait_ge(sm["counted"], at(s))
                        dve.wait_ge(sm["before_made"], U * g + s + 1)
                        dve.tensor_tensor(before[:, 1 - s, :], before[:, s, :], sel[:, s, :], ALU.add).then_inc(sm["before_made"], 1)
                        dve.tensor_scalar(pos[:, s, :], CN[:, s, 0:NE], 1.0, None, ALU.add).then_inc(sm["poss"], 1)
                    for s in range(U):
                        dve.wait_ge(sm["poss"], at(s))
                        o = dve.tensor_tensor(place[:, ds(U * g + s, 1), :].rearrange("p o e -> p (o e)"), pos[:, s, :],
                                              sel[:, s, :], ALU.mult)
                    o.then_inc(sm["trip_done"], 1)


def find_slots(nc, tag, A, place, vals, info):
    GE = 8
    NPG = GE // 2
    BF = mybir.dt.bfloat16
    NV = NT * NPAIRS * 3
    with Phase(nc, tag) as ph:
        slot1 = ph.sb("slot1", [P, GE, 64])
        R = 6
        hot = ph.sb("hot", [P, R, GE * CAP], BF)
        part = ph.sb("part", [P, NT, NPAIRS, 9], BF)
        rest1, rest2 = ph.sb("rest1", [P, NT, NPAIRS * 3]), ph.sb("rest2", [P, NT, NPAIRS * 3])
        zero = ph.sb("zero", [P, P], BF)
        pair_sum = ph.sb("pair_sum", [P, NPG, 3])
        IN = ph.ps("IN", [P, 2, 512])
        names = "loaded slots zeroed split hots used summed first_sum trip_done".split()
        sm = {n: ph.sem(n) for n in names}
        v3 = vals[:, :, :, :].rearrange("p t n c -> p (t n) c")
        p9 = part[:, :, :, :].rearrange("p t n c -> p (t n) c")
        r1, r2 = (r[:, :, :].rearrange("p t (n c) -> p (t n) c", c=3) for r in (rest1, rest2))
        with nc.Block() as block:
            @block.gpsimd
            def _(pool):
                pool.memset(zero[:, :], 0.0).then_inc(sm["zeroed"], 1)
                pool.iota(slot1[:, :, :], pattern=[[0, GE], [1, 64]], base=1, channel_multiplier=0,
                          allow_small_or_imprecise_dtypes=True).then_inc(sm["slots"], 1)

            @block.vector
            def _(dve):
                dve.sem_inc(sm["trip_done"], 1)
                dve.tensor_copy(p9[:, :, 0:3], v3).then_inc(sm["split"], 1)
                dve.wait_ge(sm["split"], 1)
                dve.tensor_tensor(r1, v3, p9[:, :, 0:3], ALU.subtract).then_inc(sm["split"], 1)
                dve.wait_ge(sm["split"], 2)
                dve.tensor_copy(p9[:, :, 3:6], r1).then_inc(sm["split"], 1)
                dve.wait_ge(sm["split"], 3)
                dve.tensor_tensor(r2, r1, p9[:, :, 3:6], ALU.subtract).then_inc(sm["split"], 1)
                dve.wait_ge(sm["split"], 4)
                dve.tensor_copy(p9[:, :, 6:9], r2).then_inc(sm["split"], 1)
                dve.wait_ge(sm["slots"], 1)
                with dve.Fori(0, NE // GE) as g:
                    for n in range(NT):
                        if n >= R:
                            dve.wait_ge(sm["used"], NT * g + n - R + 1)
                        else:
                            dve.wait_ge(sm["trip_done"], g + 1)
                        a = place[:, n, ds(g * GE, GE)].rearrange("p (e o) -> p e o", o=1).broadcast_to([P, GE, CAP])
                        dve.tensor_tensor(hot[:, n % R, :].rearrange("p (e c) -> p e c", e=GE), a, slot1[:, :, :],
                                          ALU.is_equal).then_inc(sm["hots"], 1)
                    dve.wait_ge(sm["summed"], g + 1)
                    tot = IN[:, 0, 0:9 * NPG].rearrange("p (n k c) -> p n k c", k=3, c=3)
                    dve.tensor_copy(pair_sum[:, :, :], tot[:, :, 2, :]).then_inc(sm["first_sum"], 1)
                    dve.wait_ge(sm["first_sum"], 2 * g + 1)
                    dve.tensor_tensor(pair_sum[:, :, :], tot[:, :, 1, :], pair_sum[:, :, :], ALU.add).then_inc(sm["first_sum"], 1)
                    dve.wait_ge(sm["first_sum"], 2 * g + 2)
                    dve.tensor_tensor(info[:, ds(g * NPG, NPG), :], tot[:, :, 0, :], pair_sum[:, :, :],
                                      ALU.add).then_inc(sm["trip_done"], 1)

            @block.tensor
            def _(pe):
                pe.wait_ge(sm["zeroed"], 1)
                pe.wait_ge(sm["split"], 5)
                with pe.Fori(0, NE // GE) as g:
                    pe.wait_ge(sm["trip_done"], g + 1)
                    pe.matmul(IN[:, 0, 0:9 * NPG], zero[:, :], zero[:, 0:9 * NPG], start=True, stop=True, skip_group_check=True)
                    for n in range(NT):
                        pe.wait_ge(sm["hots"], NT * g + n + 1)
                        for q in range(NPG):
                            o = pe.matmul(IN[:, 0, 9 * q:9 * q + 9], hot[:, n % R, q * P:(q + 1) * P],
                                          part[:, n, ds(g * NPG + q, 1), :].rearrange("p o c -> p (o c)"),
                                          start=False, stop=True, skip_group_check=True)
                        o.then_inc(sm["used"], 1)
                    pe.wait_ge(sm["used"], NT * g + NT)
                    pe.matmul(IN[:, 0, 0:9 * NPG], zero[:, :], zero[:, 0:9 * NPG], start=False, stop=True,
                              skip_group_check=True).then_inc(sm["summed"], 1)


def run_experts(nc, tag, A, W, ident, rows_dram, info, Eout):
    U = 2
    NPAIR = NE // 2
    with Phase(nc, tag) as ph:
        own = ph.sb("own", [P, P])
        tok = ph.sb("tok", [P, NPAIR], I32)
        ws = ph.sb("ws", [P, NPAIR])
        idx = ph.sb("idx", [P, U], I32)
        wgt, wut, wdt = ph.sb("wgt", [P, U, 2, 64]), ph.sb("wut", [P, U, 2, 64]), ph.sb("wdt", [P, U, P])
        xg, xT, gt, g2, hm = (ph.sb(n, [P, U, P]) for n in ("xg", "xT", "gt", "g2", "hm"))
        TR, GU, OU = ph.ps("TR", [P, U, 512]), ph.ps("GU", [P, U, 512]), ph.ps("OU", [P, U, 512])
        names = ("loaded toks wss own_in idxs gathered0 gathered1 turned copied gu_made gated ups hids outs weights0 weights1 "
                 "trip_done passed").split()
        sm = {n: ph.sem(n) for n in names}
        gate_w = W["gate"].rearrange("(n e) h i -> n h e i", e=2)
        up_w = W["up"].rearrange("(n e) h i -> n h e i", e=2)
        down_w = W["down"].rearrange("(n e) i h -> n (e i) h", e=2)
        with nc.Block() as block:
            @block.sync
            def _(sp):
                load(sp, own[:, :], A["block64"], sm["own_in"])
                with sp.Fori(0, NPAIR // U) as g:
                    sp.wait_ge(sm["trip_done"], g + 1)
                    for s in range(U):
                        n = U * g + s
                        w = sm[f"weights{s}"]
                        load(sp, wgt[:, s, :, :], gate_w[ds(n, 1)].rearrange("o h e i -> h (o e) i"), w)
                        load(sp, wut[:, s, :, :], up_w[ds(n, 1)].rearrange("o h e i -> h (o e) i"), w)
                        load(sp, wdt[:, s, :], down_w[ds(n, 1)].rearrange("o p h -> (o p) h"), w)

            @block.gpsimd
            def _(pool):
                with pool.Fori(0, NPAIR // U) as g:
                    pool.wait_ge(sm["trip_done"], g + 1)
                    for s in range(U):
                        pool.wait_ge(sm["idxs"], U * g + s + 1)
                        pool.sem_inc(sm["passed"], 1)
                        pool.indirect_dma_start(out=xg[:, s, :], out_offset=None, in_=rows_dram[:, :],
                                                in_offset=bass.IndirectOffsetOnAxis(ap=idx[:, s:s + 1], axis=0)
                                                ).then_inc(sm[f"gathered{s}"], 16)

            @block.tensor
            def _(pe):
                with pe.Fori(0, NPAIR // U) as g:
                    for s in range(U):
                        pe.wait_ge(sm[f"gathered{s}"], 16 * g + 16)
                        pe.wait_ge(sm["trip_done"], g + 1)
                        pe.transpose(TR[:, s, 0:P], xg[:, s, :], ident[:, :]).then_inc(sm["turned"], 1)
                    for s in range(U):
                        pe.wait_ge(sm["copied"], U * g + s + 1)
                        pe.wait_ge(sm[f"weights{s}"], 48 * g + 48)
                        pe.matmul(GU[:, s, 0:P], wgt[:, s, :, :].rearrange("p e i -> p (e i)"), xT[:, s, :], start=True, stop=True)
                        pe.matmul(GU[:, s, P:2 * P], wut[:, s, :, :].rearrange("p e i -> p (e i)"), xT[:, s, :], start=True,
                                  stop=True).then_inc(sm["gu_made"], 1)
                    for s in range(U):
                        pe.wait_ge(sm["hids"], U * g + s + 1)
                        pe.matmul(OU[:, s, 0:P], hm[:, s, :], wdt[:, s, :], start=True, stop=True).then_inc(sm["outs"], 1)

            @block.scalar
            def _(act):
                with act.Fori(0, NPAIR // U) as g:
                    for s in range(U):
                        act.wait_ge(sm["turned"], U * g + s + 1)
                        act.wait_ge(sm["trip_done"], g + 1)
                        act.activation(xT[:, s, :], TR[:, s, 0:P], ACT.Copy).then_inc(sm["copied"], 1)
                    for s in range(U):
                        act.wait_ge(sm["gu_made"], U * g + s + 1)
                        act.activation(gt[:, s, :], GU[:, s, 0:P], ACT.Silu).then_inc(sm["gated"], 1)

            @block.vector
            def _(dve):
                dve.sem_inc(sm["trip_done"], 1)
                dve.tensor_copy(tok[:, :], info[:, :, 0]).then_inc(sm["toks"], 1)
                dve.tensor_copy(ws[0:64, :], info[0:64, :, 1])
                dve.tensor_copy(ws[64:P, :], info[64:P, :, 2]).then_inc(sm["wss"], 1)
                dve.wait_ge(sm["toks"], 1)
                dve.wait_ge(sm["wss"], 1)
                dve.wait_ge(sm["own_in"], 16)
                with dve.Fori(0, NPAIR // U) as g:
                    dve.wait_ge(sm["trip_done"], g + 1)
                    for s in range(U):
                        dve.tensor_copy(idx[:, s:s + 1], tok[:, ds(U * g + s, 1)]).then_inc(sm["idxs"], 1)
                    for s in range(U):
                        dve.wait_ge(sm["gated"], U * g + s + 1)
                        dve.tensor_tensor(g2[:, s, :], GU[:, s, P:2 * P], gt[:, s, :], ALU.mult).then_inc(sm["ups"], 1)
                    for s in range(U):
                        dve.wait_ge(sm["ups"], U * g + s + 1)
                        dve.tensor_tensor(hm[:, s, :], g2[:, s, :], own[:, :], ALU.mult).then_inc(sm["hids"], 1)
                    for s in range(U):
                        dve.wait_ge(sm["outs"], U * g + s + 1)
                        o = dve.tensor_scalar(Eout[:, ds(U * g + s, 1), :].rearrange("p o c -> p (o c)"), OU[:, s, 0:P],
                                              ws[:, ds(U * g + s, 1)], None, ALU.mult)
                    o.then_inc(sm["trip_done"], 1)


def combine(nc, tag, X, XN, W, info, Eout):
    NPAIR = NE // 2
    with Phase(nc, tag) as ph:
        lane = ph.sb("lane", [P, T])
        R = 4
        hot = ph.sb("hot", [P, R, BLK])
        sgw, suw, sdw = ph.sb("sgw", [P, 64]), ph.sb("suw", [P, 64]), ph.sb("sdw", [64, P])
        gt, hid = ph.sb("gt", [64, BLK]), ph.sb("hid", [64, BLK])
        SG, SU, OUT = ph.ps("SG", [P, 512]), ph.ps("SU", [P, 512]), ph.ps("OUT", [P, 512])
        names = "loaded counted g_made u_made gated hids hots used out_made trip_done".split()
        sm = {n: ph.sem(n) for n in names}
        with nc.Block() as block:
            @block.sync
            def _(sp):
                for dst, n in ((sgw, "sgate"), (suw, "sup"), (sdw, "sdown")):
                    load(sp, dst[:, :], W[n], sm["loaded"])

            @block.gpsimd
            def _(pool):
                pool.iota(lane[:, :], pattern=[[1, T]], base=0, channel_multiplier=0,
                          allow_small_or_imprecise_dtypes=True).then_inc(sm["counted"], 1)

            @block.tensor
            def _(pe):
                pe.wait_ge(sm["loaded"], 48)
                with pe.Fori(0, NBLK) as g:
                    x = XN[:, ds(g * BLK, BLK)]
                    pe.wait_ge(sm["trip_done"], g + 1)
                    pe.matmul(SG[0:64, :], sgw[:, :], x, start=True, stop=True).then_inc(sm["g_made"], 1)
                    pe.matmul(SU[0:64, :], suw[:, :], x, start=True, stop=True).then_inc(sm["u_made"], 1)
                    for n in range(NPAIR):
                        pe.wait_ge(sm["hots"], NPAIR * g + n + 1)
                        pe.matmul(OUT[:, :], Eout[:, n, :], hot[:, n % R, :], start=n == 0, stop=False).then_inc(sm["used"], 1)
                    pe.wait_ge(sm["hids"], g + 1)
                    pe.matmul(OUT[:, :], sdw[:, :], hid[:, :], start=False, stop=True).then_inc(sm["out_made"], 1)

            @block.scalar
            def _(act):
                with act.Fori(0, NBLK) as g:
                    act.wait_ge(sm["g_made"], g + 1)
                    act.wait_ge(sm["trip_done"], g + 1)
                    act.activation(gt[:, :], SG[0:64, :], ACT.Silu).then_inc(sm["gated"], 1)

            @block.vector
            def _(dve):
                dve.sem_inc(sm["trip_done"], 1)
                dve.wait_ge(sm["counted"], 1)
                with dve.Fori(0, NBLK) as g:
                    at = ds(g * BLK, BLK)
                    for n in range(NPAIR):
                        if n >= R:
                            dve.wait_ge(sm["used"], NPAIR * g + n - R + 1)
                        else:
                            dve.wait_ge(sm["trip_done"], g + 1)
                        dve.tensor_scalar(hot[:, n % R, :], lane[:, at], info[:, n, 0:1], None, ALU.is_equal).then_inc(sm["hots"], 1)
                        if n == 4:
                            dve.wait_ge(sm["gated"], g + 1)
                            dve.wait_ge(sm["u_made"], g + 1)
                            dve.wait_ge(sm["trip_done"], g + 1)
                            dve.tensor_tensor(hid[:, :], SU[0:64, :], gt[:, :], ALU.mult).then_inc(sm["hids"], 1)
                    dve.wait_ge(sm["out_made"], g + 1)
                    dve.scalar_tensor_tensor(X[:, at], OUT[:, :], 0.5, X[:, at], ALU.mult, ALU.add).then_inc(sm["trip_done"], 1)


def build(nc, a, out):
    C = {n[2:]: v for n, v in a.items() if n.startswith("c_")}
    rows_dram = nc.dram_tensor("token_rows", (T, D), F32).ap()
    with ExitStack() as ctx:
        def sb(name, shape):
            return ctx.enter_context(nc.sbuf_tensor(name, shape, F32))

        X, XN = sb("X", [P, T]), sb("XN", [P, T])
        ident, ones_mean, eps = sb("ident", [P, P]), sb("ones_mean", [P, P]), sb("eps", [P, 1])
        with Phase(nc, "common") as ph:
            loaded = ph.sem("loaded")
            with nc.Block() as block:
                @block.sync
                def _(sp):
                    load(sp, ident[:, :], C["eye"], loaded)
                    load(sp, ones_mean[:, :], C["ones_mean"], loaded)
                    sp.wait_ge(loaded, 32)

                @block.vector
                def _(dve):
                    dve.memset(eps[:, :], LN_EPS)

        def norm(tag):
            layer_norm(nc, tag + "_norm", X, XN, ones_mean, eps)

        def pick(prefix, **names):
            return {k: a[prefix + v] for k, v in names.items()}

        def layer0_ffn(tag):
            norm(tag)
            product_key_experts(nc, tag, X, XN, C, pick("L0_ffn_", gamma="bn_gamma", beta="bn_beta", w_q="w_q",
                                                        keys="keys_p", down="down", up="up"), ident, eps)

        def layer1_ffn(tag):
            norm(tag)
            for n in range(2):
                w = {k: a["L1_ffn_" + k][n] for k in ("q", "k", "v", "q_crossed", "k_crossed", "qk_scale", "w1", "b1",
                                                      "w2", "b2", "ln_g", "ln_b")}
                w["o"] = a["L1_ffn_wo"][n].rearrange("(g p) d -> p g d", p=P)
                attention(nc, f"{tag}_att{n}", "win", XN, XN, C, w, ident)
                gated_ffn(nc, f"{tag}_ff{n}", "gelu", XN, XN, C, w, ones_mean, eps)
            add_half(nc, tag + "_add", X, XN)

        def layer2_ffn(tag):
            norm(tag)
            routed_experts(nc, tag, X, XN, C, pick("L2_ffn_", router="router_w", gate="gate_w", up="up_w", down="down_w",
                                                   sgate="shared_gate_w", sup="shared_up_w", sdown="shared_down_w"),
                           ident, rows_dram)

        def layer3_ffn(tag):
            norm(tag)
            gated_ffn(nc, tag, "int8", X, XN, C, pick("L3_ffn_", gate="w_gate", up="w_up", down="w_down"))

        enter_stream(nc, a["L0_attn_w"], X, ident)
        layer0_ffn("l0a")
        norm("l0att")
        attention(nc, "l0att", "rel", X, XN, C,
                  {"o": C["eye"], **pick("L0_attn_", q="Wq", k="Wk", v="Wv", r="Wr", r_crossed="Wr_crossed", u="u_bias",
                                         v_bias="v_bias")}, ident)
        layer0_ffn("l0b")
        layer1_ffn("l1a")
        norm("l1att")
        attention(nc, "l1att", "rope", X, XN, C,
                  pick("L1_attn_", q="q", k="k", v="v", q_crossed="q_crossed", k_crossed="k_crossed", o="W_o"), ident)
        layer1_ffn("l1b")
        layer2_ffn("l2a")
        norm("l2att")
        attention(nc, "l2att", "full", X, XN, C, pick("L2_attn_", q="W_q", k="W_k", v="W_v", bias="bias"), ident)
        layer2_ffn("l2b")
        layer3_ffn("l3a")
        norm("l3att")
        latent_attention(nc, "l3att", X, XN, C, pick("L3_attn_", k="W_k", k_crossed="k_crossed", v="W_v", p="W_p", g="W_g",
                                                     q="latent_queries"), ident)
        layer3_ffn("l3b")
        leave_stream(nc, X, out, ident)


def laid_out(inputs):
    w = {n: np.asarray(v) for n, v in inputs.items()}
    a = {"L0_attn_w": w["L0_attn_w"]}

    def crossed(m, half):
        return m.reshape(-1, 2, half, m.shape[-1])[:, ::-1].reshape(m.shape)

    for n in ("Wq", "Wk", "Wv"):
        a["L0_attn_" + n] = w["L0_attn_" + n].T
    a["L0_attn_Wr"] = w["L0_attn_Wr"]
    a["L0_attn_Wr_crossed"] = crossed(w["L0_attn_Wr"].T, 1).T
    for n in ("u_bias", "v_bias"):
        a["L0_attn_" + n] = w["L0_attn_" + n].reshape(D, 1)
    for n in ("bn_gamma", "bn_beta", "w_q"):
        a["L0_ffn_" + n] = w["L0_ffn_" + n]
    a["L0_ffn_keys_p"] = w["L0_ffn_keys_p"].transpose(3, 2, 0, 1)
    a["L0_ffn_down"] = w["L0_ffn_down"][:1024].T
    a["L0_ffn_up"] = w["L0_ffn_up"][:1024]
    q, k, v = np.split(w["L1_attn_W_qkv"], 3, axis=0)
    a["L1_attn_q"], a["L1_attn_k"], a["L1_attn_v"] = q.T, k.T, v.T
    a["L1_attn_q_crossed"], a["L1_attn_k_crossed"] = crossed(q, 1).T, crossed(k, 1).T
    a["L1_attn_W_o"] = w["L1_attn_W_o"].T
    q, k, v = np.split(w["L1_ffn_wqkv"], 3, axis=2)
    a["L1_ffn_q"], a["L1_ffn_k"], a["L1_ffn_v"] = q, k, v
    for n, m in (("q", q), ("k", k)):
        a[f"L1_ffn_{n}_crossed"] = np.stack([crossed(x.T, 32).T for x in m])
    qs, ks = w["L1_ffn_q_scale"], w["L1_ffn_k_scale"]
    both = np.stack([qs, ks], axis=1)
    other = np.concatenate([both[:, :, 32:], both[:, :, :32]], axis=2)
    scales = np.stack([both, other], axis=1)
    a["L1_ffn_qk_scale"] = np.concatenate([scales, scales], axis=3).transpose(0, 3, 1, 2)
    for n in ("wo", "w1", "b1", "w2", "b2", "ln_g", "ln_b"):
        a["L1_ffn_" + n] = w["L1_ffn_" + n]
    for n in ("W_q", "W_k", "W_v"):
        a["L2_attn_" + n] = w["L2_attn_" + n]
    a["L2_attn_bias"] = np.stack([w["L2_attn_b_" + n] for n in "qkv"], axis=1)
    for n in ("router_w", "gate_w", "up_w", "down_w", "shared_gate_w", "shared_up_w", "shared_down_w"):
        a["L2_ffn_" + n] = w["L2_ffn_" + n]
    for n in ("W_k", "W_v", "W_p", "W_g"):
        a["L3_attn_" + n] = w["L3_attn_" + n].T
    a["L3_attn_k_crossed"] = crossed(w["L3_attn_W_k"], 1).T
    a["L3_attn_latent_queries"] = w["L3_attn_latent_queries"][0].transpose(1, 2, 0)
    for n in ("w_gate", "w_up", "w_down"):
        a["L3_ffn_" + n] = w["L3_ffn_" + n].T
    return a


def kernel(**inputs):
    import concourse.bacc as bacc
    from concourse.bass_utils import run_bass_kernel_spmd

    nc = bacc.Bacc("TRN2", target_bir_lowering=False, num_devices=1)
    arrays = {n: np.ascontiguousarray(v) for n, v in laid_out(inputs).items()}
    arrays.update({"c_" + n: v for n, v in constants().items()})
    tensors = {n: nc.dram_tensor(n, v.shape, mybir.dt.from_np(v.dtype), kind="ExternalInput").ap() for n, v in arrays.items()}
    out = nc.dram_tensor("out", (NB, L, D), F32, kind="ExternalOutput").ap()
    build(nc, tensors, out)
    r = run_bass_kernel_spmd(nc, [arrays], core_ids=[0])
    return r.results[0]["out"]
```

```python
from contextlib import ExitStack

import numpy as np

import concourse.bass as bass
from concourse import mybir

F32 = mybir.dt.float32
I32 = mybir.dt.int32
U32 = mybir.dt.uint32
ALU = mybir.AluOpType
ACT = mybir.ActivationFunctionType
AX = mybir.AxisListType.X
ds = bass.ds

P = 128
D = 128
NB = 16
L = 256
T = NB * L
AHEAD = 2 * L
NT = T // P
BLK = 512
NBLK = T // BLK
LN_EPS = 1e-5


class Phase:

    def __init__(self, nc, tag):
        self.nc, self.tag, self.sems, self.ctx = nc, tag, [], ExitStack()

    def __enter__(self):
        return self

    def sb(self, name, shape, dt=F32):
        return self.ctx.enter_context(self.nc.sbuf_tensor(f"{self.tag}_{name}", shape, dt))

    def ps(self, name, shape, dt=F32):
        return self.ctx.enter_context(self.nc.psum_tensor(f"{self.tag}_{name}", shape, dt))

    def sem(self, name):
        s = self.nc.alloc_semaphore(f"{self.tag}_{name}")
        self.sems.append(s)
        return s

    def __exit__(self, *exc):
        if exc[0] is None:
            self.nc.clear_and_free_semaphores(self.sems)
            self.nc.all_engine_barrier()
            self.ctx.close()
        return False


def constants():
    f = np.float32
    out = {}
    out["ones_mean"] = np.full((P, P), 1.0 / D, f)
    out["eye"] = np.eye(P, dtype=f)
    freq = (1.0 / 10000.0 ** (np.arange(0, D, 2, dtype=f) / f(D))).astype(f).astype(np.float64)
    j = np.arange(L, dtype=np.float64)

    def table(pos):
        a = freq[:, None] * pos[None, :]
        t = np.zeros((D, len(pos)))
        t[0::2], t[1::2] = np.sin(a), np.cos(a)
        return t.astype(f)

    out["rel_low"] = table(L - 1 + j)
    out["rel_up"] = table(j - L)
    a = freq[:, None] * j[None, :]
    turn = np.zeros((D, 2, L))
    turn[0::2, 0], turn[1::2, 0] = np.cos(a), np.cos(a)
    turn[0::2, 1], turn[1::2, 1] = np.sin(a), -np.sin(a)
    out["rel_turn"] = turn.astype(f)
    i, k = np.arange(P)[:, None], np.arange(P)[None, :]
    mask = np.zeros((P, 2, 2, P), f)
    mask[:, 0, 0], mask[:, 1, 0] = k <= i, k <= i
    mask[:, 0, 1] = (k + 1) >= i + 2
    mask[:, 1, 1] = k >= i + 2
    out["rel_mask"] = mask
    q = np.arange(P)[:, None, None] + P * np.arange(2)[None, :, None]
    kk = np.arange(L)[None, None, :]
    out["causal"] = np.where(kk <= q, 0.0, -1e30).astype(f)
    out["band"] = np.where((kk <= q) & (kk >= q - 64), 0.0, -1e30).astype(f)
    out["open"] = np.zeros((P, 2, L), f)

    def rope8(inv):
        ang = j[None, :] * inv[:, None]
        t = np.zeros((P, 2, L))
        for c in range(P):
            m = (c % 8) // 2
            t[c, 0] = np.cos(ang[m])
            t[c, 1] = np.sin(ang[m]) * (1 if c % 2 else -1)
        return t.astype(f)

    theta = (f(10000.0) ** (np.arange(0, 8, 2, dtype=f) / f(8))).astype(f)
    out["rope8"] = rope8(1.0 / theta.astype(np.float64))
    half = np.arange(0, 64, 2, dtype=f)
    inv = (1.0 / 10000.0 ** (half / f(64))).astype(f).astype(np.float64)
    base = ((half + 0.4 * 64) / (1.4 * 64)).astype(np.float64)
    power = (j - L // 2) / 32.0
    t = np.zeros((P, 2, 2, L))
    for c in range(P):
        m = (c % 64) % 32
        sign = -1 if (c % 64) < 32 else 1
        sc = base[m] ** power
        t[c, 0, 0], t[c, 0, 1] = np.cos(j * inv[m]) * sc, np.cos(j * inv[m]) / sc
        t[c, 1, 0], t[c, 1, 1] = sign * np.sin(j * inv[m]) * sc, sign * np.sin(j * inv[m]) / sc
    out["xpos"] = t.astype(f)
    out["block64"] = np.kron(np.eye(2), np.ones((64, 64))).astype(f)
    out["tri"] = (np.arange(P)[:, None] < np.arange(P)[None, :]).astype(f)
    out["ones"] = np.ones((P, P), f)
    out["slot"] = np.tile(np.arange(64, dtype=f), (P, 1))
    out["token"] = (np.arange(P, dtype=f)[:, None] + P * np.arange(NT, dtype=f)[None, :]).astype(f)
    out["lane"] = np.tile(np.arange(P, dtype=f), (P, 1))
    lat = np.arange(64)
    m = np.where(lat[None, :] <= lat[:, None], 0.0, -1e30)
    out["latent_mask"] = np.concatenate([m, m], 0).astype(f)
    own = np.zeros((P, 8, P), f)
    for pair in range(8):
        for s in range(2):
            own[64 * s:64 * s + 64, pair, (2 * pair + s) * 8:(2 * pair + s) * 8 + 8] = 1
    out["own_head"] = own
    return out


def load(eng, dst, src, sem):
    return eng.dma_start(dst, src, allow_slow_non_contiguous=True).then_inc(sem, 16)


def enter_stream(nc, x, X, ident):
    U = 4
    with Phase(nc, "enter") as ph:
        raw = ph.sb("raw", [P, NT, D])
        turned = ph.ps("turned", [P, U, 512])
        loaded, turned_up, stored = ph.sem("loaded"), ph.sem("turned_up"), ph.sem("stored")
        tile = ph.sb("tile", [P, U, D])
        staged = ph.sem("staged")
        with nc.Block() as block:
            @block.sync
            def _(sp):
                load(sp, raw[:, :, :], x.rearrange("b (u p) c -> p (b u) c", p=P), loaded)

            @block.gpsimd
            def _(pool):
                pool.wait_ge(loaded, 16)
                with pool.Fori(0, NT // U) as g:
                    pool.wait_ge(stored, g + 1)
                    pool.tensor_copy(tile[:, :, :], raw[:, ds(g * U, U), :]).then_inc(staged, 1)

            @block.tensor
            def _(pe):
                with pe.Fori(0, NT // U) as g:
                    pe.wait_ge(staged, g + 1)
                    for s in range(U):
                        pe.transpose(turned[:, s, 0:P], tile[:, s, :], ident[:, :]).then_inc(turned_up, 1)

            @block.vector
            def _(dve):
                dve.sem_inc(stored, 1)
                with dve.Fori(0, NT // U) as g:
                    dve.wait_ge(turned_up, (g + 1) * U)
                    dve.tensor_copy(X[:, ds(g * U * P, U * P)].rearrange("p (s c) -> p s c", s=U),
                                    turned[:, :, 0:P]).then_inc(stored, 1)


def leave_stream(nc, X, out, ident):
    U = 4
    with Phase(nc, "leave") as ph:
        rows = ph.sb("rows", [P, NT, D])
        tile = ph.sb("tile", [P, U, D])
        turned = ph.ps("turned", [P, U, 512])
        staged, turned_up, stored, written = (ph.sem(n) for n in ("staged", "turned_up", "stored", "written"))
        with nc.Block() as block:
            @block.gpsimd
            def _(pool):
                with pool.Fori(0, NT // U) as g:
                    pool.wait_ge(stored, g + 1)
                    pool.tensor_copy(tile[:, :, :],
                                     X[:, ds(g * U * P, U * P)].rearrange("p (s c) -> p s c", s=U)).then_inc(staged, 1)

            @block.tensor
            def _(pe):
                with pe.Fori(0, NT // U) as g:
                    pe.wait_ge(staged, g + 1)
                    for s in range(U):
                        pe.transpose(turned[:, s, 0:P], tile[:, s, :], ident[:, :]).then_inc(turned_up, 1)

            @block.vector
            def _(dve):
                dve.sem_inc(stored, 1)
                with dve.Fori(0, NT // U) as g:
                    dve.wait_ge(turned_up, (g + 1) * U)
                    dve.tensor_copy(rows[:, ds(g * U, U), :], turned[:, :, 0:P]).then_inc(stored, 1)

            @block.sync
            def _(sp):
                sp.wait_ge(stored, NT // U + 1)
                sp.dma_start(out.rearrange("b (u p) c -> p (b u) c", p=P), rows[:, :, :]).then_inc(written, 16)
                sp.wait_ge(written, 16)


def layer_norm(nc, tag, X, XN, ones_mean, eps):
    U = 4
    with Phase(nc, tag) as ph:
        mean, var = ph.ps("mean", [P, U, BLK]), ph.ps("var", [P, U, BLK])
        dev, sq, log, inv = (ph.sb(n, [P, U, BLK]) for n in ("dev", "sq", "log", "inv"))
        means, devs, squares, vars_, logs, invs, trip_done = (
            ph.sem(n) for n in ("means", "devs", "squares", "vars", "logs", "invs", "trip_done"))
        with nc.Block() as block:
            @block.tensor
            def _(pe):
                with pe.Fori(0, NBLK // U) as g:
                    pe.wait_ge(trip_done, g + 1)
                    for s in range(U):
                        pe.matmul(mean[:, s, :], ones_mean[:, :], X[:, ds((g * U + s) * BLK, BLK)],
                                  start=True, stop=True).then_inc(means, 1)
                    for s in range(U):
                        pe.wait_ge(squares, g * U + s + 1)
                        pe.matmul(var[:, s, :], ones_mean[:, :], sq[:, s, :], start=True, stop=True).then_inc(vars_, 1)

            @block.vector
            def _(dve):
                dve.sem_inc(trip_done, 1)
                with dve.Fori(0, NBLK // U) as g:
                    for s in range(U):
                        dve.wait_ge(means, g * U + s + 1)
                        dve.wait_ge(trip_done, g + 1)
                        dve.tensor_tensor(dev[:, s, :], X[:, ds((g * U + s) * BLK, BLK)], mean[:, s, :],
                                          ALU.subtract).then_inc(devs, 1)
                    for s in range(U):
                        dve.wait_ge(invs, g * U + s + 1)
                        o = dve.tensor_tensor(XN[:, ds((g * U + s) * BLK, BLK)], dev[:, s, :], inv[:, s, :], ALU.mult)
                    o.then_inc(trip_done, 1)

            @block.gpsimd
            def _(pool):
                with pool.Fori(0, NBLK // U) as g:
                    for s in range(U):
                        pool.wait_ge(devs, g * U + s + 1)
                        pool.tensor_tensor(sq[:, s, :], dev[:, s, :], dev[:, s, :], ALU.mult).then_inc(squares, 1)

            @block.scalar
            def _(act):
                with act.Fori(0, NBLK // U) as g:
                    for s in range(U):
                        act.wait_ge(vars_, g * U + s + 1)
                        act.activation(log[:, s, :], var[:, s, :], ACT.Ln, bias=eps[:, 0:1]).then_inc(logs, 1)
                    for s in range(U):
                        act.wait_ge(logs, g * U + s + 1)
                        act.activation(inv[:, s, :], log[:, s, :], ACT.Exp, scale=-0.5).then_inc(invs, 1)
def full_attention(nc, tag, R, XN, A, W, ident):
    scale = D ** -0.5
    with Phase(nc, tag) as ph:
        xs = ph.sb("xs", [P, L])
        qT, kT = ph.sb("qT", [P, L]), ph.sb("kT", [P, L])
        V = ph.sb("V", [P, 2, D])
        S, E = ph.sb("S", [P, 2, L]), ph.sb("E", [P, 2, L])
        ET = ph.sb("ET", [P, 2, 2, P])
        least, total, share = (ph.sb(n, [P, 2]) for n in ("least", "total", "share"))
        zeros = ph.sb("zeros", [P, L])
        wq, wk, wv = (ph.sb(n, [P, D]) for n in ("wq", "wk", "wv"))
        bias = ph.sb("bias", [P, 3])
        PJ, VP = ph.ps("PJ", [P, 512]), ph.ps("VP", [P, 512])
        SC, TU = ph.ps("SC", [P, 2, 512]), ph.ps("TU", [P, 2, 512])
        OT = ph.ps("OT", [P, 2, 512])
        names = ("loaded cleared staged projected v_made v_copied qk_ready scored shifted exped summed shared turned "
                 "turned_copied valued trip_done passed").split()
        sm = {n: ph.sem(n) for n in names}
        with nc.Block() as block:
            @block.sync
            def _(sp):
                load(sp, wq[:, :], W["q"], sm["loaded"])
                load(sp, wk[:, :], W["k"], sm["loaded"])
                load(sp, wv[:, :], W["v"], sm["loaded"])
                load(sp, bias[:, :], W["bias"], sm["loaded"])

            @block.gpsimd
            def _(pool):
                pool.memset(zeros[:, :], 0.0).then_inc(sm["cleared"], 1)

            @block.tensor
            def _(pe):
                pe.wait_ge(sm["loaded"], 64)
                with pe.Fori(0, NB) as b:
                    pe.wait_ge(sm["trip_done"], b + 1)
                    pe.wait_ge(sm["staged"], b + 1)
                    pe.matmul(PJ[:, 0:L], wq[:, :], xs[:, :], start=True, stop=True)
                    pe.matmul(PJ[:, L:2 * L], wk[:, :], xs[:, :], start=True, stop=True).then_inc(sm["projected"], 1)
                    for t in range(2):
                        o = pe.matmul(VP[:, t * P:(t + 1) * P], xs[:, t * P:(t + 1) * P], wv[:, :], start=True, stop=True)
                    o.then_inc(sm["v_made"], 1)
                    pe.wait_ge(sm["qk_ready"], b + 1)
                    for t in range(2):
                        pe.matmul(SC[:, t, 0:L], qT[:, t * P:(t + 1) * P], kT[:, :], start=True, stop=True).then_inc(sm["scored"], 1)
                    for t in range(2):
                        pe.wait_ge(sm["shared"], 2 * b + t + 1)
                        for c in range(2):
                            o = pe.transpose(TU[:, t, c * P:(c + 1) * P], E[:, t, c * P:(c + 1) * P], ident[:, :])
                        o.then_inc(sm["turned"], 1)
                    pe.wait_ge(sm["v_copied"], b + 1)
                    for t in range(2):
                        pe.wait_ge(sm["turned_copied"], 2 * b + t + 1)
                        for c in range(2):
                            o = pe.matmul(OT[:, t, 0:P], V[:, c, :], ET[:, t, c, :], start=c == 0, stop=c == 1)
                        o.then_inc(sm["valued"], 1)

            @block.scalar
            def _(act):
                act.wait_ge(sm["loaded"], 64)
                with act.Fori(0, NB) as b:
                    act.wait_ge(sm["trip_done"], b + 1)
                    act.wait_ge(sm["projected"], b + 1)
                    act.activation(qT[:, :], PJ[:, 0:L], ACT.Identity, bias=bias[:, 0:1])
                    act.activation(kT[:, :], PJ[:, L:2 * L], ACT.Identity, bias=bias[:, 1:2]).then_inc(sm["qk_ready"], 1)
                    act.wait_ge(sm["v_made"], b + 1)
                    act.activation(V[:, :, :], VP[:, 0:L].rearrange("p (t c) -> p t c", t=2), ACT.Copy).then_inc(sm["v_copied"], 1)
                    for t in range(2):
                        act.wait_ge(sm["shifted"], 2 * b + t + 1)
                        act.activation(E[:, t, :], S[:, t, :], ACT.Exp, bias=least[:, t:t + 1], scale=-1.0,
                                       accum_out=total[:, t:t + 1]).then_inc(sm["exped"], 1)
                    for t in range(2):
                        act.wait_ge(sm["turned"], 2 * b + t + 1)
                        act.activation(ET[:, t, :, :], TU[:, t, 0:L].rearrange("p (c q) -> p c q", c=2),
                                       ACT.Copy).then_inc(sm["turned_copied"], 1)

            @block.vector
            def _(dve):
                dve.sem_inc(sm["trip_done"], 1)
                dve.wait_ge(sm["loaded"], 64)
                dve.wait_ge(sm["cleared"], 1)
                with dve.Fori(0, NB) as b:
                    seq = ds(b * L, L)
                    dve.wait_ge(sm["trip_done"], b + 1)
                    dve.tensor_copy(xs[:, :], XN[:, seq]).then_inc(sm["staged"], 1)
                    for t in range(2):
                        dve.wait_ge(sm["scored"], 2 * b + t + 1)
                        dve.sem_inc(sm["passed"], 1)
                        dve.tensor_tensor_reduce(S[:, t, :], SC[:, t, 0:L], zeros[:, :], -scale, 3e38, ALU.add, ALU.min,
                                                 least[:, t:t + 1]).then_inc(sm["shifted"], 1)
                    for t in range(2):
                        dve.wait_ge(sm["exped"], 2 * b + t + 1)
                        dve.reciprocal(share[:, t:t + 1], total[:, t:t + 1]).then_inc(sm["summed"], 1)
                        dve.wait_ge(sm["summed"], 2 * b + t + 1)
                        dve.tensor_scalar(E[:, t, :], E[:, t, :], share[:, t:t + 1], None, ALU.mult).then_inc(sm["shared"], 1)
                    dve.wait_ge(sm["valued"], 2 * b + 2)
                    at = R[:, seq].rearrange("p (t q) -> p t q", t=2)
                    dve.scalar_tensor_tensor(at, OT[:, :, 0:P], bias[:, 2:3], at, ALU.add, ALU.add).then_inc(sm["trip_done"], 1)


HEADS = {"rel": 16, "rope": 16, "win": 8}
WIDTH = {"rel": 8, "rope": 8, "win": 64}
STRIP = {"rel": 32, "rope": 32, "win": 64}
SCALE = {"rel": 8 ** -0.5, "rope": 8 ** -0.5, "win": 8.0}
TURN_BANKS = {"rel": 1, "rope": 2, "win": 1}
SHIFT_LAG = {"rel": 1, "rope": 0, "win": 0}
EXP_LAG = {"rel": 2, "rope": 0, "win": 0}
SHARE_LAG = {"rel": 4, "rope": 2, "win": 3}
TURN_LAG = {"rel": 6, "rope": 4, "win": 5}
VALUE_LAG = {"rel": 8, "rope": 6, "win": 7}
START = 14


def head_attention(nc, tag, kind, R, XN, A, W, ident):
    nh, width, strip, scale = HEADS[kind], WIDTH[kind], STRIP[kind], SCALE[kind]
    G = nh * strip // P
    VW = nh * width
    NU = 2 * nh
    small = strip == 32
    keys = (lambda t: L) if kind == "rel" else (lambda t: P * (t + 1))
    NSC, NTU = 2, TURN_BANKS[kind]
    RS, RE, RT = 4, 8, 4
    turn_lag, value_lag, exp_lag, shift_lag = TURN_LAG[kind], VALUE_LAG[kind], EXP_LAG[kind], SHIFT_LAG[kind]
    share_lag = SHARE_LAG[kind]
    with Phase(nc, tag) as ph:
        xs = ph.sb("xs", [P, L])
        QK = ph.sb("QK", [P, 2, G, 2, L])
        V = ph.sb("V", [P, 2, 2, VW])
        S, E = ph.sb("S", [P, RS, L]), ph.sb("E", [P, RE, L])
        ET = ph.sb("ET", [P, RT, 2, P])
        least, total, share = (ph.sb(n, [P, 2 * NU]) for n in ("least", "total", "share"))
        oT = ph.sb("oT", [P, G, L])
        PJ = ph.ps("PJ", [P, 2, 512])
        SC = ph.ps("SC", [P, NSC, 512])
        TU = ph.ps("TU", [P, NTU, 512])
        OT = ph.ps("OT", [P, 2, 512])
        wq, wk, wv = (ph.sb(n, [P, VW]) for n in ("wq", "wk", "wv"))
        wo = ph.sb("wo", [P, G, D])
        if kind in ("rope", "win"):
            mask = ph.sb("mask", [P, 2, L])
            wqx, wkx = ph.sb("wqx", [P, VW]), ph.sb("wkx", [P, VW])
        if small:
            spread = ph.sb("spread", [P, G, 4, 32])
            qk = ph.sb("qk", [P, 2, L])
        if kind == "rope":
            rt = ph.sb("rt", [P, 2, L])
            parts = ph.sb("parts", [P, 2, 2, L])
        if kind == "rel":
            qv = ph.sb("qv", [P, 2, L])
            AP_ = ph.ps("AP", [P, 512])
            ub, vb = ph.sb("ub", [P, 1]), ph.sb("vb", [P, 1])
            wr = ph.sb("wr", [P, nh, 2, P])
            turn = ph.sb("turn", [P, 2, L])
            low, up = ph.sb("low", [P, L]), ph.sb("up", [P, L])
            rmask = ph.sb("rmask", [P, 2, 2, P])
            tparts = ph.sb("tparts", [P, 2, 2, L])
            Ah = ph.sb("Ah", [P, 2, L + 1])
            lu = ph.sb("lu", [P, 2, 2 * P + 4])
            bd = ph.sb("bd", [P, 2, L])
        if kind == "win":
            tab = ph.sb("tab", [P, 2, 2, L])
            qs = ph.sb("qs", [P, 2, 2])
            b64 = ph.sb("b64", [P, P])
            NORM = ph.ps("NORM", [P, 512])
            sq, m1, m2 = (ph.sb(n, [P, 2 * L]) for n in ("sq", "m1", "m2"))
            clipped, log, inv, m3 = (ph.sb(n, [P, G, 2 * L]) for n in ("clipped", "log", "inv", "m3"))
            back = ph.sb("back", [P, 1])

        names = ("loaded cleared prepared staged projected v_made v_copied spread_made strips_copied scored "
                 "shifted exped turned turned_copied valued summed shared o_copied final added o_zeroed "
                 "qk_ready parts_made a_made a_parts a_ready masked bd_ready squares norms logs clips invs "
                 "m1_made m3_made passed back_set").split()
        sm = {n: ph.sem(n) for n in names}
        n_loads = [0]

        def ld(eng, dst, src):
            n_loads[0] += 1
            load(eng, dst, src, sm["loaded"])

        def steps(eng, prepare, body):
            for s in range(NU):
                prepare(0, 0, s)
            for j in range(START):
                body(0, j)
            with eng.Fori(0, NB // 2) as g:
                for j in range(START, 2 * NU + START):
                    body(g, j)

        def ahead(g, j):
            return 2 * g + j // NU + 1, (j // NU + 1) % 2, j % NU

        def behind(g, j):
            return 2 * g + j // NU - 1, (j // NU - 1) % 2, j % NU

        def units(g, j):
            return 2 * NU * g + j

        first_spread = 16

        with nc.Block() as block:
            @block.sync
            def _(sp):
                ld(sp, wq[:, :], W["q"])
                ld(sp, wk[:, :], W["k"])
                ld(sp, wv[:, :], W["v"])
                if kind == "rel":
                    ld(sp, ub[:, :], W["u"])
                    ld(sp, vb[:, :], W["v_bias"])
                    ld(sp, turn[:, :, :], A["rel_turn"])
                    ld(sp, low[:, :], A["rel_low"])
                    ld(sp, up[:, :], A["rel_up"])
                    ld(sp, rmask[:, :, :, :], A["rel_mask"])
                    sp.wait_ge(sm["cleared"], 1)
                    for h in range(nh):
                        ld(sp, wr[8 * h:8 * h + 8, h, 0, :], W["r"][8 * h:8 * h + 8, :])
                        ld(sp, wr[8 * h:8 * h + 8, h, 1, :], W["r_crossed"][8 * h:8 * h + 8, :])
                else:
                    ld(sp, wqx[:, :], W["q_crossed"])
                    ld(sp, wkx[:, :], W["k_crossed"])
                    ld(sp, mask[:, :, :], A[{"rope": "causal", "win": "band"}[kind]])
                if kind == "rope":
                    ld(sp, rt[:, :, :], A["rope8"])
                if small:
                    sp.wait_ge(sm["cleared"], 2 if kind == "rel" else 1)
                    for r in range(4):
                        for gr in range(G):
                            ld(sp, wo[32 * r:32 * r + 8, gr, :], W["o"][(4 * gr + r) * 8:(4 * gr + r) * 8 + 8, :])
                if kind == "win":
                    ld(sp, wo[:, :, :], W["o"])
                    ld(sp, qs[:, :, :], W["qk_scale"])
                    ld(sp, tab[:, :, :, :], A["xpos"])
                    ld(sp, b64[:, :], A["block64"])

            loads = 16 * n_loads[0]

            @block.gpsimd
            def _(pool):
                if kind == "rel":
                    pool.memset(wr[:, :, :, :], 0.0).then_inc(sm["cleared"], 1)
                    pool.memset(lu[:, :, :], 0.0).then_inc(sm["prepared"], 1)
                    pool.memset(bd[:, :, :], 0.0).then_inc(sm["prepared"], 1)
                    pool.memset(Ah[:, :, :], 0.0).then_inc(sm["prepared"], 1)
                if small:
                    pool.memset(wo[:, :, :], 0.0).then_inc(sm["cleared"], 1)
                    pool.memset(spread[:, :, :, :], 0.0).then_inc(sm["prepared"], 1)
                    pool.wait_ge(sm["prepared"], 4 if kind == "rel" else 1)
                    pool.tensor_copy(spread[:, :, :, 0:8],
                                     ident[:, :].rearrange("p (g s d) -> p g s d", g=4, s=4)).then_inc(sm["prepared"], 1)
                else:
                    pool.memset(xs[:, :], 0.0).then_inc(sm["cleared"], 1)
                    pool.memset(back[:, :], 10.0 * float(np.log(2.0))).then_inc(sm["back_set"], 1)
                    pool.wait_ge(sm["loaded"], loads)
                    pool.wait_ge(sm["cleared"], 1)
                    for d in range(2):
                        for w in range(2):
                            pool.tensor_scalar(tab[:, d, w, :], tab[:, d, w, :], qs[:, d, w:w + 1], None,
                                               ALU.mult).then_inc(sm["prepared"], 1)
                    pool.wait_ge(sm["prepared"], 4)

                def stage(q):
                    if not isinstance(q, int) or q > 0:
                        pool.wait_ge(sm["v_made"], q)
                        pool.sem_inc(sm["passed"], 1)
                    pool.tensor_copy(xs[:, :], XN[:, ds(q * L, L)]).then_inc(sm["staged"], 1)

                def sum_a(H, n):
                    pool.wait_ge(sm["a_parts"], n + H + 1)
                    if H >= 2:
                        pool.wait_ge(sm["scored"], 2 * (n + H - 1))
                    pool.tensor_tensor(Ah[:, H % 2, 0:L], tparts[:, H % 2, 0, :], tparts[:, H % 2, 1, :],
                                       ALU.add).then_inc(sm["a_ready"], 1)

                def prepare(q, parity, s):
                    if small and s == 11:
                        stage(q)
                    if kind == "rope" and s == 13:
                        pool.wait_ge(sm["parts_made"], 2 * q + 2)
                        pool.tensor_tensor(qk[:, :, :], parts[:, 0, :, :], parts[:, 1, :, :], ALU.add).then_inc(sm["qk_ready"], 1)

                def rel_step(g, j):
                    if j % 2 == 0:
                        sum_a(j // 2 + 1, 2 * nh * g)
                    n, t = units(g, j), j % 2
                    pool.wait_ge(sm["masked"], n + 1)
                    if j >= 2:
                        pool.wait_ge(sm["shifted"], n - 1)
                    if t == 0:
                        pool.tensor_tensor(bd[:, 0, 0:P + 1], lu[:, 0, 0:P + 1], lu[:, 0, P + 1:2 * P + 2],
                                           ALU.add).then_inc(sm["bd_ready"], 1)
                    else:
                        pool.tensor_tensor(bd[:, 1, P:L], lu[:, 1, 0:P], lu[:, 1, P + 2:2 * P + 2],
                                           ALU.add).then_inc(sm["bd_ready"], 1)

                def win_sequence(q, parity):
                    for c in range(G):
                        pool.wait_ge(sm["m1_made"], G * q + c + 1)
                        pool.tensor_tensor(m3[:, c, :], m1[:, :], m2[:, :], ALU.add).then_inc(sm["m3_made"], 1)
                    for c in range(G):
                        pool.wait_ge(sm["m3_made"], G * q + c + 1)
                        pool.wait_ge(sm["invs"], G * q + c + 1)
                        pool.tensor_tensor(QK[:, parity, c, :, :].rearrange("p w n -> p (w n)"), m3[:, c, :], inv[:, c, :],
                                           ALU.mult).then_inc(sm["strips_copied"], 1)

                def body(g, j):
                    if kind == "rel":
                        rel_step(g, j)
                    prepare(*ahead(g, j))

                if kind == "win":
                    win_sequence(0, 0)
                    win_sequence(1, 1)
                    with pool.Fori(0, NB // 2) as g:
                        win_sequence(2 * g + 2, 0)
                        win_sequence(2 * g + 3, 1)
                else:
                    for s in range(NU):
                        prepare(0, 0, s)
                    if kind == "rel":
                        sum_a(0, 0)
                    for j in range(START):
                        body(0, j)
                    with pool.Fori(0, NB // 2) as g:
                        for j in range(START, 2 * NU + START):
                            body(g, j)

            @block.tensor
            def _(pe):
                pe.wait_ge(sm["loaded"], loads)
                if small:
                    pe.wait_ge(sm["prepared"], 5 if kind == "rel" else 2)
                    pe.wait_ge(sm["o_zeroed"], 1)

                def prepare(q, parity, s):
                    later = not isinstance(q, int) or q > 0
                    if small:
                        if s == 12:
                            pe.wait_ge(sm["staged"], q + 1)
                            if later:
                                pe.wait_ge(sm["added"], q)
                                pe.wait_ge(sm["strips_copied"], G * q)
                            pe.matmul(PJ[:, 0, 0:L], wq[:, :], xs[:, :], start=True, stop=True)
                            last = pe.matmul(PJ[:, 0, L:2 * L], wk[:, :], xs[:, :], start=True, stop=True)
                            if kind == "rope":
                                pe.matmul(PJ[:, 1, 0:L], wqx[:, :], xs[:, :], start=True, stop=True)
                                last = pe.matmul(PJ[:, 1, L:2 * L], wkx[:, :], xs[:, :], start=True, stop=True)
                            last.then_inc(sm["projected"], 1)
                        if s == 14:
                            pe.wait_ge(sm["qk_ready"], q + 1)
                            for t in range(2):
                                last = pe.matmul(PJ[:, 0, t * P:(t + 1) * P], xs[:, t * P:(t + 1) * P], wv[:, :],
                                                 start=True, stop=True)
                            last.then_inc(sm["v_made"], 1)
                        gr = (s - first_spread) // 2
                        if s % 2 == 0 and 0 <= gr < G:
                            if gr == 0:
                                pe.wait_ge(sm["v_copied"], q + 1)
                            else:
                                pe.wait_ge(sm["strips_copied"], G * q + gr)
                            pe.matmul(PJ[:, gr % 2, :], spread[:, gr, :, :], qk[:, :, :], start=True,
                                      stop=True).then_inc(sm["spread_made"], 1)
                        return
                    c, cols = s // 2, slice(s // 2 * P, (s // 2 + 1) * P)
                    if s % 2 == 0 and c < G:
                        if c == 0:
                            pe.wait_ge(sm["staged"], q + 1)
                            if later:
                                pe.wait_ge(sm["v_copied"], q)
                            if not isinstance(q, int):
                                pe.wait_ge(sm["added"], q - 1)
                        else:
                            pe.wait_ge(sm["m1_made"], G * q + c)
                        pe.matmul(PJ[:, 0, 0:L], wq[:, cols], xs[:, :], start=True, stop=True)
                        pe.matmul(PJ[:, 0, L:2 * L], wk[:, cols], xs[:, :], start=True, stop=True)
                        pe.matmul(PJ[:, 1, 0:L], wqx[:, cols], xs[:, :], start=True, stop=True)
                        pe.matmul(PJ[:, 1, L:2 * L], wkx[:, cols], xs[:, :], start=True,
                                  stop=True).then_inc(sm["projected"], 1)
                    if s % 2 == 1 and c < G:
                        pe.wait_ge(sm["squares"], G * q + c + 1)
                        if later or c > 0:
                            pe.wait_ge(sm["clips"], G * q + c)
                        pe.matmul(NORM[:, :], b64[:, :], sq[:, :], start=True, stop=True).then_inc(sm["norms"], 1)
                    if s == 8:
                        pe.wait_ge(sm["m1_made"], G * q + G)
                        for t in range(2):
                            last = pe.matmul(PJ[:, t, 0:VW], xs[:, t * P:(t + 1) * P], wv[:, :], start=True, stop=True)
                        last.then_inc(sm["v_made"], 1)

                def epilogue(e, parity, s):
                    if s == 9:
                        pe.wait_ge(sm["o_copied"], 2 * e + 2)
                        if kind == "win":
                            pe.wait_ge(sm["v_copied"], e + 3)
                        for gr in range(G):
                            last = pe.matmul(PJ[:, 0, 0:L], wo[:, gr, :], oT[:, gr, :], start=gr == 0, stop=gr == G - 1)
                        last.then_inc(sm["final"], 1)

                def make_a(H, n):
                    if H >= 1:
                        pe.wait_ge(sm["a_parts"], n + H)
                    for x in range(2):
                        last = pe.matmul(AP_[:, x * L:(x + 1) * L], wr[:, H % nh, x, :], qv[:, H // nh % 2, :],
                                         start=True, stop=True)
                    last.then_inc(sm["a_made"], 1)

                def score(g, j):
                    u, parity, n = j % NU, j // NU % 2, units(g, j)
                    h, t = u // 2, u % 2
                    gr, row = h * strip // P, h * strip % P
                    rows = slice(row, row + strip)
                    if u == 0:
                        pe.wait_ge(sm["v_copied"], 2 * g + j // NU + 1)
                    if t == 0 and row == 0:
                        pe.wait_ge(sm["strips_copied"], G * (2 * g + j // NU) + gr + 1)
                    if j >= NSC:
                        pe.wait_ge(sm["shifted"], n - NSC + 1)
                    nk = keys(t)
                    sc = SC[:, j % NSC, :]
                    last = pe.matmul(sc[:, 0:nk], QK[rows, parity, gr, 0, t * P:(t + 1) * P], QK[rows, parity, gr, 1, 0:nk],
                                     start=True, stop=kind != "rel", skip_group_check=kind == "rel")
                    if kind == "rel":
                        pe.wait_ge(sm["a_ready"], 2 * nh * g + j // 2 + 1)
                        a0 = Ah[:, h % 2, t * P:(t + 1) * P]
                        a1 = Ah[:, h % 2, t * P + 1:(t + 1) * P + 1]
                        if t == 0:
                            pe.matmul(sc[:, P + 1:L], a1, up[:, P + 1:L], start=False, stop=True, skip_group_check=True)
                            pe.matmul(sc[:, L:L + P], a0, low[:, 0:P], start=False, stop=True, skip_group_check=True)
                            last = pe.matmul(sc[:, L + P:2 * L], a1, up[:, 1:P + 1], start=False, stop=True,
                                             skip_group_check=True)
                        else:
                            pe.matmul(sc[:, 0:P], a0, low[:, 0:P], start=False, stop=True, skip_group_check=True)
                            pe.matmul(sc[:, L:L + P], a0, low[:, P:L], start=False, stop=True, skip_group_check=True)
                            last = pe.matmul(sc[:, L + P:2 * L], a1, up[:, P:L], start=False, stop=True,
                                             skip_group_check=True)
                    last.then_inc(sm["scored"], 1)

                def turn_up(g, j):
                    n = units(g, j)
                    pe.wait_ge(sm["shared"], n + 1)
                    if j >= NTU:
                        pe.wait_ge(sm["turned_copied"], n - NTU + 1)
                    for c in range(keys(j % 2) // P):
                        last = pe.transpose(TU[:, j % NTU, c * P:(c + 1) * P], E[:, j % RE, c * P:(c + 1) * P], ident[:, :])
                    last.then_inc(sm["turned"], 1)

                def value(g, j):
                    u, seq = j % NU, j // NU
                    h, t = u // 2, u % 2
                    gr, row = h * strip // P, h * strip % P
                    if j >= NU and u % (NU // 2) == 0:
                        pe.wait_ge(sm["o_copied"], 2 * (2 * g + seq - 1) + u // (NU // 2) + 1)
                    pe.wait_ge(sm["turned_copied"], units(g, j) + 1)
                    nk = keys(t) // P
                    at = gr % 2 * L + t * P
                    for c in range(nk):
                        last = pe.matmul(OT[row:row + width, gr // 2, at:at + P],
                                         V[:, seq % 2, c, h * width:(h + 1) * width], ET[:, j % RT, c, :],
                                         start=c == 0, stop=c == nk - 1)
                    last.then_inc(sm["valued"], 1)

                def body(g, j):
                    if kind == "rel" and j % 2 == 0:
                        make_a(j // 2 + 1, 2 * nh * g)
                    score(g, j)
                    if j >= turn_lag:
                        turn_up(g, j - turn_lag)
                    if j >= value_lag:
                        value(g, j - value_lag)
                    prepare(*ahead(g, j))
                    if j >= NU:
                        epilogue(*behind(g, j))

                for s in range(NU):
                    prepare(0, 0, s)
                if kind == "rel":
                    make_a(0, 0)
                for j in range(START):
                    body(0, j)
                with pe.Fori(0, NB // 2) as g:
                    for j in range(START, 2 * NU + START):
                        body(g, j)

            @block.scalar
            def _(act):
                act.wait_ge(sm["loaded"], loads)
                if kind == "win":
                    act.wait_ge(sm["back_set"], 1)

                def prepare(q, parity, s):
                    if small:
                        if s == 15:
                            act.wait_ge(sm["v_made"], q + 1)
                            act.activation(V[:, parity, :, :], PJ[:, 0, 0:L].rearrange("p (t c) -> p t c", t=2),
                                           ACT.Copy).then_inc(sm["v_copied"], 1)
                        gr = (s - first_spread - 1) // 2
                        if s % 2 == 1 and 0 <= gr < G:
                            act.wait_ge(sm["spread_made"], G * q + gr + 1)
                            act.activation(QK[:, parity, gr, :, :], PJ[:, gr % 2, :].rearrange("p (w n) -> p w n", w=2),
                                           ACT.Copy).then_inc(sm["strips_copied"], 1)
                        return
                    c = s // 2
                    if s % 2 == 1 and c < G:
                        act.wait_ge(sm["projected"], G * q + c + 1)
                        act.activation(sq[:, :], PJ[:, 0, :], ACT.Square).then_inc(sm["squares"], 1)
                    if s == 9:
                        if not isinstance(q, int) or q > 0:
                            act.wait_ge(sm["strips_copied"], G * q)
                        act.wait_ge(sm["clips"], G * q + G)
                        act.activation(log[:, :, :], clipped[:, :, :], ACT.Ln, scale=2.0 ** 20).then_inc(sm["logs"], 1)
                    if 10 <= s < 10 + G:
                        c = s - 10
                        act.wait_ge(sm["logs"], q + 1)
                        act.activation(inv[:, c, :], log[:, c, :], ACT.Exp, scale=-0.5, bias=back[:, 0:1]).then_inc(sm["invs"], 1)

                def copy_output(e, i):
                    act.wait_ge(sm["valued"], NU * e + (i + 1) * (NU // 2))
                    act.activation(oT[:, i * (G // 2):(i + 1) * (G // 2), :], OT[:, i, :].rearrange("p (g q) -> p g q", g=2),
                                   ACT.Copy).then_inc(sm["o_copied"], 1)

                def raise_up(g, j):
                    n, u, nk = units(g, j), j % NU, keys(j % 2)
                    act.wait_ge(sm["shifted"], n + 1)
                    if j >= RE:
                        act.wait_ge(sm["turned"], n - RE + 1)
                    at = j % (2 * NU)
                    act.activation(E[:, j % RE, 0:nk], S[:, j % RS, 0:nk], ACT.Exp, bias=least[:, at:at + 1],
                                   scale=-1.0, accum_out=total[:, at:at + 1]).then_inc(sm["exped"], 1)

                def copy_turned(g, j):
                    n, nk = units(g, j), keys(j % 2)
                    act.wait_ge(sm["turned"], n + 1)
                    if j >= RT:
                        act.wait_ge(sm["valued"], n - RT + 1)
                    act.activation(ET[:, j % RT, 0:nk // P, :], TU[:, j % NTU, 0:nk].rearrange("p (c q) -> p c q", q=P),
                                   ACT.Copy).then_inc(sm["turned_copied"], 1)

                def body(g, j):
                    prepare(*ahead(g, j))
                    if j % NU == NU // 2 + value_lag:
                        copy_output(2 * g + j // NU, 0)
                    if j >= NU and j % NU == value_lag:
                        copy_output(2 * g + j // NU - 1, 1)
                    if j >= exp_lag:
                        raise_up(g, j - exp_lag)
                    if j >= turn_lag and kind != "win":
                        copy_turned(g, j - turn_lag)

                steps(act, prepare, body)

            @block.vector
            def _(dve):
                dve.sem_inc(sm["added"], 1)
                if small:
                    dve.memset(OT[:, :, :], 0.0).then_inc(sm["o_zeroed"], 1)
                dve.wait_ge(sm["loaded"], loads)
                if kind in ("rel", "win"):
                    dve.wait_ge(sm["prepared"], 5 if kind == "rel" else 4)

                def stage(q):
                    dve.tensor_copy(xs[0:64, :], XN[0:64, ds(q * L, L)])
                    dve.tensor_copy(xs[64:P, 1:L], XN[64:P, ds(q * L, L - 1)]).then_inc(sm["staged"], 1)

                def prepare(q, parity, s):
                    later = not isinstance(q, int) or q > 0
                    if small and s == 13:
                        dve.wait_ge(sm["projected"], q + 1)
                        if kind == "rel":
                            src = PJ[:, 0, :]
                            if later:
                                dve.wait_ge(sm["spread_made"], G * q)
                            dve.tensor_scalar(qv[:, parity, :], src[:, 0:L], vb[:, 0:1], None, ALU.add)
                            dve.tensor_scalar(qk[:, 0, :], src[:, 0:L], ub[:, 0:1], None, ALU.add)
                            dve.tensor_copy(qk[:, 1, :], src[:, L:2 * L]).then_inc(sm["qk_ready"], 1)
                        else:
                            for x in range(2):
                                tb = rt[:, x, :].rearrange("p (o n) -> p o n", o=1).broadcast_to([P, 2, L])
                                dve.tensor_tensor(parts[:, x, :, :], PJ[:, x, :].rearrange("p (w n) -> p w n", w=2), tb,
                                                  ALU.mult).then_inc(sm["parts_made"], 1)
                    if kind == "win":
                        c = s // 2
                        if s == 14:
                            dve.wait_ge(sm["v_made"], q + 1)
                            stage(q + 1)
                        if s % 2 == 1 and c < G:
                            if later or c > 0:
                                dve.wait_ge(sm["m3_made"], G * q + c)
                            dve.wait_ge(sm["projected"], G * q + c + 1)
                            dve.tensor_tensor(m2[:, :], PJ[:, 1, :], tab[:, 1, :, :].rearrange("p w n -> p (w n)"), ALU.mult)
                            dve.wait_ge(sm["squares"], G * q + c + 1)
                            dve.tensor_tensor(m1[:, :], PJ[:, 0, :], tab[:, 0, :, :].rearrange("p w n -> p (w n)"),
                                              ALU.mult).then_inc(sm["m1_made"], 1)
                        if s % 2 == 0 and 1 <= c <= G:
                            if later:
                                dve.wait_ge(sm["logs"], q)
                            dve.wait_ge(sm["norms"], G * q + c)
                            dve.tensor_scalar(clipped[:, c - 1, :], NORM[:, :], 1e-24, None, ALU.max).then_inc(sm["clips"], 1)
                        if s == 9:
                            dve.wait_ge(sm["v_made"], q + 1)
                            for t in range(2):
                                o = dve.tensor_copy(V[:, parity, t, :], PJ[:, t, 0:VW])
                            o.then_inc(sm["v_copied"], 1)

                def epilogue(e, parity, s):
                    if s == 10:
                        dve.wait_ge(sm["final"], e + 1)
                        dve.tensor_tensor(R[:, ds(e * L, L)], PJ[:, 0, 0:L], R[:, ds(e * L, L)], ALU.add).then_inc(sm["added"], 1)

                def make_parts(H, n):
                    dve.wait_ge(sm["a_made"], n + H + 1)
                    if H >= 2:
                        dve.wait_ge(sm["a_ready"], n + H - 1)
                    dve.tensor_tensor(tparts[:, H % 2, :, :], AP_[:, :].rearrange("p (x n) -> p x n", x=2),
                                      turn[:, :, :], ALU.mult).then_inc(sm["a_parts"], 1)

                def shift(g, j):
                    n, t = units(g, j), j % 2
                    nk = keys(t)
                    if kind == "rel":
                        dve.wait_ge(sm["bd_ready"], n + 1)
                        add = bd[:, t, :]
                    else:
                        dve.wait_ge(sm["scored"], n + 1)
                        add = mask[:, t, 0:nk]
                    if j >= RS:
                        dve.wait_ge(sm["exped"], n - RS + 1)
                    dve.sem_inc(sm["passed"], 1)
                    at = j % (2 * NU)
                    dve.tensor_tensor_reduce(S[:, j % RS, 0:nk], SC[:, j % NSC, 0:nk], add, -scale, 3e38, ALU.add, ALU.min,
                                             least[:, at:at + 1]).then_inc(sm["shifted"], 1)

                def copy_turned(g, j):
                    n, nk = units(g, j), keys(j % 2)
                    dve.wait_ge(sm["turned"], n + 1)
                    if j >= RT:
                        dve.wait_ge(sm["valued"], n - RT + 1)
                    dve.tensor_copy(ET[:, j % RT, 0:nk // P, :],
                                    TU[:, j % NTU, 0:nk].rearrange("p (c q) -> p c q", q=P)).then_inc(sm["turned_copied"], 1)

                def share_out(g, j):
                    n, nk, at = units(g, j), keys(j % 2), j % (2 * NU)
                    dve.wait_ge(sm["exped"], n + 1)
                    dve.reciprocal(share[:, at:at + 1], total[:, at:at + 1]).then_inc(sm["summed"], 1)
                    dve.wait_ge(sm["summed"], n + 1)
                    dve.tensor_scalar(E[:, j % RE, 0:nk], E[:, j % RE, 0:nk], share[:, at:at + 1], None,
                                      ALU.mult).then_inc(sm["shared"], 1)

                def mask_products(g, j):
                    n, t = units(g, j), j % 2
                    dve.wait_ge(sm["scored"], n + 1)
                    if j >= 2:
                        dve.wait_ge(sm["bd_ready"], n - 1)
                    dve.tensor_tensor(lu[:, t, :].rearrange("p (x n) -> p x n", x=2)[:, :, 0:P],
                                      SC[:, j % NSC, L:2 * L].rearrange("p (x n) -> p x n", x=2), rmask[:, t, :, :],
                                      ALU.mult).then_inc(sm["masked"], 1)

                def body(g, j):
                    prepare(*ahead(g, j))
                    if j >= NU:
                        epilogue(*behind(g, j))
                    if j >= shift_lag:
                        shift(g, j - shift_lag)
                    if kind == "rel" and j % 2 == 0:
                        make_parts(j // 2 + 1, 2 * nh * g)
                    if j >= share_lag:
                        share_out(g, j - share_lag)
                    if kind == "win" and j >= turn_lag:
                        copy_turned(g, j - turn_lag)
                    if kind == "rel":
                        mask_products(g, j)

                if kind == "win":
                    dve.wait_ge(sm["cleared"], 1)
                    stage(0)
                for s in range(NU):
                    prepare(0, 0, s)
                if kind == "rel":
                    make_parts(0, 0)
                for j in range(START):
                    body(0, j)
                with dve.Fori(0, NB // 2) as g:
                    for j in range(START, 2 * NU + START):
                        body(g, j)


def gated_ffn(nc, tag, kind, R, XN, A, W, om=None, eps=None):
    gelu = kind == "gelu"
    HID = 341 if gelu else 384
    NC = 3
    width = [min(P, HID - c * P) for c in range(NC)]
    U = 2
    with Phase(nc, tag) as ph:
        wg, wu = ph.sb("wg", [P, HID]), ph.sb("wu", [P, HID])
        wd = ph.sb("wd", [P, NC, D])
        gate_on, hid = ph.sb("gate_on", [P, 2, BLK]), ph.sb("hid", [P, U, NC, BLK])
        G, UP = ph.ps("G", [P, 2, BLK]), ph.ps("UP", [P, 2, BLK])
        OUT = ph.ps("OUT", [P, U, BLK])
        names = ("loaded weights_ready shifted means devs squares vars logs invs scaled normed gate_made up_made gated "
                 "hidden out_made trip_done zeroed").split()
        sm = {n: ph.sem(n) for n in names}
        if gelu:
            ba, bg, b2 = ph.sb("ba", [P, NC]), ph.sb("bg", [P, NC]), ph.sb("b2", [P, 1])
            lg, lb = ph.sb("lg", [P, 1]), ph.sb("lb", [P, 1])
            hs, dev, sq, log, inv, hn, hx = (ph.sb(n, [P, U, BLK]) for n in ("hs", "dev", "sq", "log", "inv", "hn", "hx"))
            STAT = ph.ps("STAT", [P, U, BLK])
            loads = 16 * (2 + (2 + 2 * 2 + 1 + 2) + 2)
        else:
            ig, iu, idn = ph.sb("ig", [P, HID], I32), ph.sb("iu", [P, HID], I32), ph.sb("idn", [P, NC, D], I32)
            loads = 16 * 3
        with nc.Block() as block:
            @block.sync
            def _(sp):
                if gelu:
                    load(sp, wu[:, :], W["w1"][:, 0:HID], sm["loaded"])
                    load(sp, wg[:, :], W["w1"][:, HID:2 * HID], sm["loaded"])
                    load(sp, wd[:, 0:2, :], W["w2"][0:2 * P, :].rearrange("(c p) d -> p c d", p=P), sm["loaded"])
                    load(sp, wd[0:width[2], 2, :], W["w2"][2 * P:HID, :], sm["loaded"])
                    for dst, o in ((ba, 0), (bg, HID)):
                        load(sp, dst[:, 0:2], W["b1"][o:o + 2 * P].rearrange("(c p) -> p c", p=P), sm["loaded"])
                        load(sp, dst[0:width[2], 2:3], W["b1"][o + 2 * P:o + HID].rearrange("(p c) -> p c", c=1), sm["loaded"])
                    for dst, n in ((b2, "b2"), (lg, "ln_g"), (lb, "ln_b")):
                        load(sp, dst[:, :], W[n].rearrange("(p c) -> p c", c=1), sm["loaded"])
                else:
                    load(sp, ig[:, :], W["gate"], sm["loaded"])
                    load(sp, iu[:, :], W["up"], sm["loaded"])
                    load(sp, idn[:, :, :], W["down"].rearrange("(c p) d -> p c d", p=P), sm["loaded"])

            @block.gpsimd
            def _(pool):
                if gelu:
                    pool.memset(hs[64:P, :, :], 0.0).then_inc(sm["zeroed"], 1)
                    with pool.Fori(0, NBLK // U) as g:
                        for s in range(U):
                            pool.wait_ge(sm["invs"], U * g + s + 1)
                            pool.wait_ge(sm["trip_done"], g + 1)
                            pool.tensor_tensor(hn[:, s, :], dev[:, s, :], inv[:, s, :], ALU.mult).then_inc(sm["scaled"], 1)

            @block.tensor
            def _(pe):
                pe.wait_ge(sm["loaded"], 16 * 11 if gelu else loads)
                if not gelu:
                    pe.wait_ge(sm["weights_ready"], 3)
                with pe.Fori(0, NBLK // U) as g:
                    pe.wait_ge(sm["trip_done"], g + 1)
                    if gelu:
                        for s in range(U):
                            pe.wait_ge(sm["shifted"], U * g + s + 1)
                            pe.matmul(STAT[:, s, :], om[:, :], hs[:, s, :], start=True, stop=True).then_inc(sm["means"], 1)
                        for s in range(U):
                            pe.wait_ge(sm["squares"], U * g + s + 1)
                            pe.wait_ge(sm["devs"], U * g + s + 1)
                            pe.matmul(STAT[:, s, :], om[:, :], sq[:, s, :], start=True, stop=True).then_inc(sm["vars"], 1)

                    def down(s):
                        pe.wait_ge(sm["hidden"], NC * (U * g + s) + NC)
                        for c in range(NC):
                            last = pe.matmul(OUT[:, s, :], wd[0:width[c], c, :], hid[0:width[c], s, c, :],
                                             start=c == 0, stop=c == NC - 1)
                        last.then_inc(sm["out_made"], 1)

                    for k in range(U * NC):
                        s, c = k // NC, k % NC
                        x = hx[:, s, :] if gelu else XN[:, ds((U * g + s) * BLK, BLK)]
                        if gelu and c == 0:
                            pe.wait_ge(sm["normed"], U * g + s + 1)
                        if k >= 2:
                            pe.wait_ge(sm["hidden"], NC * U * g + k - 1)
                        cols = slice(c * P, c * P + width[c])
                        pe.matmul(G[0:width[c], k % 2, :], wg[:, cols], x, start=True, stop=True).then_inc(sm["gate_made"], 1)
                        pe.matmul(UP[0:width[c], k % 2, :], wu[:, cols], x, start=True, stop=True).then_inc(sm["up_made"], 1)
                        if k == NC + 1:
                            down(0)
                    down(1)

            @block.scalar
            def _(act):
                act.wait_ge(sm["loaded"], 16 * 11 if gelu else loads)
                with act.Fori(0, NBLK // U) as g:
                    act.wait_ge(sm["trip_done"], g + 1)
                    if gelu:
                        for s in range(U):
                            act.wait_ge(sm["devs"], U * g + s + 1)
                            act.activation(sq[:, s, :], dev[:, s, :], ACT.Square).then_inc(sm["squares"], 1)
                        for s in range(U):
                            act.wait_ge(sm["vars"], U * g + s + 1)
                            act.activation(log[:, s, :], STAT[:, s, :], ACT.Ln, bias=eps[:, 0:1]).then_inc(sm["logs"], 1)
                        for s in range(U):
                            act.wait_ge(sm["logs"], U * g + s + 1)
                            act.activation(inv[:, s, :], log[:, s, :], ACT.Exp, scale=-0.5).then_inc(sm["invs"], 1)
                        for s in range(U):
                            act.wait_ge(sm["scaled"], U * g + s + 1)
                            act.activation(hx[:, s, :], hn[:, s, :], ACT.Identity, bias=lb[:, 0:1],
                                           scale=lg[:, 0:1]).then_inc(sm["normed"], 1)
                    for k in range(U * NC):
                        c = k % NC
                        w = width[c]
                        act.wait_ge(sm["gate_made"], NC * U * g + k + 1)
                        if k >= 2:
                            act.wait_ge(sm["hidden"], NC * U * g + k - 1)
                        if gelu:
                            act.activation(gate_on[0:w, k % 2, :], G[0:w, k % 2, :], ACT.Gelu,
                                           bias=bg[0:w, c:c + 1]).then_inc(sm["gated"], 1)
                        else:
                            act.activation(gate_on[0:w, k % 2, :], G[0:w, k % 2, :], ACT.Silu).then_inc(sm["gated"], 1)

            @block.vector
            def _(dve):
                dve.sem_inc(sm["trip_done"], 1)
                dve.wait_ge(sm["loaded"], 16 * 11 if gelu else loads)
                if gelu:
                    dve.wait_ge(sm["zeroed"], 1)
                else:
                    for dst, src in ((wg, ig), (wu, iu)):
                        dve.tensor_scalar(dst[:, :], src[:, :], 1.0 / 127.0, None, ALU.mult).then_inc(sm["weights_ready"], 1)
                    dve.tensor_scalar(wd[:, :, :], idn[:, :, :], 1.0 / 127.0, None, ALU.mult).then_inc(sm["weights_ready"], 1)
                with dve.Fori(0, NBLK // U) as g:
                    if gelu:
                        for s in range(U):
                            dve.wait_ge(sm["trip_done"], g + 1)
                            dve.tensor_copy(hs[0:64, s, :], R[0:64, ds((U * g + s) * BLK, BLK)])
                            for q in range(2):
                                o = dve.tensor_copy(hs[64:P, s, q * L + 1:(q + 1) * L],
                                                    R[64:P, ds((U * g + s) * BLK + q * L, L - 1)])
                            o.then_inc(sm["shifted"], 1)
                        for s in range(U):
                            dve.wait_ge(sm["means"], U * g + s + 1)
                            dve.tensor_tensor(dev[:, s, :], hs[:, s, :], STAT[:, s, :], ALU.subtract).then_inc(sm["devs"], 1)

                    def residual(s):
                        dve.wait_ge(sm["out_made"], U * g + s + 1)
                        at = ds((U * g + s) * BLK, BLK)
                        if gelu:
                            o = dve.scalar_tensor_tensor(R[:, at], OUT[:, s, :], b2[:, 0:1], R[:, at], ALU.add, ALU.add)
                        else:
                            o = dve.scalar_tensor_tensor(R[:, at], OUT[:, s, :], 0.5, R[:, at], ALU.mult, ALU.add)
                        if s == U - 1:
                            o.then_inc(sm["trip_done"], 1)

                    for k in range(U * NC):
                        s, c = k // NC, k % NC
                        w = width[c]
                        dve.wait_ge(sm["gated"], NC * U * g + k + 1)
                        dve.wait_ge(sm["up_made"], NC * U * g + k + 1)
                        if gelu:
                            dve.scalar_tensor_tensor(hid[0:w, s, c, :], UP[0:w, k % 2, :], ba[0:w, c:c + 1],
                                                     gate_on[0:w, k % 2, :], ALU.add, ALU.mult).then_inc(sm["hidden"], 1)
                        else:
                            dve.tensor_tensor(hid[0:w, s, c, :], UP[0:w, k % 2, :], gate_on[0:w, k % 2, :],
                                              ALU.mult).then_inc(sm["hidden"], 1)
                    residual(0)
                    residual(1)


def add_half(nc, tag, X, Y):
    with Phase(nc, tag) as ph:
        with nc.Block() as block:
            @block.vector
            def _(dve):
                dve.scalar_tensor_tensor(X[:, :], Y[:, 0:T], 0.5, X[:, :], ALU.mult, ALU.add)


def latent_attention(nc, tag, X, XN, A, W, ident):
    scale = 8 ** -0.5
    NP_ = 8
    with Phase(nc, tag) as ph:
        xs, xopen = ph.sb("xs", [P, L]), ph.sb("xopen", [P, 2, 64])
        wk, wkx, wv, wp = (ph.sb(n, [P, P]) for n in ("wk", "wkx", "wv", "wp"))
        wg = ph.sb("wg", [P, 1024])
        lat = ph.sb("lat", [P, NP_, P])
        rt = ph.sb("rt", [P, 2, L])
        lmask = ph.sb("lmask", [P, 64])
        own = ph.sb("own", [P, NP_, P])
        parts, kr = ph.sb("parts", [P, 2, L]), ph.sb("kr", [P, L])
        V = ph.sb("V", [P, P])
        s1, s2, pr = ph.sb("s1", [P, 16, 64]), ph.sb("s2", [P, 16, 64]), ph.sb("pr", [P, 16, 64])
        smax, ssum, sinv = (ph.sb(n, [P, 16]) for n in ("smax", "ssum", "sinv"))
        prT, att = ph.sb("prT", [P, NP_, P]), ph.sb("att", [P, NP_, P])
        gmax, gsum, ginv = (ph.sb(n, [P, 2, 16]) for n in ("gmax", "gsum", "ginv"))
        g1, g2, g3 = (ph.sb(n, [P, 2, 16, 64]) for n in ("g1", "g2", "g3"))
        gT = ph.sb("gT", [P, NP_, L])
        wt = ph.sb("wt", [P, L])
        PJ, PV = ph.ps("PJ", [P, 512]), ph.ps("PV", [P, 512])
        SC, GA, TR = ph.ps("SC", [P, 2, 512]), ph.ps("GA", [P, 2, 512]), ph.ps("TR", [P, 2, 512])
        names = ("loaded cleared staged k_made v_made parts_made k_ready v_copied scored s1_made smaxed s2_made s_exped "
                 "ssummed sinverted probs p_turned p_copied att_made att_ready g_made gmaxed g1_made g_exped gsummed "
                 "ginverted gates g_turned g_copied weighted w_copied final trip_done").split()
        sm = {n: ph.sem(n) for n in names}
        loads = 16 * (8 + 16)
        flat = (lambda ap: ap.rearrange("p (h l) -> p h l", l=64))

        def spread(ap, n):
            return ap.rearrange("p (h o) -> p h o", o=1).broadcast_to([P, ap.shape[1], n])

        with nc.Block() as block:
            @block.sync
            def _(sp):
                for dst, n in ((wk, "k"), (wkx, "k_crossed"), (wv, "v"), (wp, "p"), (wg, "g")):
                    load(sp, dst[:, :], W[n], sm["loaded"])
                load(sp, rt[:, :, :], A["rope8"], sm["loaded"])
                load(sp, lmask[:, :], A["latent_mask"], sm["loaded"])
                load(sp, own[:, :, :], A["own_head"], sm["loaded"])
                sp.wait_ge(sm["cleared"], 1)
                for h in range(16):
                    load(sp, lat[8 * h:8 * h + 8, h // 2, (h % 2) * 64:(h % 2) * 64 + 64], W["q"][h, :, :], sm["loaded"])

            @block.gpsimd
            def _(pool):
                pool.memset(lat[:, :, :], 0.0).then_inc(sm["cleared"], 1)
                with pool.Fori(0, NB) as b:
                    pool.wait_ge(sm["parts_made"], b + 1)
                    pool.tensor_tensor(kr[:, :], parts[:, 0, :], parts[:, 1, :], ALU.add).then_inc(sm["k_ready"], 1)
                    for t in range(2):
                        pool.wait_ge(sm["ginverted"], 2 * b + t + 1)
                        pool.tensor_tensor(g3[:, t, :, :], g2[:, t, :, :], spread(ginv[:, t, :], 64), ALU.mult).then_inc(sm["gates"], 1)

            @block.tensor
            def _(pe):
                pe.wait_ge(sm["loaded"], loads)
                with pe.Fori(0, NB) as b:
                    pe.wait_ge(sm["staged"], 2 * b + 2)
                    pe.matmul(PJ[:, 0:L], wk[:, :], xs[:, :], start=True, stop=True)
                    pe.matmul(PJ[:, L:2 * L], wkx[:, :], xs[:, :], start=True, stop=True).then_inc(sm["k_made"], 1)
                    pe.matmul(PV[:, 0:P], xopen[:, :, :], wv[:, :], start=True,
                              stop=True).then_inc(sm["v_made"], 1)
                    for q in range(2):
                        pe.matmul(GA[:, q, :], xs[:, 0:P], wg[:, q * 512:(q + 1) * 512], start=True, stop=True).then_inc(sm["g_made"], 1)
                    pe.wait_ge(sm["k_ready"], b + 1)
                    open_keys = kr[:, :].rearrange("p (n t) -> p n t", n=2)[:, :, 0:64]
                    for i in range(NP_):
                        o = pe.matmul(SC[:, i // 4, (i % 4) * P:(i % 4 + 1) * P], lat[:, i, :], open_keys, start=True, stop=True)
                        if i % 4 == 3:
                            o.then_inc(sm["scored"], 1)
                    for q in range(2):
                        pe.wait_ge(sm["g1_made"], 4 * b + q + 1)
                        pe.matmul(GA[:, q, :], xs[:, P:L], wg[:, q * 512:(q + 1) * 512], start=True, stop=True).then_inc(sm["g_made"], 1)
                    pe.wait_ge(sm["probs"], b + 1)
                    for i in range(NP_):
                        o = pe.transpose(TR[:, i // 4, (i % 4) * P:(i % 4 + 1) * P],
                                         pr[:, 2 * i:2 * i + 2, :], ident[:, :])
                        if i % 4 == 3:
                            o.then_inc(sm["p_turned"], 1)
                    pe.wait_ge(sm["p_copied"], 2 * b + 2)
                    pe.wait_ge(sm["v_copied"], b + 1)
                    pe.wait_ge(sm["s1_made"], 2 * b + 2)
                    for i in range(NP_):
                        o = pe.matmul(SC[:, i // 4, (i % 4) * P:(i % 4 + 1) * P], prT[:, i, :], V[:, :], start=True, stop=True)
                        if i % 4 == 3:
                            o.then_inc(sm["att_made"], 1)
                    for t in range(2):
                        pe.wait_ge(sm["gates"], 2 * b + t + 1)
                        for q in range(2):
                            if t == 1:
                                pe.wait_ge(sm["g_copied"], 4 * b + q + 1)
                            for i in range(4):
                                pair = 4 * q + i
                                o = pe.transpose(TR[:, q, i * P:(i + 1) * P], g3[:, t, 2 * pair:2 * pair + 2, :], ident[:, :])
                            o.then_inc(sm["g_turned"], 1)
                    pe.wait_ge(sm["g_copied"], 4 * b + 4)
                    pe.wait_ge(sm["att_ready"], 2 * b + 2)
                    for i in range(NP_):
                        o = pe.matmul(PV[:, 0:L], att[:, i, :], gT[:, i, :], start=i == 0, stop=i == NP_ - 1)
                    o.then_inc(sm["weighted"], 1)
                    pe.wait_ge(sm["w_copied"], b + 1)
                    pe.matmul(PJ[:, 0:L], wp[:, :], wt[:, :], start=True, stop=True).then_inc(sm["final"], 1)

            @block.scalar
            def _(act):
                with act.Fori(0, NB) as b:
                    act.wait_ge(sm["v_made"], b + 1)
                    act.activation(V[:, :], PV[:, 0:P], ACT.Copy).then_inc(sm["v_copied"], 1)
                    act.wait_ge(sm["g1_made"], 4 * b + 2)
                    act.activation(g2[:, 0, :, :], g1[:, 0, :, :], ACT.Exp, scale=scale).then_inc(sm["g_exped"], 1)
                    act.wait_ge(sm["s2_made"], b + 1)
                    act.activation(pr[:, :, :], s2[:, :, :], ACT.Exp).then_inc(sm["s_exped"], 1)
                    act.wait_ge(sm["g1_made"], 4 * b + 4)
                    act.activation(g2[:, 1, :, :], g1[:, 1, :, :], ACT.Exp, scale=scale).then_inc(sm["g_exped"], 1)
                    for q in range(2):
                        act.wait_ge(sm["p_turned"], 2 * b + q + 1)
                        act.activation(prT[:, 4 * q:4 * q + 4, :], TR[:, q, :].rearrange("p (i c) -> p i c", i=4),
                                       ACT.Copy).then_inc(sm["p_copied"], 1)
                    for t in range(2):
                        for q in range(2):
                            act.wait_ge(sm["g_turned"], 4 * b + 2 * t + q + 1)
                            act.activation(gT[:, 4 * q:4 * q + 4, t * P:(t + 1) * P],
                                           TR[:, q, :].rearrange("p (i c) -> p i c", i=4), ACT.Copy).then_inc(sm["g_copied"], 1)
                    act.wait_ge(sm["weighted"], b + 1)
                    act.activation(wt[:, :], PV[:, 0:L], ACT.Copy).then_inc(sm["w_copied"], 1)

            @block.vector
            def _(dve):
                dve.sem_inc(sm["trip_done"], 1)
                dve.wait_ge(sm["loaded"], loads)
                with dve.Fori(0, NB) as b:
                    dve.wait_ge(sm["trip_done"], b + 1)
                    dve.tensor_copy(xs[:, :], XN[:, ds(b * L, L)]).then_inc(sm["staged"], 1)
                    for n in range(2):
                        o = dve.tensor_copy(xopen[:, n, :], XN[:, ds(b * L + n * P, 64)])
                    o.then_inc(sm["staged"], 1)
                    dve.wait_ge(sm["k_made"], b + 1)
                    dve.tensor_tensor(parts[:, :, :], PJ[:, :].rearrange("p (w n) -> p w n", w=2), rt[:, :, :],
                                      ALU.mult).then_inc(sm["parts_made"], 1)

                    def gate_tile(t):
                        for q in range(2):
                            dve.wait_ge(sm["g_made"], 4 * b + 2 * t + q + 1)
                            dve.tensor_reduce(gmax[:, t, 8 * q:8 * q + 8], flat(GA[:, q, :]), AX, ALU.max).then_inc(sm["gmaxed"], 1)
                        for q in range(2):
                            dve.wait_ge(sm["gmaxed"], 4 * b + 2 * t + q + 1)
                            dve.tensor_tensor(g1[:, t, 8 * q:8 * q + 8, :], flat(GA[:, q, :]),
                                              spread(gmax[:, t, 8 * q:8 * q + 8], 64), ALU.subtract).then_inc(sm["g1_made"], 1)

                    gate_tile(0)
                    for q in range(2):
                        dve.wait_ge(sm["scored"], 2 * b + q + 1)
                        m = lmask[:, :].rearrange("p (o c) -> p o c", o=1).broadcast_to([P, 8, 64])
                        dve.scalar_tensor_tensor(s1[:, 8 * q:8 * q + 8, :], flat(SC[:, q, :]), scale, m, ALU.mult,
                                                 ALU.add).then_inc(sm["s1_made"], 1)
                    dve.wait_ge(sm["s1_made"], 2 * b + 2)
                    dve.tensor_reduce(smax[:, :], s1[:, :, :], AX, ALU.max).then_inc(sm["smaxed"], 1)
                    dve.wait_ge(sm["smaxed"], b + 1)
                    dve.tensor_tensor(s2[:, :, :], s1[:, :, :], spread(smax[:, :], 64), ALU.subtract).then_inc(sm["s2_made"], 1)
                    gate_tile(1)
                    dve.wait_ge(sm["s_exped"], b + 1)
                    dve.tensor_reduce(ssum[:, :], pr[:, :, :], AX, ALU.add).then_inc(sm["ssummed"], 1)
                    dve.wait_ge(sm["ssummed"], b + 1)
                    dve.reciprocal(sinv[:, :], ssum[:, :]).then_inc(sm["sinverted"], 1)
                    dve.wait_ge(sm["sinverted"], b + 1)
                    dve.tensor_tensor(pr[:, :, :], pr[:, :, :], spread(sinv[:, :], 64), ALU.mult).then_inc(sm["probs"], 1)
                    for t in range(2):
                        dve.wait_ge(sm["g_exped"], 2 * b + t + 1)
                        dve.tensor_reduce(gsum[:, t, :], g2[:, t, :, :], AX, ALU.add).then_inc(sm["gsummed"], 1)
                        dve.wait_ge(sm["gsummed"], 2 * b + t + 1)
                        dve.reciprocal(ginv[:, t, :], gsum[:, t, :]).then_inc(sm["ginverted"], 1)
                    for q in range(2):
                        dve.wait_ge(sm["att_made"], 2 * b + q + 1)
                        dve.tensor_tensor(att[:, 4 * q:4 * q + 4, :], SC[:, q, :].rearrange("p (i c) -> p i c", i=4),
                                          own[:, 4 * q:4 * q + 4, :], ALU.mult).then_inc(sm["att_ready"], 1)
                    dve.wait_ge(sm["final"], b + 1)
                    at = ds(b * L, L)
                    dve.tensor_tensor(X[:, at], PJ[:, 0:L], X[:, at], ALU.add).then_inc(sm["trip_done"], 1)


def product_key_experts(nc, tag, X, XN, A, W, ident, eps):
    NH, NK, E = 8, 32, 1024
    U = 2
    NU = U * NH
    RING = 4
    with Phase(nc, tag) as ph:
        wq = ph.sb("wq", [P, 16, P])
        keys = ph.sb("keys", [P, 2, NH, NK])
        fused = ph.sb("fused", [P, 2, NH, NK])
        down, up = ph.sb("down", [P, E]), ph.sb("up", [P, 8, P])
        gam, bet = ph.sb("gam", [P, 1]), ph.sb("bet", [P, 1])
        st, mv = ph.sb("st", [P, NBLK, 6]), ph.sb("mv", [P, 2])
        col = ph.sb("col", [P, 4])
        ms = ph.sb("ms", [P, 1])
        xb = ph.sb("xb", [P, P])
        sim = ph.sb("sim", [P, U, 2, NH, NK])
        top = ph.sb("top", [P, 2, NH, 8])
        cand = ph.sb("cand", [P, NH, 64])
        best = ph.sb("best", [P, U, NH, 8])
        S, sg, w = ph.sb("S", [P, RING, E]), ph.sb("sg", [P, RING, E]), ph.sb("w", [P, RING, E])
        act_h = ph.sb("act_h", [P, 8, U * P])
        mix = ph.sb("mix", [P, 8, U * P])
        SIM = ph.ps("SIM", [P, 512])
        WT = ph.ps("WT", [P, U, 2, 512])
        HT = ph.ps("HT", [P, 2, 512])
        OUT = ph.ps("OUT", [P, 512])
        names = ("loaded stats moments sds invs scales negs affine fused_made fused_ready normed sim_made sim_copied "
                 "tops cands bests summed sigm weighed w_turned h_made h_on mixed out_made added passed").split()
        sm = {n: ph.sem(n) for n in names}
        loads = 16 * 6
        with nc.Block() as block:
            @block.sync
            def _(sp):
                load(sp, gam[:, :], W["gamma"].rearrange("(p c) -> p c", c=1), sm["loaded"])
                load(sp, bet[:, :], W["beta"].rearrange("(p c) -> p c", c=1), sm["loaded"])
                load(sp, wq[:, :, :], W["w_q"].rearrange("(n k) c -> k n c", k=P), sm["loaded"])
                load(sp, keys[:, :, :, :], W["keys"], sm["loaded"])
                load(sp, down[:, :], W["down"], sm["loaded"])
                load(sp, up[:, :, :], W["up"].rearrange("(n e) c -> e n c", e=P), sm["loaded"])

            @block.gpsimd
            def _(pool):
                with pool.Fori(0, NT // U) as g:
                    for k in range(NU):
                        s, h = k // NH, k % NH
                        if h == 0:
                            pool.wait_ge(sm["sim_copied"], U * g + s + 1)
                        pool.wait_ge(sm["weighed"], NU * g + k + 1)
                        a = sim[:, s, 0, h, :].rearrange("p (i o) -> p i o", o=1).broadcast_to([P, NK, NK])
                        c = sim[:, s, 1, h, :].rearrange("p (o i) -> p o i", o=1).broadcast_to([P, NK, NK])
                        pool.tensor_tensor(S[:, k % RING, :].rearrange("p (a c) -> p a c", a=NK), a, c,
                                           ALU.add).then_inc(sm["summed"], 1)

            @block.tensor
            def _(pe):
                pe.wait_ge(sm["loaded"], loads)
                for n in range(16):
                    o = pe.matmul(SIM[:, n * NK:(n + 1) * NK], wq[:, n, :], keys[:, n // NH, n % NH, :], start=True, stop=True)
                o.then_inc(sm["fused_made"], 1)
                pe.wait_ge(sm["fused_ready"], 1)

                def similarities(tile):
                    pe.wait_ge(sm["normed"], tile + 1)
                    if not isinstance(tile, int):
                        pe.wait_ge(sm["sim_copied"], tile)
                    pe.matmul(SIM[:, :], xb[:, :], fused[:, :, :, :], start=True, stop=True).then_inc(sm["sim_made"], 1)

                similarities(0)
                with pe.Fori(0, NT // U) as g:
                    for k in range(NU):
                        s, h = k // NH, k % NH
                        if h == 0:
                            pe.wait_ge(sm["mixed"], 4 * g + 2 * s + 2)
                        pe.wait_ge(sm["weighed"], NU * g + k + 1 + RING)
                        for n in range(8):
                            o = pe.matmul(WT[:, s, n // 4, (n % 4) * P:(n % 4 + 1) * P], w[:, k % RING, n * P:(n + 1) * P],
                                          ident[:, :], start=h == 0 and n % 4 == 0, stop=h == NH - 1,
                                          is_transpose=True, skip_group_check=True)
                        o.then_inc(sm["w_turned"], 1)
                        if h == 0:
                            similarities(U * g + s + 1)
                        if s == 0 and h in (2, 4):
                            for r in (h - 2, h - 1):
                                pe.wait_ge(sm["h_on"], 4 * g + r + 1)
                                for n in (2 * r, 2 * r + 1):
                                    o = pe.matmul(HT[:, r % 2, (n % 2) * U * P:(n % 2 + 1) * U * P], down[:, n * P:(n + 1) * P],
                                                  XN[:, ds(g * U * P, U * P)], start=True, stop=True)
                                o.then_inc(sm["h_made"], 1)
                    pe.wait_ge(sm["mixed"], 4 * g + 8)
                    pe.wait_ge(sm["added"], g + 1)
                    for n in range(8):
                        o = pe.matmul(OUT[:, 0:U * P], up[:, n, :], mix[:, n, :], start=n == 0, stop=n == 7)
                    o.then_inc(sm["out_made"], 1)

            @block.scalar
            def _(act):
                act.wait_ge(sm["moments"], 1)
                act.activation(col[:, 0:1], mv[:, 1:2], ACT.Sqrt, bias=eps[:, 0:1]).then_inc(sm["sds"], 1)
                act.wait_ge(sm["fused_made"], 1)
                act.activation(fused[:, :, :, :], SIM[:, :].rearrange("p (a b c) -> p a b c", a=2, b=NH), ACT.Copy).then_inc(sm["fused_ready"], 1)
                act.wait_ge(sm["affine"], 1)

                def normed(tile):
                    act.activation(xb[:, :], XN[:, ds(tile * P, P)], ACT.Identity, bias=col[:, 3:4],
                                   scale=col[:, 2:3]).then_inc(sm["normed"], 1)

                def copy_similarities(tile, slot):
                    act.wait_ge(sm["sim_made"], tile + 1)
                    act.activation(sim[:, slot, :, :, :], SIM[:, :].rearrange("p (a b c) -> p a b c", a=2, b=NH),
                                   ACT.Copy).then_inc(sm["sim_copied"], 1)

                act.wait_ge(sm["fused_ready"], 1)
                normed(0)
                copy_similarities(0, 0)
                with act.Fori(0, NT // U) as g:
                    for k in range(NU):
                        s, h = k // NH, k % NH
                        if h == 0:
                            normed(U * g + s + 1)
                        if h == 4:
                            copy_similarities(U * g + s + 1, 1 - s)
                        if k == 6:
                            act.wait_ge(sm["mixed"], 4 * g + 4)
                            for r in range(4):
                                act.wait_ge(sm["h_made"], 4 * g + r + 1)
                                act.activation(act_h[:, 2 * r:2 * r + 2, :], HT[:, r % 2, :].rearrange("p (n c) -> p n c", n=2),
                                               ACT.Gelu).then_inc(sm["h_on"], 1)
                        act.wait_ge(sm["summed"], NU * g + k + 1)
                        act.wait_ge(sm["weighed"], NU * g + k + 1)
                        act.activation(sg[:, k % RING, :], S[:, k % RING, :], ACT.Sigmoid).then_inc(sm["sigm"], 1)

            @block.vector
            def _(dve):
                dve.sem_inc(sm["weighed"], RING)
                dve.sem_inc(sm["w_turned"], RING)
                dve.sem_inc(sm["mixed"], 4)
                dve.sem_inc(sm["h_on"], 2)
                dve.sem_inc(sm["added"], 1)
                for j in range(NBLK):
                    dve.bn_stats(st[:, j, :], XN[:, j * BLK:(j + 1) * BLK]).then_inc(sm["stats"], 1)
                dve.wait_ge(sm["stats"], NBLK)
                dve.bn_aggr(mv[:, :], st[:, :, :]).then_inc(sm["moments"], 1)
                dve.wait_ge(sm["sds"], 1)
                dve.reciprocal(col[:, 1:2], col[:, 0:1]).then_inc(sm["invs"], 1)
                dve.wait_ge(sm["invs"], 1)
                dve.wait_ge(sm["loaded"], loads)
                dve.tensor_tensor(col[:, 2:3], col[:, 1:2], gam[:, :], ALU.mult).then_inc(sm["scales"], 1)
                dve.wait_ge(sm["scales"], 1)
                dve.tensor_tensor(ms[:, :], mv[:, 0:1], col[:, 2:3], ALU.mult).then_inc(sm["negs"], 1)
                dve.wait_ge(sm["negs"], 1)
                dve.tensor_tensor(col[:, 3:4], bet[:, :], ms[:, :], ALU.subtract).then_inc(sm["affine"], 1)

                def best_of_sides(tile, slot):
                    dve.wait_ge(sm["sim_copied"], tile + 1)
                    dve.sem_inc(sm["passed"], 1)
                    for n in range(16):
                        o = dve.max(top[:, n // NH, n % NH, :], sim[:, slot, n // NH, n % NH, :])
                    o.then_inc(sm["tops"], 1)

                def best_pairs(tile, slot):
                    dve.wait_ge(sm["tops"], tile + 1)
                    a = top[:, 0, :, :].rearrange("p h (i o) -> p h i o", o=1).broadcast_to([P, NH, 8, 8])
                    c = top[:, 1, :, :].rearrange("p h (o i) -> p h o i", o=1).broadcast_to([P, NH, 8, 8])
                    dve.tensor_tensor(cand[:, :, :].rearrange("p h (i j) -> p h i j", i=8), a, c, ALU.add).then_inc(sm["cands"], 1)
                    dve.wait_ge(sm["cands"], tile + 1)
                    dve.sem_inc(sm["passed"], 1)
                    for h in range(NH):
                        o = dve.max(best[:, slot, h, :], cand[:, h, :])
                    o.then_inc(sm["bests"], 1)

                best_of_sides(0, 0)
                best_pairs(0, 0)
                with dve.Fori(0, NT // U) as g:
                    for s in range(U):
                        dve.wait_ge(sm["bests"], U * g + s + 1)
                        for h in range(NH):
                            k = s * NH + h
                            dve.wait_ge(sm["sigm"], NU * g + k + 1)
                            dve.wait_ge(sm["w_turned"], NU * g + k + 1)
                            dve.scalar_tensor_tensor(w[:, k % RING, :], S[:, k % RING, :], best[:, s, h, 7:8], sg[:, k % RING, :],
                                                     ALU.is_ge, ALU.mult).then_inc(sm["weighed"], 1)
                        best_of_sides(U * g + s + 1, 1 - s)
                        dve.wait_ge(sm["w_turned"], NU * g + (s + 1) * NH + RING)
                        dve.wait_ge(sm["h_on"], 4 * g + 4 + 2)
                        for q in range(2):
                            dve.tensor_tensor(mix[:, 4 * q:4 * q + 4, s * P:(s + 1) * P],
                                              WT[:, s, q, :].rearrange("p (n c) -> p n c", n=4),
                                              act_h[:, 4 * q:4 * q + 4, s * P:(s + 1) * P], ALU.mult).then_inc(sm["mixed"], 1)
                        best_pairs(U * g + s + 1, 1 - s)
                    dve.wait_ge(sm["out_made"], g + 1)
                    at = ds(g * U * P, U * P)
                    dve.scalar_tensor_tensor(X[:, at], OUT[:, 0:U * P], 0.5, X[:, at], ALU.mult, ALU.add).then_inc(sm["added"], 1)


NE, CAP = 64, 64
NPAIRS = NE // 2


def routed_experts(nc, tag, X, XN, A, W, ident, rows_dram):
    NPAIR = NE // 2
    with ExitStack() as keep:
        place = keep.enter_context(nc.sbuf_tensor(f"{tag}_place", [P, NT, NE], F32))
        vals = keep.enter_context(nc.sbuf_tensor(f"{tag}_vals", [P, NT, NPAIR, 3], F32))
        info = keep.enter_context(nc.sbuf_tensor(f"{tag}_info", [P, NPAIR, 3], F32))
        Eout = keep.enter_context(nc.sbuf_tensor(f"{tag}_Eout", [P, NPAIR, P], F32))
        route(nc, tag + "r", XN, A, W, ident, rows_dram, place, vals)
        find_slots(nc, tag + "s", A, place, vals, info)
        run_experts(nc, tag + "e", A, W, ident, rows_dram, info, Eout)
        combine(nc, tag + "c", X, XN, W, info, Eout)


def route(nc, tag, XN, A, W, ident, rows_dram, place, vals):
    with Phase(nc, tag) as ph:
        wr = ph.sb("wr", [P, NE])
        tri, ones, token = ph.sb("tri", [P, P]), ph.sb("ones", [P, P]), ph.sb("token", [P, NT])
        U = 2
        xs = ph.sb("xs", [P, U, P])
        rows = ph.sb("rows", [P, U, P])
        sc, masked, left, sel = (ph.sb(n, [P, U, NE]) for n in ("sc", "masked", "left", "sel"))
        gmax, gtop, gopen, top = (ph.sb(n, [P, U, 8]) for n in ("gmax", "gtop", "gopen", "top"))
        tsum, tclip, tinv = (ph.sb(n, [P, U]) for n in ("tsum", "tclip", "tinv"))
        wsel, wall, pos = (ph.sb(n, [P, U, NE]) for n in ("wsel", "wall", "pos"))
        before = ph.sb("before", [P, 2, NE])
        LG, RW, CN = ph.ps("LG", [P, U, 512]), ph.ps("RW", [P, U, 512]), ph.ps("CN", [P, U, 512])
        names = ("loaded staged logits rows_made rows_copied rows_out scored gmaxed gtopped gopened masks topped lefted "
                 "selected tsums tclips tinvs wsels walls vals_made counted before_made poss places zeroed trip_done passed").split()
        sm = {n: ph.sem(n) for n in names}
        with nc.Block() as block:
            @block.sync
            def _(sp):
                for dst, src in ((wr, W["router"]), (tri, A["tri"]), (ones, A["ones"]), (token, A["token"])):
                    load(sp, dst[:, :], src, sm["loaded"])
                sp.sem_inc(sm["rows_out"], 16)
                with sp.Fori(0, NT // U) as g:
                    for s in range(U):
                        sp.wait_ge(sm["rows_copied"], U * g + s + 1)
                        sp.dma_start(rows_dram[ds((U * g + s) * P, P), :], rows[:, s, :]).then_inc(sm["rows_out"], 16)
                sp.wait_ge(sm["rows_out"], 16 * NT + 16)

            @block.tensor
            def _(pe):
                pe.wait_ge(sm["loaded"], 64)
                pe.wait_ge(sm["zeroed"], 1)
                with pe.Fori(0, NT // U) as g:
                    pe.wait_ge(sm["trip_done"], g + 1)
                    for s in range(U):
                        pe.wait_ge(sm["staged"], U * g + s + 1)
                        pe.matmul(LG[:, s, 0:NE], xs[:, s, :], wr[:, :], start=True, stop=True).then_inc(sm["logits"], 1)
                        pe.transpose(RW[:, s, 0:P], xs[:, s, :], ident[:, :]).then_inc(sm["rows_made"], 1)
                    for s in range(U):
                        pe.wait_ge(sm["selected"], U * g + s + 1)
                        pe.matmul(CN[:, s, 0:NE], tri[:, :], sel[:, s, :], start=True, stop=False)
                        pe.wait_ge(sm["before_made"], U * g + s + 1)
                        pe.matmul(CN[:, s, 0:NE], ones[:, :], before[:, s, :], start=False, stop=True).then_inc(sm["counted"], 1)

            @block.scalar
            def _(act):
                with act.Fori(0, NT // U) as g:
                    act.wait_ge(sm["trip_done"], g + 1)
                    act.wait_ge(sm["rows_out"], 16 * U * g + 16)
                    for s in range(U):
                        act.activation(xs[:, s, :], XN[:, ds((U * g + s) * P, P)], ACT.Copy).then_inc(sm["staged"], 1)
                    for s in range(U):
                        act.wait_ge(sm["logits"], U * g + s + 1)
                        act.activation(sc[:, s, :], LG[:, s, 0:NE], ACT.Sigmoid).then_inc(sm["scored"], 1)
                        act.wait_ge(sm["rows_made"], U * g + s + 1)
                        act.activation(rows[:, s, :], RW[:, s, 0:P], ACT.Copy).then_inc(sm["rows_copied"], 1)

            @block.vector
            def _(dve):
                dve.sem_inc(sm["trip_done"], 1)
                dve.sem_inc(sm["before_made"], 1)
                dve.memset(before[:, :, :], 0.0).then_inc(sm["zeroed"], 1)
                dve.wait_ge(sm["zeroed"], 1)
                dve.wait_ge(sm["loaded"], 64)
                with dve.Fori(0, NT // U) as g:
                    at = lambda s: U * g + s + 1
                    grp = lambda ap: ap.rearrange("p (g e) -> p g e", g=8)
                    dve.wait_ge(sm["trip_done"], g + 1)
                    for s in range(U):
                        dve.wait_ge(sm["scored"], at(s))
                        dve.tensor_reduce(gmax[:, s, :], grp(sc[:, s, :]), AX, ALU.max).then_inc(sm["gmaxed"], 1)
                    for s in range(U):
                        dve.wait_ge(sm["gmaxed"], at(s))
                        dve.sem_inc(sm["passed"], 1)
                        dve.max(gtop[:, s, :], gmax[:, s, :]).then_inc(sm["gtopped"], 1)
                    for s in range(U):
                        dve.wait_ge(sm["gtopped"], at(s))
                        dve.tensor_scalar(gopen[:, s, :], gmax[:, s, :], gtop[:, s, 3:4], None, ALU.is_ge).then_inc(sm["gopened"], 1)
                    for s in range(U):
                        dve.wait_ge(sm["gopened"], at(s))
                        dve.tensor_tensor(grp(masked[:, s, :]), grp(sc[:, s, :]),
                                          gopen[:, s, :].rearrange("p (g o) -> p g o", o=1).broadcast_to([P, 8, 8]),
                                          ALU.mult).then_inc(sm["masks"], 1)
                    for s in range(U):
                        dve.wait_ge(sm["masks"], at(s))
                        dve.sem_inc(sm["passed"], 1)
                        dve.max(top[:, s, :], masked[:, s, :]).then_inc(sm["topped"], 1)
                    for s in range(U):
                        dve.wait_ge(sm["topped"], at(s))
                        dve.sem_inc(sm["passed"], 1)
                        dve.match_replace(left[:, s, :], top[:, s, :], masked[:, s, :], -1.0).then_inc(sm["lefted"], 1)
                    for s in range(U):
                        dve.wait_ge(sm["lefted"], at(s))
                        dve.tensor_tensor(sel[:, s, :], left[:, s, :], masked[:, s, :], ALU.not_equal).then_inc(sm["selected"], 1)
                        dve.tensor_reduce(tsum[:, s:s + 1], top[:, s, :], AX, ALU.add).then_inc(sm["tsums"], 1)
                    for s in range(U):
                        dve.wait_ge(sm["tsums"], at(s))
                        dve.tensor_scalar(tclip[:, s:s + 1], tsum[:, s:s + 1], 1e-9, None, ALU.max).then_inc(sm["tclips"], 1)
                    for s in range(U):
                        dve.wait_ge(sm["tclips"], at(s))
                        dve.reciprocal(tinv[:, s:s + 1], tclip[:, s:s + 1]).then_inc(sm["tinvs"], 1)
                    for s in range(U):
                        dve.wait_ge(sm["selected"], at(s))
                        dve.tensor_tensor(wsel[:, s, :], sel[:, s, :], masked[:, s, :], ALU.mult).then_inc(sm["wsels"], 1)
                    for s in range(U):
                        dve.wait_ge(sm["tinvs"], at(s))
                        dve.wait_ge(sm["wsels"], at(s))
                        one = vals[:, ds(U * g + s, 1), :, :].rearrange("p o n c -> p (o n) c")
                        dve.tensor_scalar(one[:, :, 1:3], wsel[:, s, :].rearrange("p (n e) -> p n e", e=2), tinv[:, s:s + 1],
                                          2.5, ALU.mult, ALU.mult).then_inc(sm["walls"], 1)
                        dve.tensor_copy(one[:, :, 0], token[:, ds(U * g + s, 1)].broadcast_to([P, NE // 2])).then_inc(sm["vals_made"], 1)
                    for s in range(U):
                        dve.wait_ge(sm["counted"], at(s))
                        dve.wait_ge(sm["before_made"], U * g + s + 1)
                        dve.tensor_tensor(before[:, 1 - s, :], before[:, s, :], sel[:, s, :], ALU.add).then_inc(sm["before_made"], 1)
                        dve.tensor_scalar(pos[:, s, :], CN[:, s, 0:NE], 1.0, None, ALU.add).then_inc(sm["poss"], 1)
                    for s in range(U):
                        dve.wait_ge(sm["poss"], at(s))
                        o = dve.tensor_tensor(place[:, ds(U * g + s, 1), :].rearrange("p o e -> p (o e)"), pos[:, s, :],
                                              sel[:, s, :], ALU.mult)
                    o.then_inc(sm["trip_done"], 1)


def find_slots(nc, tag, A, place, vals, info):
    GE = 8
    NPG = GE // 2
    BF = mybir.dt.bfloat16
    NV = NT * NPAIRS * 3
    with Phase(nc, tag) as ph:
        slot1 = ph.sb("slot1", [P, GE, 64])
        R = 6
        hot = ph.sb("hot", [P, R, GE * CAP], BF)
        part = ph.sb("part", [P, NT, NPAIRS, 9], BF)
        rest1, rest2 = ph.sb("rest1", [P, NT, NPAIRS * 3]), ph.sb("rest2", [P, NT, NPAIRS * 3])
        zero = ph.sb("zero", [P, P], BF)
        pair_sum = ph.sb("pair_sum", [P, NPG, 3])
        IN = ph.ps("IN", [P, 2, 512])
        names = "loaded slots zeroed split hots used summed first_sum trip_done".split()
        sm = {n: ph.sem(n) for n in names}
        v3 = vals[:, :, :, :].rearrange("p t n c -> p (t n) c")
        p9 = part[:, :, :, :].rearrange("p t n c -> p (t n) c")
        r1, r2 = (r[:, :, :].rearrange("p t (n c) -> p (t n) c", c=3) for r in (rest1, rest2))
        with nc.Block() as block:
            @block.gpsimd
            def _(pool):
                pool.memset(zero[:, :], 0.0).then_inc(sm["zeroed"], 1)
                pool.iota(slot1[:, :, :], pattern=[[0, GE], [1, 64]], base=1, channel_multiplier=0,
                          allow_small_or_imprecise_dtypes=True).then_inc(sm["slots"], 1)

            @block.vector
            def _(dve):
                dve.sem_inc(sm["trip_done"], 1)
                dve.tensor_copy(p9[:, :, 0:3], v3).then_inc(sm["split"], 1)
                dve.wait_ge(sm["split"], 1)
                dve.tensor_tensor(r1, v3, p9[:, :, 0:3], ALU.subtract).then_inc(sm["split"], 1)
                dve.wait_ge(sm["split"], 2)
                dve.tensor_copy(p9[:, :, 3:6], r1).then_inc(sm["split"], 1)
                dve.wait_ge(sm["split"], 3)
                dve.tensor_tensor(r2, r1, p9[:, :, 3:6], ALU.subtract).then_inc(sm["split"], 1)
                dve.wait_ge(sm["split"], 4)
                dve.tensor_copy(p9[:, :, 6:9], r2).then_inc(sm["split"], 1)
                dve.wait_ge(sm["slots"], 1)
                with dve.Fori(0, NE // GE) as g:
                    for n in range(NT):
                        if n >= R:
                            dve.wait_ge(sm["used"], NT * g + n - R + 1)
                        else:
                            dve.wait_ge(sm["trip_done"], g + 1)
                        a = place[:, n, ds(g * GE, GE)].rearrange("p (e o) -> p e o", o=1).broadcast_to([P, GE, CAP])
                        dve.tensor_tensor(hot[:, n % R, :].rearrange("p (e c) -> p e c", e=GE), a, slot1[:, :, :],
                                          ALU.is_equal).then_inc(sm["hots"], 1)
                    dve.wait_ge(sm["summed"], g + 1)
                    tot = IN[:, 0, 0:9 * NPG].rearrange("p (n k c) -> p n k c", k=3, c=3)
                    dve.tensor_copy(pair_sum[:, :, :], tot[:, :, 2, :]).then_inc(sm["first_sum"], 1)
                    dve.wait_ge(sm["first_sum"], 2 * g + 1)
                    dve.tensor_tensor(pair_sum[:, :, :], tot[:, :, 1, :], pair_sum[:, :, :], ALU.add).then_inc(sm["first_sum"], 1)
                    dve.wait_ge(sm["first_sum"], 2 * g + 2)
                    dve.tensor_tensor(info[:, ds(g * NPG, NPG), :], tot[:, :, 0, :], pair_sum[:, :, :],
                                      ALU.add).then_inc(sm["trip_done"], 1)

            @block.tensor
            def _(pe):
                pe.wait_ge(sm["zeroed"], 1)
                pe.wait_ge(sm["split"], 5)
                with pe.Fori(0, NE // GE) as g:
                    pe.wait_ge(sm["trip_done"], g + 1)
                    pe.matmul(IN[:, 0, 0:9 * NPG], zero[:, :], zero[:, 0:9 * NPG], start=True, stop=True, skip_group_check=True)
                    for n in range(NT):
                        pe.wait_ge(sm["hots"], NT * g + n + 1)
                        for q in range(NPG):
                            o = pe.matmul(IN[:, 0, 9 * q:9 * q + 9], hot[:, n % R, q * P:(q + 1) * P],
                                          part[:, n, ds(g * NPG + q, 1), :].rearrange("p o c -> p (o c)"),
                                          start=False, stop=True, skip_group_check=True)
                        o.then_inc(sm["used"], 1)
                    pe.wait_ge(sm["used"], NT * g + NT)
                    pe.matmul(IN[:, 0, 0:9 * NPG], zero[:, :], zero[:, 0:9 * NPG], start=False, stop=True,
                              skip_group_check=True).then_inc(sm["summed"], 1)


def run_experts(nc, tag, A, W, ident, rows_dram, info, Eout):
    U = 2
    NPAIR = NE // 2
    with Phase(nc, tag) as ph:
        own = ph.sb("own", [P, P])
        tok = ph.sb("tok", [P, NPAIR], I32)
        ws = ph.sb("ws", [P, NPAIR])
        idx = ph.sb("idx", [P, U], I32)
        wgt, wut, wdt = ph.sb("wgt", [P, U, 2, 64]), ph.sb("wut", [P, U, 2, 64]), ph.sb("wdt", [P, U, P])
        xg, xT, gt, g2, hm = (ph.sb(n, [P, U, P]) for n in ("xg", "xT", "gt", "g2", "hm"))
        TR, GU, OU = ph.ps("TR", [P, U, 512]), ph.ps("GU", [P, U, 512]), ph.ps("OU", [P, U, 512])
        names = ("loaded toks wss own_in idxs gathered0 gathered1 turned copied gu_made gated ups hids outs weights0 weights1 "
                 "trip_done passed").split()
        sm = {n: ph.sem(n) for n in names}
        gate_w = W["gate"].rearrange("(n e) h i -> n h e i", e=2)
        up_w = W["up"].rearrange("(n e) h i -> n h e i", e=2)
        down_w = W["down"].rearrange("(n e) i h -> n (e i) h", e=2)
        with nc.Block() as block:
            @block.sync
            def _(sp):
                load(sp, own[:, :], A["block64"], sm["own_in"])
                with sp.Fori(0, NPAIR // U) as g:
                    sp.wait_ge(sm["trip_done"], g + 1)
                    for s in range(U):
                        n = U * g + s
                        w = sm[f"weights{s}"]
                        load(sp, wgt[:, s, :, :], gate_w[ds(n, 1)].rearrange("o h e i -> h (o e) i"), w)
                        load(sp, wut[:, s, :, :], up_w[ds(n, 1)].rearrange("o h e i -> h (o e) i"), w)
                        load(sp, wdt[:, s, :], down_w[ds(n, 1)].rearrange("o p h -> (o p) h"), w)

            @block.gpsimd
            def _(pool):
                with pool.Fori(0, NPAIR // U) as g:
                    pool.wait_ge(sm["trip_done"], g + 1)
                    for s in range(U):
                        pool.wait_ge(sm["idxs"], U * g + s + 1)
                        pool.sem_inc(sm["passed"], 1)
                        pool.indirect_dma_start(out=xg[:, s, :], out_offset=None, in_=rows_dram[:, :],
                                                in_offset=bass.IndirectOffsetOnAxis(ap=idx[:, s:s + 1], axis=0)
                                                ).then_inc(sm[f"gathered{s}"], 16)

            @block.tensor
            def _(pe):
                with pe.Fori(0, NPAIR // U) as g:
                    for s in range(U):
                        pe.wait_ge(sm[f"gathered{s}"], 16 * g + 16)
                        pe.wait_ge(sm["trip_done"], g + 1)
                        pe.transpose(TR[:, s, 0:P], xg[:, s, :], ident[:, :]).then_inc(sm["turned"], 1)
                    for s in range(U):
                        pe.wait_ge(sm["copied"], U * g + s + 1)
                        pe.wait_ge(sm[f"weights{s}"], 48 * g + 48)
                        pe.matmul(GU[:, s, 0:P], wgt[:, s, :, :].rearrange("p e i -> p (e i)"), xT[:, s, :], start=True, stop=True)
                        pe.matmul(GU[:, s, P:2 * P], wut[:, s, :, :].rearrange("p e i -> p (e i)"), xT[:, s, :], start=True,
                                  stop=True).then_inc(sm["gu_made"], 1)
                    for s in range(U):
                        pe.wait_ge(sm["hids"], U * g + s + 1)
                        pe.matmul(OU[:, s, 0:P], hm[:, s, :], wdt[:, s, :], start=True, stop=True).then_inc(sm["outs"], 1)

            @block.scalar
            def _(act):
                with act.Fori(0, NPAIR // U) as g:
                    for s in range(U):
                        act.wait_ge(sm["turned"], U * g + s + 1)
                        act.wait_ge(sm["trip_done"], g + 1)
                        act.activation(xT[:, s, :], TR[:, s, 0:P], ACT.Copy).then_inc(sm["copied"], 1)
                    for s in range(U):
                        act.wait_ge(sm["gu_made"], U * g + s + 1)
                        act.activation(gt[:, s, :], GU[:, s, 0:P], ACT.Silu).then_inc(sm["gated"], 1)

            @block.vector
            def _(dve):
                dve.sem_inc(sm["trip_done"], 1)
                dve.tensor_copy(tok[:, :], info[:, :, 0]).then_inc(sm["toks"], 1)
                dve.tensor_copy(ws[0:64, :], info[0:64, :, 1])
                dve.tensor_copy(ws[64:P, :], info[64:P, :, 2]).then_inc(sm["wss"], 1)
                dve.wait_ge(sm["toks"], 1)
                dve.wait_ge(sm["wss"], 1)
                dve.wait_ge(sm["own_in"], 16)
                with dve.Fori(0, NPAIR // U) as g:
                    dve.wait_ge(sm["trip_done"], g + 1)
                    for s in range(U):
                        dve.tensor_copy(idx[:, s:s + 1], tok[:, ds(U * g + s, 1)]).then_inc(sm["idxs"], 1)
                    for s in range(U):
                        dve.wait_ge(sm["gated"], U * g + s + 1)
                        dve.tensor_tensor(g2[:, s, :], GU[:, s, P:2 * P], gt[:, s, :], ALU.mult).then_inc(sm["ups"], 1)
                    for s in range(U):
                        dve.wait_ge(sm["ups"], U * g + s + 1)
                        dve.tensor_tensor(hm[:, s, :], g2[:, s, :], own[:, :], ALU.mult).then_inc(sm["hids"], 1)
                    for s in range(U):
                        dve.wait_ge(sm["outs"], U * g + s + 1)
                        o = dve.tensor_scalar(Eout[:, ds(U * g + s, 1), :].rearrange("p o c -> p (o c)"), OU[:, s, 0:P],
                                              ws[:, ds(U * g + s, 1)], None, ALU.mult)
                    o.then_inc(sm["trip_done"], 1)


def combine(nc, tag, X, XN, W, info, Eout):
    NPAIR = NE // 2
    with Phase(nc, tag) as ph:
        lane = ph.sb("lane", [P, T])
        R = 4
        hot = ph.sb("hot", [P, R, BLK])
        sgw, suw, sdw = ph.sb("sgw", [P, 64]), ph.sb("suw", [P, 64]), ph.sb("sdw", [64, P])
        gt, hid = ph.sb("gt", [64, BLK]), ph.sb("hid", [64, BLK])
        SG, SU, OUT = ph.ps("SG", [P, 512]), ph.ps("SU", [P, 512]), ph.ps("OUT", [P, 512])
        names = "loaded counted g_made u_made gated hids hots used out_made trip_done".split()
        sm = {n: ph.sem(n) for n in names}
        with nc.Block() as block:
            @block.sync
            def _(sp):
                for dst, n in ((sgw, "sgate"), (suw, "sup"), (sdw, "sdown")):
                    load(sp, dst[:, :], W[n], sm["loaded"])

            @block.gpsimd
            def _(pool):
                pool.iota(lane[:, :], pattern=[[1, T]], base=0, channel_multiplier=0,
                          allow_small_or_imprecise_dtypes=True).then_inc(sm["counted"], 1)

            @block.tensor
            def _(pe):
                pe.wait_ge(sm["loaded"], 48)
                with pe.Fori(0, NBLK) as g:
                    x = XN[:, ds(g * BLK, BLK)]
                    pe.wait_ge(sm["trip_done"], g + 1)
                    pe.matmul(SG[0:64, :], sgw[:, :], x, start=True, stop=True).then_inc(sm["g_made"], 1)
                    pe.matmul(SU[0:64, :], suw[:, :], x, start=True, stop=True).then_inc(sm["u_made"], 1)
                    for n in range(NPAIR):
                        pe.wait_ge(sm["hots"], NPAIR * g + n + 1)
                        pe.matmul(OUT[:, :], Eout[:, n, :], hot[:, n % R, :], start=n == 0, stop=False).then_inc(sm["used"], 1)
                    pe.wait_ge(sm["hids"], g + 1)
                    pe.matmul(OUT[:, :], sdw[:, :], hid[:, :], start=False, stop=True).then_inc(sm["out_made"], 1)

            @block.scalar
            def _(act):
                with act.Fori(0, NBLK) as g:
                    act.wait_ge(sm["g_made"], g + 1)
                    act.wait_ge(sm["trip_done"], g + 1)
                    act.activation(gt[:, :], SG[0:64, :], ACT.Silu).then_inc(sm["gated"], 1)

            @block.vector
            def _(dve):
                dve.sem_inc(sm["trip_done"], 1)
                dve.wait_ge(sm["counted"], 1)
                with dve.Fori(0, NBLK) as g:
                    at = ds(g * BLK, BLK)
                    for n in range(NPAIR):
                        if n >= R:
                            dve.wait_ge(sm["used"], NPAIR * g + n - R + 1)
                        else:
                            dve.wait_ge(sm["trip_done"], g + 1)
                        dve.tensor_scalar(hot[:, n % R, :], lane[:, at], info[:, n, 0:1], None, ALU.is_equal).then_inc(sm["hots"], 1)
                        if n == 4:
                            dve.wait_ge(sm["gated"], g + 1)
                            dve.wait_ge(sm["u_made"], g + 1)
                            dve.wait_ge(sm["trip_done"], g + 1)
                            dve.tensor_tensor(hid[:, :], SU[0:64, :], gt[:, :], ALU.mult).then_inc(sm["hids"], 1)
                    dve.wait_ge(sm["out_made"], g + 1)
                    dve.scalar_tensor_tensor(X[:, at], OUT[:, :], 0.5, X[:, at], ALU.mult, ALU.add).then_inc(sm["trip_done"], 1)


def build(nc, a, out):
    C = {n[2:]: v for n, v in a.items() if n.startswith("c_")}
    rows_dram = nc.dram_tensor("token_rows", (T, D), F32).ap()
    with ExitStack() as ctx:
        def sb(name, shape):
            return ctx.enter_context(nc.sbuf_tensor(name, shape, F32))

        X, XN = sb("X", [P, T]), sb("XN", [P, T + AHEAD])
        ident, ones_mean, eps = sb("ident", [P, P]), sb("ones_mean", [P, P]), sb("eps", [P, 1])
        with Phase(nc, "common") as ph:
            loaded = ph.sem("loaded")
            with nc.Block() as block:
                @block.sync
                def _(sp):
                    load(sp, ident[:, :], C["eye"], loaded)
                    load(sp, ones_mean[:, :], C["ones_mean"], loaded)
                    sp.wait_ge(loaded, 32)

                @block.vector
                def _(dve):
                    dve.memset(eps[:, :], LN_EPS)
                    dve.memset(XN[:, T:], 0.0)

        def norm(tag):
            layer_norm(nc, tag + "_norm", X, XN, ones_mean, eps)

        def pick(prefix, **names):
            return {k: a[prefix + v] for k, v in names.items()}

        def layer0_ffn(tag):
            norm(tag)
            product_key_experts(nc, tag, X, XN, C, pick("L0_ffn_", gamma="bn_gamma", beta="bn_beta", w_q="w_q",
                                                        keys="keys_p", down="down", up="up"), ident, eps)

        def layer1_ffn(tag):
            norm(tag)
            for n in range(2):
                w = {k: a["L1_ffn_" + k][n] for k in ("q", "k", "v", "q_crossed", "k_crossed", "qk_scale", "w1", "b1",
                                                      "w2", "b2", "ln_g", "ln_b")}
                w["o"] = a["L1_ffn_wo"][n].rearrange("(g p) d -> p g d", p=P)
                head_attention(nc, f"{tag}_att{n}", "win", XN, XN, C, w, ident)
                gated_ffn(nc, f"{tag}_ff{n}", "gelu", XN, XN, C, w, ones_mean, eps)
            add_half(nc, tag + "_add", X, XN)

        def layer2_ffn(tag):
            norm(tag)
            routed_experts(nc, tag, X, XN, C, pick("L2_ffn_", router="router_w", gate="gate_w", up="up_w", down="down_w",
                                                   sgate="shared_gate_w", sup="shared_up_w", sdown="shared_down_w"),
                           ident, rows_dram)

        def layer3_ffn(tag):
            norm(tag)
            gated_ffn(nc, tag, "int8", X, XN, C, pick("L3_ffn_", gate="w_gate", up="w_up", down="w_down"))

        enter_stream(nc, a["L0_attn_w"], X, ident)
        layer0_ffn("l0a")
        norm("l0att")
        head_attention(nc, "l0att", "rel", X, XN, C,
                       {"o": C["eye"], **pick("L0_attn_", q="Wq", k="Wk", v="Wv", r="Wr", r_crossed="Wr_crossed",
                                              u="u_bias", v_bias="v_bias")}, ident)
        layer0_ffn("l0b")
        layer1_ffn("l1a")
        norm("l1att")
        w = pick("L1_attn_", q="q", k="k", v="v", q_crossed="q_crossed", k_crossed="k_crossed", o="W_o")
        head_attention(nc, "l1att", "rope", X, XN, C, w, ident)
        layer1_ffn("l1b")
        layer2_ffn("l2a")
        norm("l2att")
        full_attention(nc, "l2att", X, XN, C, pick("L2_attn_", q="W_q", k="W_k", v="W_v", bias="bias"), ident)
        layer2_ffn("l2b")
        layer3_ffn("l3a")
        norm("l3att")
        latent_attention(nc, "l3att", X, XN, C, pick("L3_attn_", k="W_k", k_crossed="k_crossed", v="W_v", p="W_p", g="W_g",
                                                     q="latent_queries"), ident)
        layer3_ffn("l3b")
        leave_stream(nc, X, out, ident)


def laid_out(inputs):
    w = {n: np.asarray(v) for n, v in inputs.items()}
    a = {"L0_attn_w": w["L0_attn_w"]}

    def crossed(m, half):
        return m.reshape(-1, 2, half, m.shape[-1])[:, ::-1].reshape(m.shape)

    for n in ("Wq", "Wk", "Wv"):
        a["L0_attn_" + n] = w["L0_attn_" + n].T
    a["L0_attn_Wr"] = w["L0_attn_Wr"]
    a["L0_attn_Wr_crossed"] = crossed(w["L0_attn_Wr"].T, 1).T
    for n in ("u_bias", "v_bias"):
        a["L0_attn_" + n] = w["L0_attn_" + n].reshape(D, 1)
    for n in ("bn_gamma", "bn_beta", "w_q"):
        a["L0_ffn_" + n] = w["L0_ffn_" + n]
    a["L0_ffn_keys_p"] = w["L0_ffn_keys_p"].transpose(3, 2, 0, 1)
    a["L0_ffn_down"] = w["L0_ffn_down"][:1024].T
    a["L0_ffn_up"] = w["L0_ffn_up"][:1024]
    q, k, v = np.split(w["L1_attn_W_qkv"], 3, axis=0)
    a["L1_attn_q"], a["L1_attn_k"], a["L1_attn_v"] = q.T, k.T, v.T
    a["L1_attn_q_crossed"], a["L1_attn_k_crossed"] = crossed(q, 1).T, crossed(k, 1).T
    a["L1_attn_W_o"] = w["L1_attn_W_o"].T
    q, k, v = np.split(w["L1_ffn_wqkv"], 3, axis=2)
    a["L1_ffn_q"], a["L1_ffn_k"], a["L1_ffn_v"] = q, k, v
    for n, m in (("q", q), ("k", k)):
        a[f"L1_ffn_{n}_crossed"] = np.stack([crossed(x.T, 32).T for x in m])
    qs, ks = w["L1_ffn_q_scale"], w["L1_ffn_k_scale"]
    both = np.stack([qs, ks], axis=1)
    other = np.concatenate([both[:, :, 32:], both[:, :, :32]], axis=2)
    scales = np.stack([both, other], axis=1)
    a["L1_ffn_qk_scale"] = np.concatenate([scales, scales], axis=3).transpose(0, 3, 1, 2)
    for n in ("wo", "w1", "b1", "w2", "b2", "ln_g", "ln_b"):
        a["L1_ffn_" + n] = w["L1_ffn_" + n]
    for n in ("W_q", "W_k", "W_v"):
        a["L2_attn_" + n] = w["L2_attn_" + n]
    a["L2_attn_bias"] = np.stack([w["L2_attn_b_" + n] for n in "qkv"], axis=1)
    for n in ("router_w", "gate_w", "up_w", "down_w", "shared_gate_w", "shared_up_w", "shared_down_w"):
        a["L2_ffn_" + n] = w["L2_ffn_" + n]
    for n in ("W_k", "W_v", "W_p", "W_g"):
        a["L3_attn_" + n] = w["L3_attn_" + n].T
    a["L3_attn_k_crossed"] = crossed(w["L3_attn_W_k"], 1).T
    a["L3_attn_latent_queries"] = w["L3_attn_latent_queries"][0].transpose(1, 2, 0)
    for n in ("w_gate", "w_up", "w_down"):
        a["L3_ffn_" + n] = w["L3_ffn_" + n].T
    return a


def kernel(**inputs):
    import concourse.bacc as bacc
    from concourse.bass_utils import run_bass_kernel_spmd

    nc = bacc.Bacc("TRN2", target_bir_lowering=False, num_devices=1)
    arrays = {n: np.ascontiguousarray(v) for n, v in laid_out(inputs).items()}
    arrays.update({"c_" + n: v for n, v in constants().items()})
    tensors = {n: nc.dram_tensor(n, v.shape, mybir.dt.from_np(v.dtype), kind="ExternalInput").ap() for n, v in arrays.items()}
    out = nc.dram_tensor("out", (NB, L, D), F32, kind="ExternalOutput").ap()
    build(nc, tensors, out)
    r = run_bass_kernel_spmd(nc, [arrays], core_ids=[0])
    return r.results[0]["out"]
```

```python
from contextlib import ExitStack

import numpy as np

import concourse.bass as bass
from concourse import mybir

F32 = mybir.dt.float32
I32 = mybir.dt.int32
U32 = mybir.dt.uint32
ALU = mybir.AluOpType
ACT = mybir.ActivationFunctionType
AX = mybir.AxisListType.X
ds = bass.ds

P = 128
D = 128
NB = 16
L = 256
T = NB * L
AHEAD = 2 * L
NT = T // P
BLK = 512
NBLK = T // BLK
LN_EPS = 1e-5


class Phase:

    def __init__(self, nc, tag):
        self.nc, self.tag, self.sems, self.ctx = nc, tag, [], ExitStack()

    def __enter__(self):
        return self

    def sb(self, name, shape, dt=F32):
        return self.ctx.enter_context(self.nc.sbuf_tensor(f"{self.tag}_{name}", shape, dt))

    def ps(self, name, shape, dt=F32):
        return self.ctx.enter_context(self.nc.psum_tensor(f"{self.tag}_{name}", shape, dt))

    def sem(self, name):
        s = self.nc.alloc_semaphore(f"{self.tag}_{name}")
        self.sems.append(s)
        return s

    def __exit__(self, *exc):
        if exc[0] is None:
            self.nc.clear_and_free_semaphores(self.sems)
            self.nc.all_engine_barrier()
            self.ctx.close()
        return False


def constants():
    f = np.float32
    out = {}
    out["ones_mean"] = np.full((P, P), 1.0 / D, f)
    out["eye"] = np.eye(P, dtype=f)
    freq = (1.0 / 10000.0 ** (np.arange(0, D, 2, dtype=f) / f(D))).astype(f).astype(np.float64)
    j = np.arange(L, dtype=np.float64)

    def table(pos):
        a = freq[:, None] * pos[None, :]
        t = np.zeros((D, len(pos)))
        t[0::2], t[1::2] = np.sin(a), np.cos(a)
        return t.astype(f)

    out["rel_low"] = table(L - 1 + j)
    out["rel_up"] = table(j - L)
    a = freq[:, None] * j[None, :]
    turn = np.zeros((D, 2, L))
    turn[0::2, 0], turn[1::2, 0] = np.cos(a), np.cos(a)
    turn[0::2, 1], turn[1::2, 1] = np.sin(a), -np.sin(a)
    out["rel_turn"] = turn.astype(f)
    i, k = np.arange(P)[:, None], np.arange(P)[None, :]
    mask = np.zeros((P, 2, 2, P), f)
    mask[:, 0, 0], mask[:, 1, 0] = k <= i, k <= i
    mask[:, 0, 1] = (k + 1) >= i + 2
    mask[:, 1, 1] = k >= i + 2
    out["rel_mask"] = mask
    q = np.arange(P)[:, None, None] + P * np.arange(2)[None, :, None]
    kk = np.arange(L)[None, None, :]
    out["causal"] = np.where(kk <= q, 0.0, -1e30).astype(f)
    out["band"] = np.where((kk <= q) & (kk >= q - 64), 0.0, -1e30).astype(f)

    def rope8(inv):
        ang = j[None, :] * inv[:, None]
        t = np.zeros((P, 2, L))
        for c in range(P):
            m = (c % 8) // 2
            t[c, 0] = np.cos(ang[m])
            t[c, 1] = np.sin(ang[m]) * (1 if c % 2 else -1)
        return t.astype(f)

    theta = (f(10000.0) ** (np.arange(0, 8, 2, dtype=f) / f(8))).astype(f)
    out["rope8"] = rope8(1.0 / theta.astype(np.float64))
    half = np.arange(0, 64, 2, dtype=f)
    inv = (1.0 / 10000.0 ** (half / f(64))).astype(f).astype(np.float64)
    base = ((half + 0.4 * 64) / (1.4 * 64)).astype(np.float64)
    power = (j - L // 2) / 32.0
    t = np.zeros((P, 2, 2, L))
    for c in range(P):
        m = (c % 64) % 32
        sign = -1 if (c % 64) < 32 else 1
        sc = base[m] ** power
        t[c, 0, 0], t[c, 0, 1] = np.cos(j * inv[m]) * sc, np.cos(j * inv[m]) / sc
        t[c, 1, 0], t[c, 1, 1] = sign * np.sin(j * inv[m]) * sc, sign * np.sin(j * inv[m]) / sc
    out["xpos"] = t.astype(f)
    out["block64"] = np.kron(np.eye(2), np.ones((64, 64))).astype(f)
    out["tri"] = (np.arange(P)[:, None] < np.arange(P)[None, :]).astype(f)
    out["ones"] = np.ones((P, P), f)
    out["token"] = (np.arange(P, dtype=f)[:, None] + P * np.arange(NT, dtype=f)[None, :]).astype(f)
    lat = np.arange(64)
    m = np.where(lat[None, :] <= lat[:, None], 0.0, -1e30)
    out["latent_mask"] = np.concatenate([m, m], 0).astype(f)
    own = np.zeros((P, 8, P), f)
    for pair in range(8):
        for s in range(2):
            own[64 * s:64 * s + 64, pair, (2 * pair + s) * 8:(2 * pair + s) * 8 + 8] = 1
    out["own_head"] = own
    return out


def load(eng, dst, src, sem):
    return eng.dma_start(dst, src, allow_slow_non_contiguous=True).then_inc(sem, 16)


QUARTER = NT // 4


def enter_stream(nc, x, X, ident):
    with Phase(nc, "enter") as ph:
        raw = ph.sb("raw", [P, NT, D])
        turned = ph.ps("turned", [P, NBLK, BLK])
        loaded = [ph.sem(f"loaded{q}") for q in range(4)]
        turned_up = ph.sem("turned_up")
        rows = x.rearrange("b (u p) c -> p (b u) c", p=P)
        with nc.Block() as block:
            @block.sync
            def _(sp):
                for q in range(4):
                    load(sp, raw[:, q * QUARTER:(q + 1) * QUARTER, :], rows[:, q * QUARTER:(q + 1) * QUARTER, :], loaded[q])

            @block.tensor
            def _(pe):
                for n in range(NT):
                    if n % QUARTER == 0:
                        pe.wait_ge(loaded[n // QUARTER], 16)
                    o = pe.transpose(turned[:, n // 4, n % 4 * P:(n % 4 + 1) * P], raw[:, n, :], ident[:, :])
                    if n % 4 == 3:
                        o.then_inc(turned_up, 1)

            @block.vector
            def _(dve):
                for n in range(0, NBLK, 2):
                    dve.wait_ge(turned_up, n + 1)
                    dve.tensor_copy(X[:, n * BLK:(n + 1) * BLK], turned[:, n, :])

            @block.scalar
            def _(act):
                for n in range(1, NBLK, 2):
                    act.wait_ge(turned_up, n + 1)
                    act.activation(X[:, n * BLK:(n + 1) * BLK], turned[:, n, :], ACT.Copy)


def leave_stream(nc, X, out, ident):
    with Phase(nc, "leave") as ph:
        rows = ph.sb("rows", [P, NT, D])
        turned = ph.ps("turned", [P, NBLK, BLK])
        turned_up, stored_even, stored_odd, written = (
            ph.sem(n) for n in ("turned_up", "stored_even", "stored_odd", "written"))
        out_rows = out.rearrange("b (u p) c -> p (b u) c", p=P)
        with nc.Block() as block:
            @block.tensor
            def _(pe):
                for n in range(NT):
                    o = pe.transpose(turned[:, n // 4, n % 4 * P:(n % 4 + 1) * P], X[:, n * P:(n + 1) * P], ident[:, :])
                    if n % 4 == 3:
                        o.then_inc(turned_up, 1)

            @block.vector
            def _(dve):
                for n in range(0, NBLK, 2):
                    dve.wait_ge(turned_up, n + 1)
                    dve.tensor_copy(rows[:, 4 * n:4 * n + 4, :].rearrange("p n c -> p (n c)"), turned[:, n, :]).then_inc(stored_even, 1)

            @block.scalar
            def _(act):
                for n in range(1, NBLK, 2):
                    act.wait_ge(turned_up, n + 1)
                    act.activation(rows[:, 4 * n:4 * n + 4, :].rearrange("p n c -> p (n c)"), turned[:, n, :],
                                   ACT.Copy).then_inc(stored_odd, 1)

            @block.sync
            def _(sp):
                for q in range(4):
                    sp.wait_ge(stored_even, q + 1)
                    sp.wait_ge(stored_odd, q + 1)
                    sp.dma_start(out_rows[:, q * QUARTER:(q + 1) * QUARTER, :],
                                 rows[:, q * QUARTER:(q + 1) * QUARTER, :]).then_inc(written, 16)
                sp.wait_ge(written, 4 * 16)


def layer_norm(nc, tag, X, XN, ones_mean, eps, learned=None):
    with Phase(nc, tag) as ph:
        stat = ph.ps("stat", [P, NBLK, BLK])
        dev, sq, log, inv = (ph.sb(n, [P, NBLK, BLK]) for n in ("dev", "sq", "log", "inv"))
        means, devs, squares, vars_, logs, invs = (ph.sem(n) for n in ("means", "devs", "squares", "vars", "logs", "invs"))
        at = [slice(s * BLK, (s + 1) * BLK) for s in range(NBLK)]
        if learned:
            hs = ph.sb("hs", [P, T])
            lg, lb = ph.sb("lg", [P, 1]), ph.sb("lb", [P, 1])
            loaded, zeroed, shifted, scaled = (ph.sem(n) for n in ("loaded", "zeroed", "shifted", "scaled"))
        src = hs if learned else X
        by_sequence = (lambda ap: ap.rearrange("p (q l) -> p q l", l=L))
        with nc.Block() as block:
            if learned:
                @block.sync
                def _(sp):
                    for dst, w in zip((lg, lb), learned):
                        load(sp, dst[:, :], w.rearrange("(p c) -> p c", c=1), loaded)

                @block.gpsimd
                def _(pool):
                    pool.memset(by_sequence(hs[64:P, :])[:, :, 0:1], 0.0).then_inc(zeroed, 1)

            @block.tensor
            def _(pe):
                if learned:
                    pe.wait_ge(zeroed, 1)
                for s in range(NBLK):
                    if learned:
                        pe.wait_ge(shifted, s + 1)
                    pe.matmul(stat[:, s, :], ones_mean[:, :], src[:, at[s]], start=True, stop=True).then_inc(means, 1)
                for s in range(NBLK):
                    pe.wait_ge(squares, s + 1)
                    pe.matmul(stat[:, s, :], ones_mean[:, :], sq[:, s, :], start=True, stop=True).then_inc(vars_, 1)

            @block.vector
            def _(dve):
                if learned:
                    for s in range(NBLK):
                        dve.tensor_copy(hs[0:64, at[s]], X[0:64, at[s]])
                        dve.tensor_copy(by_sequence(hs[64:P, at[s]])[:, :, 1:L],
                                        by_sequence(X[64:P, at[s]])[:, :, 0:L - 1]).then_inc(shifted, 1)
                    dve.wait_ge(shifted, NBLK)
                    dve.wait_ge(zeroed, 1)
                    dve.wait_ge(loaded, 32)
                for s in range(NBLK):
                    dve.wait_ge(means, s + 1)
                    dve.tensor_tensor(dev[:, s, :], src[:, at[s]], stat[:, s, :], ALU.subtract).then_inc(devs, 1)
                dve.wait_ge(devs, NBLK)
                for s in range(NBLK):
                    dve.wait_ge(invs, s + 1)
                    if learned:
                        dve.scalar_tensor_tensor(sq[:, s, :], dev[:, s, :], lg[:, 0:1], inv[:, s, :], ALU.mult,
                                                 ALU.mult).then_inc(scaled, 1)
                    else:
                        dve.tensor_tensor(XN[:, at[s]], dev[:, s, :], inv[:, s, :], ALU.mult)

            @block.scalar
            def _(act):
                for s in range(NBLK):
                    act.wait_ge(devs, s + 1)
                    act.activation(sq[:, s, :], dev[:, s, :], ACT.Square).then_inc(squares, 1)
                for half in range(2):
                    part = range(half * NBLK // 2, (half + 1) * NBLK // 2)
                    for s in part:
                        act.wait_ge(vars_, s + 1)
                        act.activation(log[:, s, :], stat[:, s, :], ACT.Ln, bias=eps[:, 0:1]).then_inc(logs, 1)
                    for s in part:
                        act.wait_ge(logs, s + 1)
                        act.activation(inv[:, s, :], log[:, s, :], ACT.Exp, scale=-0.5).then_inc(invs, 1)
                if learned:
                    act.wait_ge(loaded, 32)
                    for s in range(NBLK):
                        act.wait_ge(scaled, s + 1)
                        act.activation(XN[:, at[s]], sq[:, s, :], ACT.Identity, bias=lb[:, 0:1])
def full_attention(nc, tag, R, XN, A, W, ident):
    scale = D ** -0.5
    with Phase(nc, tag) as ph:
        xs = ph.sb("xs", [P, L])
        qT, kT = ph.sb("qT", [P, L]), ph.sb("kT", [P, L])
        V = ph.sb("V", [P, 2, D])
        S, E = ph.sb("S", [P, 2, L]), ph.sb("E", [P, 2, L])
        ET = ph.sb("ET", [P, 2, 2, P])
        least, total, share = (ph.sb(n, [P, 2]) for n in ("least", "total", "share"))
        zeros = ph.sb("zeros", [P, L])
        wq, wk, wv = (ph.sb(n, [P, D]) for n in ("wq", "wk", "wv"))
        bias = ph.sb("bias", [P, 3])
        PJ, VP = ph.ps("PJ", [P, 512]), ph.ps("VP", [P, 512])
        SC, TU = ph.ps("SC", [P, 2, 512]), ph.ps("TU", [P, 2, 512])
        OT = ph.ps("OT", [P, 2, 512])
        names = ("loaded cleared staged projected v_made v_copied qk_ready scored shifted exped summed shared turned "
                 "turned_copied valued trip_done passed").split()
        sm = {n: ph.sem(n) for n in names}
        with nc.Block() as block:
            @block.sync
            def _(sp):
                load(sp, wq[:, :], W["q"], sm["loaded"])
                load(sp, wk[:, :], W["k"], sm["loaded"])
                load(sp, wv[:, :], W["v"], sm["loaded"])
                load(sp, bias[:, :], W["bias"], sm["loaded"])

            @block.gpsimd
            def _(pool):
                pool.memset(zeros[:, :], 0.0).then_inc(sm["cleared"], 1)

            @block.tensor
            def _(pe):
                pe.wait_ge(sm["loaded"], 64)
                with pe.Fori(0, NB) as b:
                    pe.wait_ge(sm["trip_done"], b + 1)
                    pe.wait_ge(sm["staged"], b + 1)
                    pe.matmul(PJ[:, 0:L], wq[:, :], xs[:, :], start=True, stop=True)
                    pe.matmul(PJ[:, L:2 * L], wk[:, :], xs[:, :], start=True, stop=True).then_inc(sm["projected"], 1)
                    for t in range(2):
                        o = pe.matmul(VP[:, t * P:(t + 1) * P], xs[:, t * P:(t + 1) * P], wv[:, :], start=True, stop=True)
                    o.then_inc(sm["v_made"], 1)
                    pe.wait_ge(sm["qk_ready"], b + 1)
                    for t in range(2):
                        pe.matmul(SC[:, t, 0:L], qT[:, t * P:(t + 1) * P], kT[:, :], start=True, stop=True).then_inc(sm["scored"], 1)
                    for t in range(2):
                        pe.wait_ge(sm["shared"], 2 * b + t + 1)
                        for c in range(2):
                            o = pe.transpose(TU[:, t, c * P:(c + 1) * P], E[:, t, c * P:(c + 1) * P], ident[:, :])
                        o.then_inc(sm["turned"], 1)
                    pe.wait_ge(sm["v_copied"], b + 1)
                    for t in range(2):
                        pe.wait_ge(sm["turned_copied"], 2 * b + t + 1)
                        for c in range(2):
                            o = pe.matmul(OT[:, t, 0:P], V[:, c, :], ET[:, t, c, :], start=c == 0, stop=c == 1)
                        o.then_inc(sm["valued"], 1)

            @block.scalar
            def _(act):
                act.wait_ge(sm["loaded"], 64)
                with act.Fori(0, NB) as b:
                    act.wait_ge(sm["trip_done"], b + 1)
                    act.wait_ge(sm["projected"], b + 1)
                    act.activation(qT[:, :], PJ[:, 0:L], ACT.Identity, bias=bias[:, 0:1])
                    act.activation(kT[:, :], PJ[:, L:2 * L], ACT.Identity, bias=bias[:, 1:2]).then_inc(sm["qk_ready"], 1)
                    act.wait_ge(sm["v_made"], b + 1)
                    act.activation(V[:, :, :], VP[:, 0:L].rearrange("p (t c) -> p t c", t=2), ACT.Copy).then_inc(sm["v_copied"], 1)
                    for t in range(2):
                        act.wait_ge(sm["shifted"], 2 * b + t + 1)
                        act.activation(E[:, t, :], S[:, t, :], ACT.Exp, bias=least[:, t:t + 1], scale=-1.0,
                                       accum_out=total[:, t:t + 1]).then_inc(sm["exped"], 1)
                    for t in range(2):
                        act.wait_ge(sm["turned"], 2 * b + t + 1)
                        act.activation(ET[:, t, :, :], TU[:, t, 0:L].rearrange("p (c q) -> p c q", c=2),
                                       ACT.Copy).then_inc(sm["turned_copied"], 1)

            @block.vector
            def _(dve):
                dve.sem_inc(sm["trip_done"], 1)
                dve.wait_ge(sm["loaded"], 64)
                dve.wait_ge(sm["cleared"], 1)
                with dve.Fori(0, NB) as b:
                    seq = ds(b * L, L)
                    dve.wait_ge(sm["trip_done"], b + 1)
                    dve.tensor_copy(xs[:, :], XN[:, seq]).then_inc(sm["staged"], 1)
                    for t in range(2):
                        dve.wait_ge(sm["scored"], 2 * b + t + 1)
                        dve.sem_inc(sm["passed"], 1)
                        dve.tensor_tensor_reduce(S[:, t, :], SC[:, t, 0:L], zeros[:, :], -scale, 3e38, ALU.add, ALU.min,
                                                 least[:, t:t + 1]).then_inc(sm["shifted"], 1)
                    for t in range(2):
                        dve.wait_ge(sm["exped"], 2 * b + t + 1)
                        dve.reciprocal(share[:, t:t + 1], total[:, t:t + 1]).then_inc(sm["summed"], 1)
                        dve.wait_ge(sm["summed"], 2 * b + t + 1)
                        dve.tensor_scalar(E[:, t, :], E[:, t, :], share[:, t:t + 1], None, ALU.mult).then_inc(sm["shared"], 1)
                    dve.wait_ge(sm["valued"], 2 * b + 2)
                    at = R[:, seq].rearrange("p (t q) -> p t q", t=2)
                    dve.scalar_tensor_tensor(at, OT[:, :, 0:P], bias[:, 2:3], at, ALU.add, ALU.add).then_inc(sm["trip_done"], 1)


HEADS = {"rel": 16, "rope": 16, "win": 8}
WIDTH = {"rel": 8, "rope": 8, "win": 64}
STRIP = 64
OUT_STRIP = {"rel": 32, "rope": 32, "win": 64}
PART_OF_Q = (0, 0, 1, 0, 2, 1, 1, 2)
PART_OF_K = (0, 1, 0, 2, 0, 1, 2, 1)
SCALE = {"rel": 8 ** -0.5, "rope": 8 ** -0.5, "win": 8.0}
TURN_BANKS = {"rel": 1, "rope": 2, "win": 1}
SHIFT_LAG = {"rel": 1, "rope": 0, "win": 0}
EXP_LAG = {"rel": 2, "rope": 0, "win": 0}
SHARE_LAG = {"rel": 4, "rope": 2, "win": 2}
TURN_LAG = {"rel": 6, "rope": 4, "win": 5}
VALUE_LAG = {"rel": 9, "rope": 6, "win": 7}
FINAL_STEP = {"rel": 10, "rope": 9, "win": 9}
START = 14


def head_attention(nc, tag, kind, R, XN, A, W, ident):
    nh, width, strip, ostrip, scale = HEADS[kind], WIDTH[kind], STRIP, OUT_STRIP[kind], SCALE[kind]
    G, GO = nh * strip // P, nh * ostrip // P
    VW = nh * width
    NU = 2 * nh
    small = width == 8
    BF = mybir.dt.bfloat16
    keys = (lambda t: L) if kind == "rel" else (lambda t: P * (t + 1))
    NSC, NTU = 2, TURN_BANKS[kind]
    RS, RE, RT = 4, 8, 4
    turn_lag, value_lag, exp_lag, shift_lag = TURN_LAG[kind], VALUE_LAG[kind], EXP_LAG[kind], SHIFT_LAG[kind]
    share_lag = SHARE_LAG[kind]
    with Phase(nc, tag) as ph:
        xs = ph.sb("xs", [P, L])
        QK = ph.sb("QK", [P, 2, G, 2, L], BF if small else F32)
        V = ph.sb("V", [P, 2, 2, VW])
        S, E = ph.sb("S", [P, RS, L]), ph.sb("E", [P, RE, L])
        ET = ph.sb("ET", [P, RT, 2, P])
        least, total, share = (ph.sb(n, [P, 2 * NU]) for n in ("least", "total", "share"))
        oT = ph.sb("oT", [P, GO, L])
        PJ = ph.ps("PJ", [P, 2, 512])
        SC = ph.ps("SC", [P, NSC, 512])
        TU = ph.ps("TU", [P, NTU, 512])
        OT = ph.ps("OT", [P, 2, 512])
        wq, wk, wv = (ph.sb(n, [P, VW]) for n in ("wq", "wk", "wv"))
        wo = ph.sb("wo", [P, GO, D])
        if kind in ("rope", "win"):
            mask = ph.sb("mask", [P, 2, L])
            wqx, wkx = ph.sb("wqx", [P, VW]), ph.sb("wkx", [P, VW])
        if small:
            spread = ph.sb("spread", [P, 2, 3, G, 2, 8, 8], BF)
            qk, rest1, rest2 = (ph.sb(n, [P, 2, L]) for n in ("qk", "rest1", "rest2"))
            part = ph.sb("part", [P, 3, 2, L], BF)
        if kind == "rope":
            rt = ph.sb("rt", [P, 2, L])
            parts = ph.sb("parts", [P, 2, 2, L])
        if kind == "rel":
            qv = ph.sb("qv", [P, 2, L])
            TP = ph.ps("TP", [P, 512])
            ub, vb = ph.sb("ub", [P, 1]), ph.sb("vb", [P, 1])
            wr = ph.sb("wr", [P, nh, 2, P])
            turn = ph.sb("turn", [P, 2, L])
            low, up = ph.sb("low", [P, L]), ph.sb("up", [P, L])
            rmask = ph.sb("rmask", [P, 2, 2, P])
            tparts = ph.sb("tparts", [P, 2, 2, L])
            Ah = ph.sb("Ah", [P, 2, L + 1])
            lu = ph.sb("lu", [P, 2, 2 * P + 4])
            bd = ph.sb("bd", [P, 2, L])
        if kind == "win":
            tab = ph.sb("tab", [P, 2, 2, L])
            qs = ph.sb("qs", [P, 2, 2])
            b64 = ph.sb("b64", [P, P])
            NORM = ph.ps("NORM", [P, 512])
            sq, m1, m2 = (ph.sb(n, [P, 2 * L]) for n in ("sq", "m1", "m2"))
            clipped, log, inv, m3 = (ph.sb(n, [P, G, 2 * L]) for n in ("clipped", "log", "inv", "m3"))
            back = ph.sb("back", [P, 1])

        names = ("loaded cleared prepared staged projected v_made v_copied spread_made strips_copied scored "
                 "shifted exped turned turned_copied valued summed shared o_copied final added o_zeroed "
                 "qk_ready split parts_made a_made a_parts a_ready masked bd_ready squares norms logs clips invs "
                 "m1_made m3_made passed back_set").split()
        sm = {n: ph.sem(n) for n in names}
        n_loads = [0]

        def ld(eng, dst, src):
            n_loads[0] += 1
            load(eng, dst, src, sm["loaded"])

        def steps(eng, prepare, body):
            for s in range(NU):
                prepare(0, 0, s)
            for j in range(START):
                body(0, j)
            with eng.Fori(0, NB // 2) as g:
                for j in range(START, 2 * NU + START):
                    body(g, j)

        def ahead(g, j):
            return 2 * g + j // NU + 1, (j // NU + 1) % 2, j % NU

        def behind(g, j):
            return 2 * g + j // NU - 1, (j // NU - 1) % 2, j % NU

        def units(g, j):
            return 2 * NU * g + j

        first_spread = 20 if kind == "rel" else 23

        with nc.Block() as block:
            @block.sync
            def _(sp):
                ld(sp, wq[:, :], W["q"])
                ld(sp, wk[:, :], W["k"])
                ld(sp, wv[:, :], W["v"])
                if kind == "rel":
                    ld(sp, ub[:, :], W["u"])
                    ld(sp, vb[:, :], W["v_bias"])
                    ld(sp, turn[:, :, :], A["rel_turn"])
                    ld(sp, low[:, :], A["rel_low"])
                    ld(sp, up[:, :], A["rel_up"])
                    ld(sp, rmask[:, :, :, :], A["rel_mask"])
                    sp.wait_ge(sm["cleared"], 1)
                    for h in range(nh):
                        ld(sp, wr[8 * h:8 * h + 8, h, 0, :], W["r"][8 * h:8 * h + 8, :])
                        ld(sp, wr[8 * h:8 * h + 8, h, 1, :], W["r_crossed"][8 * h:8 * h + 8, :])
                else:
                    ld(sp, wqx[:, :], W["q_crossed"])
                    ld(sp, wkx[:, :], W["k_crossed"])
                    ld(sp, mask[:, :, :], A[{"rope": "causal", "win": "band"}[kind]])
                if kind == "rope":
                    ld(sp, rt[:, :, :], A["rope8"])
                if small:
                    sp.wait_ge(sm["cleared"], 2 if kind == "rel" else 1)
                    for r in range(4):
                        for gr in range(GO):
                            ld(sp, wo[32 * r:32 * r + 8, gr, :], W["o"][(4 * gr + r) * 8:(4 * gr + r) * 8 + 8, :])
                if kind == "win":
                    ld(sp, wo[:, :, :], W["o"])
                    ld(sp, qs[:, :, :], W["qk_scale"])
                    ld(sp, tab[:, :, :, :], A["xpos"])
                    ld(sp, b64[:, :], A["block64"])

            loads = 16 * n_loads[0]

            @block.gpsimd
            def _(pool):
                if kind == "rel":
                    pool.memset(wr[:, :, :, :], 0.0).then_inc(sm["cleared"], 1)
                    pool.memset(lu[:, :, :], 0.0).then_inc(sm["prepared"], 1)
                    pool.memset(bd[:, :, :], 0.0).then_inc(sm["prepared"], 1)
                    pool.memset(Ah[:, :, :], 0.0).then_inc(sm["prepared"], 1)
                if small:
                    pool.memset(wo[:, :, :], 0.0).then_inc(sm["cleared"], 1)
                    pool.memset(spread[:, :, :, :, :, :, :].rearrange("p w k g r c d -> p (w k g r c d)"),
                                0.0).then_inc(sm["prepared"], 1)
                    pool.wait_ge(sm["prepared"], 4 if kind == "rel" else 1)
                    for w, parts_of in enumerate((PART_OF_Q, PART_OF_K)):
                        for c in range(8):
                            o = pool.tensor_copy(spread[:, w, parts_of[c], :, :, c, :],
                                                 ident[:, :].rearrange("p (g r d) -> p g r d", g=G, r=2))
                    o.then_inc(sm["prepared"], 1)
                else:
                    pool.memset(xs[:, :], 0.0).then_inc(sm["cleared"], 1)
                    pool.memset(back[:, :], 10.0 * float(np.log(2.0))).then_inc(sm["back_set"], 1)
                    pool.wait_ge(sm["loaded"], loads)
                    pool.wait_ge(sm["cleared"], 1)
                    for d in range(2):
                        for w in range(2):
                            pool.tensor_scalar(tab[:, d, w, :], tab[:, d, w, :], qs[:, d, w:w + 1], None,
                                               ALU.mult).then_inc(sm["prepared"], 1)
                    pool.wait_ge(sm["prepared"], 4)

                def stage(q):
                    if not isinstance(q, int) or q > 0:
                        pool.wait_ge(sm["v_made"], q)
                        pool.sem_inc(sm["passed"], 1)
                    pool.tensor_copy(xs[:, :], XN[:, ds(q * L, L)]).then_inc(sm["staged"], 1)

                def sum_a(H, n):
                    pool.wait_ge(sm["a_parts"], n + H + 1)
                    if H >= 2:
                        pool.wait_ge(sm["scored"], 2 * (n + H - 1))
                    pool.tensor_tensor(Ah[:, H % 2, 0:L], tparts[:, H % 2, 0, :], tparts[:, H % 2, 1, :],
                                       ALU.add).then_inc(sm["a_ready"], 1)

                def split(q):
                    n = 5 * q
                    pool.wait_ge(sm["qk_ready"], q + 1)
                    if not isinstance(q, int) or q > 0:
                        pool.wait_ge(sm["spread_made"], G * q)
                    pool.sem_inc(sm["passed"], 1)
                    pool.tensor_copy(part[:, 0, :, :], qk[:, :, :]).then_inc(sm["split"], 1)
                    pool.wait_ge(sm["split"], n + 1)
                    pool.tensor_tensor(rest1[:, :, :], qk[:, :, :], part[:, 0, :, :], ALU.subtract).then_inc(sm["split"], 1)
                    pool.wait_ge(sm["split"], n + 2)
                    pool.sem_inc(sm["passed"], 1)
                    pool.tensor_copy(part[:, 1, :, :], rest1[:, :, :]).then_inc(sm["split"], 1)
                    pool.wait_ge(sm["split"], n + 3)
                    pool.tensor_tensor(rest2[:, :, :], rest1[:, :, :], part[:, 1, :, :], ALU.subtract).then_inc(sm["split"], 1)
                    pool.wait_ge(sm["split"], n + 4)
                    pool.sem_inc(sm["passed"], 1)
                    pool.tensor_copy(part[:, 2, :, :], rest2[:, :, :]).then_inc(sm["split"], 1)

                def prepare(q, parity, s):
                    if small and s == 11:
                        stage(q)
                    if kind == "rope" and s == 14:
                        pool.wait_ge(sm["parts_made"], 2 * q + 2)
                        pool.tensor_tensor(qk[:, :, :], parts[:, 0, :, :], parts[:, 1, :, :], ALU.add).then_inc(sm["qk_ready"], 1)
                        split(q)

                def rel_step(g, j):
                    n, t = units(g, j), j % 2
                    pool.wait_ge(sm["masked"], n + 1)
                    if j >= 2:
                        pool.wait_ge(sm["shifted"], n - 1)
                    if t == 0:
                        pool.tensor_tensor(bd[:, 0, 0:P + 1], lu[:, 0, 0:P + 1], lu[:, 0, P + 1:2 * P + 2],
                                           ALU.add).then_inc(sm["bd_ready"], 1)
                    else:
                        pool.tensor_tensor(bd[:, 1, P:L], lu[:, 1, 0:P], lu[:, 1, P + 2:2 * P + 2],
                                           ALU.add).then_inc(sm["bd_ready"], 1)
                    if j % 2 == 0:
                        sum_a(j // 2 + 1, 2 * nh * g)

                def win_sequence(q, parity):
                    for c in range(G):
                        pool.wait_ge(sm["m1_made"], G * q + c + 1)
                        pool.tensor_tensor(m3[:, c, :], m1[:, :], m2[:, :], ALU.add).then_inc(sm["m3_made"], 1)
                    for c in range(G):
                        pool.wait_ge(sm["m3_made"], G * q + c + 1)
                        pool.wait_ge(sm["invs"], G * q + c + 1)
                        pool.tensor_tensor(QK[:, parity, c, :, :].rearrange("p w n -> p (w n)"), m3[:, c, :], inv[:, c, :],
                                           ALU.mult).then_inc(sm["strips_copied"], 1)

                def body(g, j):
                    if kind == "rel":
                        rel_step(g, j)
                    prepare(*ahead(g, j))

                if kind == "win":
                    win_sequence(0, 0)
                    win_sequence(1, 1)
                    with pool.Fori(0, NB // 2) as g:
                        win_sequence(2 * g + 2, 0)
                        win_sequence(2 * g + 3, 1)
                else:
                    for s in range(NU):
                        prepare(0, 0, s)
                    if kind == "rel":
                        sum_a(0, 0)
                    for j in range(START):
                        body(0, j)
                    with pool.Fori(0, NB // 2) as g:
                        for j in range(START, 2 * NU + START):
                            body(g, j)

            @block.tensor
            def _(pe):
                pe.wait_ge(sm["loaded"], loads)
                if small:
                    pe.wait_ge(sm["prepared"], 5 if kind == "rel" else 2)
                    pe.wait_ge(sm["o_zeroed"], 1)

                def prepare(q, parity, s):
                    later = not isinstance(q, int) or q > 0
                    if small:
                        if s == 12:
                            pe.wait_ge(sm["staged"], q + 1)
                            if later:
                                pe.wait_ge(sm["added"], q)
                                pe.wait_ge(sm["strips_copied"], G * q)
                            pe.matmul(PJ[:, 0, 0:L], wq[:, :], xs[:, :], start=True, stop=True)
                            last = pe.matmul(PJ[:, 0, L:2 * L], wk[:, :], xs[:, :], start=True, stop=True)
                            if kind == "rope":
                                pe.matmul(PJ[:, 1, 0:L], wqx[:, :], xs[:, :], start=True, stop=True)
                                last = pe.matmul(PJ[:, 1, L:2 * L], wkx[:, :], xs[:, :], start=True, stop=True)
                            last.then_inc(sm["projected"], 1)
                        if s == 16:
                            pe.wait_ge(sm["qk_ready"], q + 1)
                            for t in range(2):
                                last = pe.matmul(PJ[:, 0, t * P:(t + 1) * P], xs[:, t * P:(t + 1) * P], wv[:, :],
                                                 start=True, stop=True)
                            last.then_inc(sm["v_made"], 1)
                        gr = s - first_spread
                        if 0 <= gr < G:
                            if gr == 0:
                                pe.wait_ge(sm["v_copied"], q + 1)
                                pe.wait_ge(sm["split"], 5 * q + 5)
                            elif gr >= 2:
                                pe.wait_ge(sm["strips_copied"], G * q + gr - 1)
                            for w in range(2):
                                for n in range(3):
                                    last = pe.matmul(PJ[:, gr % 2, w * L:(w + 1) * L], spread[:, w, n, gr, :, :, :],
                                                     part[:, n, w, :], start=n == 0, stop=n == 2)
                            last.then_inc(sm["spread_made"], 1)
                        return
                    c, cols = s // 2, slice(s // 2 * P, (s // 2 + 1) * P)
                    if s % 2 == 0 and c < G:
                        if c == 0:
                            pe.wait_ge(sm["staged"], q + 1)
                            if later:
                                pe.wait_ge(sm["v_copied"], q)
                            if not isinstance(q, int):
                                pe.wait_ge(sm["added"], q - 1)
                        else:
                            pe.wait_ge(sm["m1_made"], G * q + c)
                        pe.matmul(PJ[:, 0, 0:L], wq[:, cols], xs[:, :], start=True, stop=True)
                        pe.matmul(PJ[:, 0, L:2 * L], wk[:, cols], xs[:, :], start=True, stop=True)
                        pe.matmul(PJ[:, 1, 0:L], wqx[:, cols], xs[:, :], start=True, stop=True)
                        pe.matmul(PJ[:, 1, L:2 * L], wkx[:, cols], xs[:, :], start=True,
                                  stop=True).then_inc(sm["projected"], 1)
                    if s % 2 == 1 and c < G:
                        pe.wait_ge(sm["squares"], G * q + c + 1)
                        if later or c > 0:
                            pe.wait_ge(sm["clips"], G * q + c)
                        pe.matmul(NORM[:, :], b64[:, :], sq[:, :], start=True, stop=True).then_inc(sm["norms"], 1)
                    if s == 8:
                        pe.wait_ge(sm["m1_made"], G * q + G)
                        for t in range(2):
                            last = pe.matmul(PJ[:, t, 0:VW], xs[:, t * P:(t + 1) * P], wv[:, :], start=True, stop=True)
                        last.then_inc(sm["v_made"], 1)

                def epilogue(e, parity, s):
                    if s == FINAL_STEP[kind]:
                        pe.wait_ge(sm["o_copied"], 2 * e + 2)
                        if kind == "win":
                            pe.wait_ge(sm["v_copied"], e + 3)
                        for gr in range(GO):
                            last = pe.matmul(PJ[:, 0, 0:L], wo[:, gr, :], oT[:, gr, :], start=gr == 0, stop=gr == GO - 1)
                        last.then_inc(sm["final"], 1)

                def make_a(H, n):
                    if H >= 1:
                        pe.wait_ge(sm["a_parts"], n + H)
                    for x in range(2):
                        last = pe.matmul(TP[:, x * L:(x + 1) * L], wr[:, H % nh, x, :], qv[:, H // nh % 2, :],
                                         start=True, stop=True)
                    last.then_inc(sm["a_made"], 1)

                def score(g, j):
                    u, parity, n = j % NU, j // NU % 2, units(g, j)
                    h, t = u // 2, u % 2
                    gr, row = h * strip // P, h * strip % P
                    rows = slice(row, row + strip)
                    if u == 0:
                        pe.wait_ge(sm["v_copied"], 2 * g + j // NU + 1)
                    if t == 0 and row == 0:
                        pe.wait_ge(sm["strips_copied"], G * (2 * g + j // NU) + gr + 1)
                    if j >= NSC:
                        pe.wait_ge(sm["shifted"], n - NSC + 1)
                    nk = keys(t)
                    sc = SC[:, j % NSC, :]
                    last = pe.matmul(sc[:, 0:nk], QK[rows, parity, gr, 0, t * P:(t + 1) * P], QK[rows, parity, gr, 1, 0:nk],
                                     start=True, stop=kind != "rel", skip_group_check=kind == "rel")
                    if kind == "rel":
                        pe.wait_ge(sm["a_ready"], 2 * nh * g + j // 2 + 1)
                        a0 = Ah[:, h % 2, t * P:(t + 1) * P]
                        a1 = Ah[:, h % 2, t * P + 1:(t + 1) * P + 1]
                        if t == 0:
                            pe.matmul(sc[:, P + 1:L], a1, up[:, P + 1:L], start=False, stop=True, skip_group_check=True)
                            pe.matmul(sc[:, L:L + P], a0, low[:, 0:P], start=False, stop=True, skip_group_check=True)
                            last = pe.matmul(sc[:, L + P:2 * L], a1, up[:, 1:P + 1], start=False, stop=True,
                                             skip_group_check=True)
                        else:
                            pe.matmul(sc[:, 0:P], a0, low[:, 0:P], start=False, stop=True, skip_group_check=True)
                            pe.matmul(sc[:, L:L + P], a0, low[:, P:L], start=False, stop=True, skip_group_check=True)
                            last = pe.matmul(sc[:, L + P:2 * L], a1, up[:, P:L], start=False, stop=True,
                                             skip_group_check=True)
                    last.then_inc(sm["scored"], 1)

                def turn_up(g, j):
                    n = units(g, j)
                    pe.wait_ge(sm["shared"], n + 1)
                    if j >= NTU:
                        pe.wait_ge(sm["turned_copied"], n - NTU + 1)
                    for c in range(keys(j % 2) // P):
                        last = pe.transpose(TU[:, j % NTU, c * P:(c + 1) * P], E[:, j % RE, c * P:(c + 1) * P], ident[:, :])
                    last.then_inc(sm["turned"], 1)

                def value(g, j):
                    u, seq = j % NU, j // NU
                    h, t = u // 2, u % 2
                    gr, row = h * ostrip // P, h * ostrip % P
                    if j >= NU and u % (NU // 2) == 0:
                        pe.wait_ge(sm["o_copied"], 2 * (2 * g + seq - 1) + u // (NU // 2) + 1)
                    pe.wait_ge(sm["turned_copied"], units(g, j) + 1)
                    nk = keys(t) // P
                    at = gr % 2 * L + t * P
                    for c in range(nk):
                        last = pe.matmul(OT[row:row + width, gr // 2, at:at + P],
                                         V[:, seq % 2, c, h * width:(h + 1) * width], ET[:, j % RT, c, :],
                                         start=c == 0, stop=c == nk - 1)
                    last.then_inc(sm["valued"], 1)

                def body(g, j):
                    if kind == "rel" and j % 2 == 0:
                        make_a(j // 2 + 1, 2 * nh * g)
                    score(g, j)
                    if j >= turn_lag:
                        turn_up(g, j - turn_lag)
                    if j >= value_lag:
                        value(g, j - value_lag)
                    prepare(*ahead(g, j))
                    if j >= NU:
                        epilogue(*behind(g, j))

                for s in range(NU):
                    prepare(0, 0, s)
                if kind == "rel":
                    make_a(0, 0)
                for j in range(START):
                    body(0, j)
                with pe.Fori(0, NB // 2) as g:
                    for j in range(START, 2 * NU + START):
                        body(g, j)

            @block.scalar
            def _(act):
                act.wait_ge(sm["loaded"], loads)
                if kind == "win":
                    act.wait_ge(sm["back_set"], 1)

                def prepare(q, parity, s):
                    if small:
                        if s == 17:
                            act.wait_ge(sm["v_made"], q + 1)
                            act.activation(V[:, parity, :, :], PJ[:, 0, 0:L].rearrange("p (t c) -> p t c", t=2),
                                           ACT.Copy).then_inc(sm["v_copied"], 1)
                        gr = s - first_spread - 1
                        if 0 <= gr < G:
                            act.wait_ge(sm["spread_made"], G * q + gr + 1)
                            act.activation(QK[:, parity, gr, :, :], PJ[:, gr % 2, :].rearrange("p (w n) -> p w n", w=2),
                                           ACT.Copy).then_inc(sm["strips_copied"], 1)
                        return
                    c = s // 2
                    if s % 2 == 1 and c < G:
                        act.wait_ge(sm["projected"], G * q + c + 1)
                        act.activation(sq[:, :], PJ[:, 0, :], ACT.Square).then_inc(sm["squares"], 1)
                    if s == 9:
                        if not isinstance(q, int) or q > 0:
                            act.wait_ge(sm["strips_copied"], G * q)
                        act.wait_ge(sm["clips"], G * q + G)
                        act.activation(log[:, :, :], clipped[:, :, :], ACT.Ln, scale=2.0 ** 20).then_inc(sm["logs"], 1)
                    if 10 <= s < 10 + G:
                        c = s - 10
                        act.wait_ge(sm["logs"], q + 1)
                        act.activation(inv[:, c, :], log[:, c, :], ACT.Exp, scale=-0.5, bias=back[:, 0:1]).then_inc(sm["invs"], 1)

                def copy_output(e, i):
                    act.wait_ge(sm["valued"], NU * e + (i + 1) * (NU // 2))
                    act.activation(oT[:, i * (GO // 2):(i + 1) * (GO // 2), :], OT[:, i, :].rearrange("p (g q) -> p g q", g=2),
                                   ACT.Copy).then_inc(sm["o_copied"], 1)

                def raise_up(g, j):
                    n, u, nk = units(g, j), j % NU, keys(j % 2)
                    act.wait_ge(sm["shifted"], n + 1)
                    if j >= RE:
                        act.wait_ge(sm["turned"], n - RE + 1)
                    at = j % (2 * NU)
                    act.activation(E[:, j % RE, 0:nk], S[:, j % RS, 0:nk], ACT.Exp, bias=least[:, at:at + 1],
                                   scale=-1.0, accum_out=total[:, at:at + 1]).then_inc(sm["exped"], 1)

                def share_out(g, j):
                    n, nk, at = units(g, j), keys(j % 2), j % (2 * NU)
                    act.wait_ge(sm["summed"], n + 1)
                    act.activation(E[:, j % RE, 0:nk], E[:, j % RE, 0:nk], ACT.Copy,
                                   scale=share[:, at:at + 1]).then_inc(sm["shared"], 1)

                def copy_turned(g, j):
                    n, nk = units(g, j), keys(j % 2)
                    act.wait_ge(sm["turned"], n + 1)
                    if j >= RT:
                        act.wait_ge(sm["valued"], n - RT + 1)
                    act.activation(ET[:, j % RT, 0:nk // P, :], TU[:, j % NTU, 0:nk].rearrange("p (c q) -> p c q", q=P),
                                   ACT.Copy).then_inc(sm["turned_copied"], 1)

                def body(g, j):
                    prepare(*ahead(g, j))
                    if j % NU == NU // 2 + value_lag:
                        copy_output(2 * g + j // NU, 0)
                    if j >= NU and j % NU == value_lag:
                        copy_output(2 * g + j // NU - 1, 1)
                    if j >= exp_lag:
                        raise_up(g, j - exp_lag)
                    if kind == "win":
                        if j >= share_lag:
                            share_out(g, j - share_lag)
                    elif j >= turn_lag:
                        copy_turned(g, j - turn_lag)

                steps(act, prepare, body)

            @block.vector
            def _(dve):
                dve.sem_inc(sm["added"], 1)
                if small:
                    dve.memset(OT[:, :, :], 0.0).then_inc(sm["o_zeroed"], 1)
                dve.wait_ge(sm["loaded"], loads)
                if kind in ("rel", "win"):
                    dve.wait_ge(sm["prepared"], 5 if kind == "rel" else 4)

                def stage(q):
                    dve.tensor_copy(xs[0:64, :], XN[0:64, ds(q * L, L)])
                    dve.tensor_copy(xs[64:P, 1:L], XN[64:P, ds(q * L, L - 1)]).then_inc(sm["staged"], 1)

                def split(q, n):
                    if n == 0:
                        dve.wait_ge(sm["qk_ready"], q + 1)
                        if not isinstance(q, int) or q > 0:
                            dve.wait_ge(sm["spread_made"], G * q)
                    else:
                        dve.wait_ge(sm["split"], 5 * q + n)
                    whole, rest = (qk, rest1, rest2)[n // 2], (rest1, rest2, None)[n // 2]
                    if n % 2 == 0:
                        dve.tensor_copy(part[:, n // 2, :, :], whole[:, :, :]).then_inc(sm["split"], 1)
                    else:
                        dve.tensor_tensor(rest[:, :, :], whole[:, :, :], part[:, n // 2, :, :], ALU.subtract).then_inc(sm["split"], 1)

                def prepare(q, parity, s):
                    later = not isinstance(q, int) or q > 0
                    if small and s == 14:
                        dve.wait_ge(sm["projected"], q + 1)
                        if kind == "rel":
                            src = PJ[:, 0, :]
                            dve.tensor_scalar(qv[:, parity, :], src[:, 0:L], vb[:, 0:1], None, ALU.add)
                            dve.tensor_scalar(qk[:, 0, :], src[:, 0:L], ub[:, 0:1], None, ALU.add)
                            dve.tensor_copy(qk[:, 1, :], src[:, L:2 * L]).then_inc(sm["qk_ready"], 1)
                        else:
                            for x in range(2):
                                tb = rt[:, x, :].rearrange("p (o n) -> p o n", o=1).broadcast_to([P, 2, L])
                                dve.tensor_tensor(parts[:, x, :, :], PJ[:, x, :].rearrange("p (w n) -> p w n", w=2), tb,
                                                  ALU.mult).then_inc(sm["parts_made"], 1)
                    if kind == "rel" and 15 <= s < 20:
                        split(q, s - 15)
                    if kind == "win":
                        c = s // 2
                        if s == 14:
                            dve.wait_ge(sm["v_made"], q + 1)
                            stage(q + 1)
                        if s % 2 == 1 and c < G:
                            if later or c > 0:
                                dve.wait_ge(sm["m3_made"], G * q + c)
                            dve.wait_ge(sm["projected"], G * q + c + 1)
                            dve.tensor_tensor(m2[:, :], PJ[:, 1, :], tab[:, 1, :, :].rearrange("p w n -> p (w n)"), ALU.mult)
                            dve.wait_ge(sm["squares"], G * q + c + 1)
                            dve.tensor_tensor(m1[:, :], PJ[:, 0, :], tab[:, 0, :, :].rearrange("p w n -> p (w n)"),
                                              ALU.mult).then_inc(sm["m1_made"], 1)
                        if s % 2 == 0 and 1 <= c <= G:
                            if later:
                                dve.wait_ge(sm["logs"], q)
                            dve.wait_ge(sm["norms"], G * q + c)
                            dve.tensor_scalar(clipped[:, c - 1, :], NORM[:, :], 1e-24, None, ALU.max).then_inc(sm["clips"], 1)
                        if s == 9:
                            dve.wait_ge(sm["v_made"], q + 1)
                            for t in range(2):
                                o = dve.tensor_copy(V[:, parity, t, :], PJ[:, t, 0:VW])
                            o.then_inc(sm["v_copied"], 1)

                def epilogue(e, parity, s):
                    if s == FINAL_STEP[kind] + 2:
                        dve.wait_ge(sm["final"], e + 1)
                        dve.tensor_tensor(R[:, ds(e * L, L)], PJ[:, 0, 0:L], R[:, ds(e * L, L)], ALU.add).then_inc(sm["added"], 1)

                def make_parts(H, n):
                    dve.wait_ge(sm["a_made"], n + H + 1)
                    if H >= 2:
                        dve.wait_ge(sm["a_ready"], n + H - 1)
                    dve.tensor_tensor(tparts[:, H % 2, :, :], TP[:, :].rearrange("p (x n) -> p x n", x=2),
                                      turn[:, :, :], ALU.mult).then_inc(sm["a_parts"], 1)

                def shift(g, j):
                    n, t = units(g, j), j % 2
                    nk = keys(t)
                    if kind == "rel":
                        dve.wait_ge(sm["bd_ready"], n + 1)
                        add = bd[:, t, :]
                    else:
                        dve.wait_ge(sm["scored"], n + 1)
                        add = mask[:, t, 0:nk]
                    if j >= RS:
                        dve.wait_ge(sm["exped"], n - RS + 1)
                    dve.sem_inc(sm["passed"], 1)
                    at = j % (2 * NU)
                    dve.tensor_tensor_reduce(S[:, j % RS, 0:nk], SC[:, j % NSC, 0:nk], add, -scale, 3e38, ALU.add, ALU.min,
                                             least[:, at:at + 1]).then_inc(sm["shifted"], 1)

                def copy_turned(g, j):
                    n, nk = units(g, j), keys(j % 2)
                    dve.wait_ge(sm["turned"], n + 1)
                    if j >= RT:
                        dve.wait_ge(sm["valued"], n - RT + 1)
                    dve.tensor_copy(ET[:, j % RT, 0:nk // P, :],
                                    TU[:, j % NTU, 0:nk].rearrange("p (c q) -> p c q", q=P)).then_inc(sm["turned_copied"], 1)

                def share_out(g, j):
                    n, nk, at = units(g, j), keys(j % 2), j % (2 * NU)
                    dve.wait_ge(sm["exped"], n + 1)
                    dve.reciprocal(share[:, at:at + 1], total[:, at:at + 1]).then_inc(sm["summed"], 1)
                    if kind == "win":
                        return
                    dve.wait_ge(sm["summed"], n + 1)
                    dve.tensor_scalar(E[:, j % RE, 0:nk], E[:, j % RE, 0:nk], share[:, at:at + 1], None,
                                      ALU.mult).then_inc(sm["shared"], 1)

                def mask_products(g, j):
                    n, t = units(g, j), j % 2
                    dve.wait_ge(sm["scored"], n + 1)
                    if j >= 2:
                        dve.wait_ge(sm["bd_ready"], n - 1)
                    dve.tensor_tensor(lu[:, t, :].rearrange("p (x n) -> p x n", x=2)[:, :, 0:P],
                                      SC[:, j % NSC, L:2 * L].rearrange("p (x n) -> p x n", x=2), rmask[:, t, :, :],
                                      ALU.mult).then_inc(sm["masked"], 1)

                def body(g, j):
                    prepare(*ahead(g, j))
                    if j >= NU:
                        epilogue(*behind(g, j))
                    if j >= shift_lag:
                        shift(g, j - shift_lag)
                    if kind == "rel":
                        mask_products(g, j)
                    if j >= share_lag:
                        share_out(g, j - share_lag)
                    if kind == "win" and j >= turn_lag:
                        copy_turned(g, j - turn_lag)
                    if kind == "rel" and j % 2 == 0:
                        make_parts(j // 2 + 1, 2 * nh * g)

                if kind == "win":
                    dve.wait_ge(sm["cleared"], 1)
                    stage(0)
                for s in range(NU):
                    prepare(0, 0, s)
                if kind == "rel":
                    make_parts(0, 0)
                for j in range(START):
                    body(0, j)
                with dve.Fori(0, NB // 2) as g:
                    for j in range(START, 2 * NU + START):
                        body(g, j)


def gated_ffn(nc, tag, kind, R, XN, W):
    gelu = kind == "gelu"
    HID = 341 if gelu else 384
    NC = 3
    width = [min(P, HID - c * P) for c in range(NC)]
    U = 2
    with Phase(nc, tag) as ph:
        wg, wu = ph.sb("wg", [P, HID]), ph.sb("wu", [P, HID])
        wd = ph.sb("wd", [P, NC, D])
        gate_on, hid = ph.sb("gate_on", [P, 2, BLK]), ph.sb("hid", [P, U, NC, BLK])
        G, UP = ph.ps("G", [P, 2, BLK]), ph.ps("UP", [P, 2, BLK])
        OUT = ph.ps("OUT", [P, U, BLK])
        names = "loaded weights_ready gate_made up_made gated hidden out_made trip_done".split()
        sm = {n: ph.sem(n) for n in names}
        if gelu:
            ba, bg, b2 = ph.sb("ba", [P, NC]), ph.sb("bg", [P, NC]), ph.sb("b2", [P, 1])
            loads = 16 * 9
        else:
            ig, iu, idn = ph.sb("ig", [P, HID], I32), ph.sb("iu", [P, HID], I32), ph.sb("idn", [P, NC, D], I32)
            loads = 16 * 3
        with nc.Block() as block:
            @block.sync
            def _(sp):
                if gelu:
                    load(sp, wu[:, :], W["w1"][:, 0:HID], sm["loaded"])
                    load(sp, wg[:, :], W["w1"][:, HID:2 * HID], sm["loaded"])
                    load(sp, wd[:, 0:2, :], W["w2"][0:2 * P, :].rearrange("(c p) d -> p c d", p=P), sm["loaded"])
                    load(sp, wd[0:width[2], 2, :], W["w2"][2 * P:HID, :], sm["loaded"])
                    for dst, o in ((ba, 0), (bg, HID)):
                        load(sp, dst[:, 0:2], W["b1"][o:o + 2 * P].rearrange("(c p) -> p c", p=P), sm["loaded"])
                        load(sp, dst[0:width[2], 2:3], W["b1"][o + 2 * P:o + HID].rearrange("(p c) -> p c", c=1), sm["loaded"])
                    load(sp, b2[:, :], W["b2"].rearrange("(p c) -> p c", c=1), sm["loaded"])
                else:
                    load(sp, ig[:, :], W["gate"], sm["loaded"])
                    load(sp, iu[:, :], W["up"], sm["loaded"])
                    load(sp, idn[:, :, :], W["down"].rearrange("(c p) d -> p c d", p=P), sm["loaded"])

            @block.tensor
            def _(pe):
                pe.wait_ge(sm["loaded"], loads)
                if not gelu:
                    pe.wait_ge(sm["weights_ready"], 3)
                with pe.Fori(0, NBLK // U) as g:
                    pe.wait_ge(sm["trip_done"], g + 1)
                    def down(s):
                        pe.wait_ge(sm["hidden"], NC * (U * g + s) + NC)
                        for c in range(NC):
                            last = pe.matmul(OUT[:, s, :], wd[0:width[c], c, :], hid[0:width[c], s, c, :],
                                             start=c == 0, stop=c == NC - 1)
                        last.then_inc(sm["out_made"], 1)

                    for k in range(U * NC):
                        s, c = k // NC, k % NC
                        x = XN[:, ds((U * g + s) * BLK, BLK)]
                        if k >= 2:
                            pe.wait_ge(sm["hidden"], NC * U * g + k - 1)
                        cols = slice(c * P, c * P + width[c])
                        pe.matmul(G[0:width[c], k % 2, :], wg[:, cols], x, start=True, stop=True).then_inc(sm["gate_made"], 1)
                        pe.matmul(UP[0:width[c], k % 2, :], wu[:, cols], x, start=True, stop=True).then_inc(sm["up_made"], 1)
                        if k == NC + 1:
                            down(0)
                    down(1)

            @block.scalar
            def _(act):
                act.wait_ge(sm["loaded"], loads)
                with act.Fori(0, NBLK // U) as g:
                    act.wait_ge(sm["trip_done"], g + 1)
                    for k in range(U * NC):
                        c = k % NC
                        w = width[c]
                        act.wait_ge(sm["gate_made"], NC * U * g + k + 1)
                        if k >= 2:
                            act.wait_ge(sm["hidden"], NC * U * g + k - 1)
                        if gelu:
                            act.activation(gate_on[0:w, k % 2, :], G[0:w, k % 2, :], ACT.Gelu,
                                           bias=bg[0:w, c:c + 1]).then_inc(sm["gated"], 1)
                        else:
                            act.activation(gate_on[0:w, k % 2, :], G[0:w, k % 2, :], ACT.Silu).then_inc(sm["gated"], 1)

            @block.vector
            def _(dve):
                dve.sem_inc(sm["trip_done"], 1)
                dve.wait_ge(sm["loaded"], loads)
                if not gelu:
                    for dst, src in ((wg, ig), (wu, iu)):
                        dve.tensor_scalar(dst[:, :], src[:, :], 1.0 / 127.0, None, ALU.mult).then_inc(sm["weights_ready"], 1)
                    dve.tensor_scalar(wd[:, :, :], idn[:, :, :], 1.0 / 127.0, None, ALU.mult).then_inc(sm["weights_ready"], 1)
                with dve.Fori(0, NBLK // U) as g:
                    def residual(s):
                        dve.wait_ge(sm["out_made"], U * g + s + 1)
                        at = ds((U * g + s) * BLK, BLK)
                        if gelu:
                            o = dve.scalar_tensor_tensor(R[:, at], OUT[:, s, :], b2[:, 0:1], R[:, at], ALU.add, ALU.add)
                        else:
                            o = dve.scalar_tensor_tensor(R[:, at], OUT[:, s, :], 0.5, R[:, at], ALU.mult, ALU.add)
                        if s == U - 1:
                            o.then_inc(sm["trip_done"], 1)

                    for k in range(U * NC):
                        s, c = k // NC, k % NC
                        w = width[c]
                        dve.wait_ge(sm["gated"], NC * U * g + k + 1)
                        dve.wait_ge(sm["up_made"], NC * U * g + k + 1)
                        if gelu:
                            dve.scalar_tensor_tensor(hid[0:w, s, c, :], UP[0:w, k % 2, :], ba[0:w, c:c + 1],
                                                     gate_on[0:w, k % 2, :], ALU.add, ALU.mult).then_inc(sm["hidden"], 1)
                        else:
                            dve.tensor_tensor(hid[0:w, s, c, :], UP[0:w, k % 2, :], gate_on[0:w, k % 2, :],
                                              ALU.mult).then_inc(sm["hidden"], 1)
                    residual(0)
                    residual(1)


def add_half(nc, tag, X, Y):
    with Phase(nc, tag) as ph:
        with nc.Block() as block:
            @block.vector
            def _(dve):
                dve.scalar_tensor_tensor(X[:, :], Y[:, 0:T], 0.5, X[:, :], ALU.mult, ALU.add)


def latent_attention(nc, tag, X, XN, A, W, ident):
    scale = 8 ** -0.5
    NP_ = 8
    with Phase(nc, tag) as ph:
        xs, xopen = ph.sb("xs", [P, L]), ph.sb("xopen", [P, 2, 64])
        wk, wkx, wv, wp = (ph.sb(n, [P, P]) for n in ("wk", "wkx", "wv", "wp"))
        wg = ph.sb("wg", [P, 1024])
        lat = ph.sb("lat", [P, NP_, P])
        rt = ph.sb("rt", [P, 2, L])
        lmask = ph.sb("lmask", [P, 64])
        own = ph.sb("own", [P, NP_, P])
        parts, kr = ph.sb("parts", [P, 2, L]), ph.sb("kr", [P, L])
        V = ph.sb("V", [P, P])
        s1, s2, pr = ph.sb("s1", [P, 16, 64]), ph.sb("s2", [P, 16, 64]), ph.sb("pr", [P, 16, 64])
        smax, ssum, sinv = (ph.sb(n, [P, 16]) for n in ("smax", "ssum", "sinv"))
        prT, att = ph.sb("prT", [P, NP_, P]), ph.sb("att", [P, NP_, P])
        gmax, gsum, ginv = (ph.sb(n, [P, 2, 16]) for n in ("gmax", "gsum", "ginv"))
        g1, g2, g3 = (ph.sb(n, [P, 2, 16, 64]) for n in ("g1", "g2", "g3"))
        gT = ph.sb("gT", [P, NP_, L])
        wt = ph.sb("wt", [P, L])
        PJ, PV = ph.ps("PJ", [P, 512]), ph.ps("PV", [P, 512])
        SC, GA, TR = ph.ps("SC", [P, 2, 512]), ph.ps("GA", [P, 2, 512]), ph.ps("TR", [P, 2, 512])
        names = ("loaded cleared staged k_made v_made parts_made k_ready v_copied scored s1_made smaxed s2_made s_exped "
                 "ssummed sinverted probs p_turned p_copied att_made att_ready g_made gmaxed g1_made g_exped gsummed "
                 "ginverted gates g_turned g_copied weighted w_copied final added").split()
        sm = {n: ph.sem(n) for n in names}
        loads = 16 * (8 + 16)
        flat = (lambda ap: ap.rearrange("p (h l) -> p h l", l=64))

        def spread(ap, n):
            return ap.rearrange("p (h o) -> p h o", o=1).broadcast_to([P, ap.shape[1], n])

        with nc.Block() as block:
            @block.sync
            def _(sp):
                for dst, n in ((wk, "k"), (wkx, "k_crossed"), (wv, "v"), (wp, "p"), (wg, "g")):
                    load(sp, dst[:, :], W[n], sm["loaded"])
                load(sp, rt[:, :, :], A["rope8"], sm["loaded"])
                load(sp, lmask[:, :], A["latent_mask"], sm["loaded"])
                load(sp, own[:, :, :], A["own_head"], sm["loaded"])
                sp.wait_ge(sm["cleared"], 1)
                for h in range(16):
                    load(sp, lat[8 * h:8 * h + 8, h // 2, (h % 2) * 64:(h % 2) * 64 + 64], W["q"][h, :, :], sm["loaded"])

            @block.gpsimd
            def _(pool):
                pool.memset(lat[:, :, :], 0.0).then_inc(sm["cleared"], 1)

                def rotated_keys(q):
                    pool.wait_ge(sm["parts_made"], q + 1)
                    pool.tensor_tensor(kr[:, :], parts[:, 0, :], parts[:, 1, :], ALU.add).then_inc(sm["k_ready"], 1)

                rotated_keys(0)
                with pool.Fori(0, NB) as b:
                    for t in range(2):
                        pool.wait_ge(sm["ginverted"], 2 * b + t + 1)
                        pool.tensor_tensor(g3[:, t, :, :], g2[:, t, :, :], spread(ginv[:, t, :], 64), ALU.mult).then_inc(sm["gates"], 1)
                    rotated_keys(b + 1)

            @block.tensor
            def _(pe):
                pe.wait_ge(sm["loaded"], loads)

                def open_sequence(n):
                    pe.wait_ge(sm["staged"], 2 * n + 2)
                    if not isinstance(n, int):
                        pe.wait_ge(sm["added"], n)
                        pe.wait_ge(sm["g1_made"], 4 * n)
                    pe.matmul(PJ[:, 0:L], wk[:, :], xs[:, :], start=True, stop=True)
                    pe.matmul(PJ[:, L:2 * L], wkx[:, :], xs[:, :], start=True, stop=True).then_inc(sm["k_made"], 1)
                    pe.matmul(PV[:, 0:P], xopen[:, :, :], wv[:, :], start=True,
                              stop=True).then_inc(sm["v_made"], 1)
                    for q in range(2):
                        pe.matmul(GA[:, q, :], xs[:, 0:P], wg[:, q * 512:(q + 1) * 512], start=True, stop=True).then_inc(sm["g_made"], 1)

                def scores(n):
                    pe.wait_ge(sm["k_ready"], n + 1)
                    if not isinstance(n, int):
                        pe.wait_ge(sm["att_ready"], 2 * n)
                    open_keys = kr[:, :].rearrange("p (n t) -> p n t", n=2)[:, :, 0:64]
                    for i in range(NP_):
                        o = pe.matmul(SC[:, i // 4, (i % 4) * P:(i % 4 + 1) * P], lat[:, i, :], open_keys, start=True, stop=True)
                        if i % 4 == 3:
                            o.then_inc(sm["scored"], 1)
                    for q in range(2):
                        pe.wait_ge(sm["g1_made"], 4 * n + q + 1)
                        pe.matmul(GA[:, q, :], xs[:, P:L], wg[:, q * 512:(q + 1) * 512], start=True, stop=True).then_inc(sm["g_made"], 1)

                open_sequence(0)
                scores(0)
                with pe.Fori(0, NB) as b:
                    pe.wait_ge(sm["probs"], b + 1)
                    for i in range(NP_):
                        o = pe.transpose(TR[:, i // 4, (i % 4) * P:(i % 4 + 1) * P],
                                         pr[:, 2 * i:2 * i + 2, :], ident[:, :])
                        if i % 4 == 3:
                            o.then_inc(sm["p_turned"], 1)
                    pe.wait_ge(sm["p_copied"], 2 * b + 2)
                    pe.wait_ge(sm["v_copied"], b + 1)
                    pe.wait_ge(sm["s1_made"], 2 * b + 2)
                    for i in range(NP_):
                        o = pe.matmul(SC[:, i // 4, (i % 4) * P:(i % 4 + 1) * P], prT[:, i, :], V[:, :], start=True, stop=True)
                        if i % 4 == 3:
                            o.then_inc(sm["att_made"], 1)
                    open_sequence(b + 1)
                    for t in range(2):
                        pe.wait_ge(sm["gates"], 2 * b + t + 1)
                        for q in range(2):
                            if t == 1:
                                pe.wait_ge(sm["g_copied"], 4 * b + q + 1)
                            for i in range(4):
                                pair = 4 * q + i
                                o = pe.transpose(TR[:, q, i * P:(i + 1) * P], g3[:, t, 2 * pair:2 * pair + 2, :], ident[:, :])
                            o.then_inc(sm["g_turned"], 1)
                    scores(b + 1)
                    pe.wait_ge(sm["g_copied"], 4 * b + 4)
                    pe.wait_ge(sm["att_ready"], 2 * b + 2)
                    pe.wait_ge(sm["v_copied"], b + 2)
                    for i in range(NP_):
                        o = pe.matmul(PV[:, 0:L], att[:, i, :], gT[:, i, :], start=i == 0, stop=i == NP_ - 1)
                    o.then_inc(sm["weighted"], 1)
                    pe.wait_ge(sm["w_copied"], b + 1)
                    pe.wait_ge(sm["parts_made"], b + 2)
                    pe.matmul(PJ[:, 0:L], wp[:, :], wt[:, :], start=True, stop=True).then_inc(sm["final"], 1)

            @block.scalar
            def _(act):

                def copy_values(n):
                    act.wait_ge(sm["v_made"], n + 1)
                    act.activation(V[:, :], PV[:, 0:P], ACT.Copy).then_inc(sm["v_copied"], 1)

                def first_gates(n):
                    act.wait_ge(sm["g1_made"], 4 * n + 2)
                    act.activation(g2[:, 0, :, :], g1[:, 0, :, :], ACT.Exp, scale=scale).then_inc(sm["g_exped"], 1)

                def exponentials(n):
                    act.wait_ge(sm["s2_made"], n + 1)
                    act.activation(pr[:, :, :], s2[:, :, :], ACT.Exp).then_inc(sm["s_exped"], 1)
                    act.wait_ge(sm["g1_made"], 4 * n + 4)
                    act.activation(g2[:, 1, :, :], g1[:, 1, :, :], ACT.Exp, scale=scale).then_inc(sm["g_exped"], 1)

                copy_values(0)
                first_gates(0)
                exponentials(0)
                with act.Fori(0, NB) as b:
                    for q in range(2):
                        act.wait_ge(sm["p_turned"], 2 * b + q + 1)
                        act.activation(prT[:, 4 * q:4 * q + 4, :], TR[:, q, :].rearrange("p (i c) -> p i c", i=4),
                                       ACT.Copy).then_inc(sm["p_copied"], 1)
                    copy_values(b + 1)
                    for t in range(2):
                        for q in range(2):
                            act.wait_ge(sm["g_turned"], 4 * b + 2 * t + q + 1)
                            act.activation(gT[:, 4 * q:4 * q + 4, t * P:(t + 1) * P],
                                           TR[:, q, :].rearrange("p (i c) -> p i c", i=4), ACT.Copy).then_inc(sm["g_copied"], 1)
                    first_gates(b + 1)
                    act.wait_ge(sm["weighted"], b + 1)
                    act.activation(wt[:, :], PV[:, 0:L], ACT.Copy).then_inc(sm["w_copied"], 1)
                    exponentials(b + 1)

            @block.vector
            def _(dve):
                dve.sem_inc(sm["added"], 1)
                dve.wait_ge(sm["loaded"], loads)

                def stage(q):
                    if not isinstance(q, int):
                        dve.wait_ge(sm["g_made"], 4 * q)
                    dve.tensor_copy(xs[:, :], XN[:, ds(q * L, L)]).then_inc(sm["staged"], 1)
                    for n in range(2):
                        o = dve.tensor_copy(xopen[:, n, :], XN[:, ds(q * L + n * P, 64)])
                    o.then_inc(sm["staged"], 1)

                def rotate_keys(q):
                    dve.wait_ge(sm["k_made"], q + 1)
                    dve.tensor_tensor(parts[:, :, :], PJ[:, :].rearrange("p (w n) -> p w n", w=2), rt[:, :, :],
                                      ALU.mult).then_inc(sm["parts_made"], 1)

                def gate_tile(n, t):
                    for q in range(2):
                        dve.wait_ge(sm["g_made"], 4 * n + 2 * t + q + 1)
                        dve.tensor_reduce(gmax[:, t, 8 * q:8 * q + 8], flat(GA[:, q, :]), AX, ALU.max).then_inc(sm["gmaxed"], 1)
                    for q in range(2):
                        dve.wait_ge(sm["gmaxed"], 4 * n + 2 * t + q + 1)
                        dve.tensor_tensor(g1[:, t, 8 * q:8 * q + 8, :], flat(GA[:, q, :]),
                                          spread(gmax[:, t, 8 * q:8 * q + 8], 64), ALU.subtract).then_inc(sm["g1_made"], 1)

                def first_half(n):
                    rotate_keys(n)
                    gate_tile(n, 0)
                    for q in range(2):
                        dve.wait_ge(sm["scored"], 2 * n + q + 1)
                        m = lmask[:, :].rearrange("p (o c) -> p o c", o=1).broadcast_to([P, 8, 64])
                        dve.scalar_tensor_tensor(s1[:, 8 * q:8 * q + 8, :], flat(SC[:, q, :]), scale, m, ALU.mult,
                                                 ALU.add).then_inc(sm["s1_made"], 1)
                    dve.wait_ge(sm["s1_made"], 2 * n + 2)
                    dve.tensor_reduce(smax[:, :], s1[:, :, :], AX, ALU.max).then_inc(sm["smaxed"], 1)
                    dve.wait_ge(sm["smaxed"], n + 1)
                    dve.tensor_tensor(s2[:, :, :], s1[:, :, :], spread(smax[:, :], 64), ALU.subtract).then_inc(sm["s2_made"], 1)
                    gate_tile(n, 1)

                stage(0)
                first_half(0)
                with dve.Fori(0, NB) as b:
                    stage(b + 1)
                    dve.wait_ge(sm["s_exped"], b + 1)
                    dve.tensor_reduce(ssum[:, :], pr[:, :, :], AX, ALU.add).then_inc(sm["ssummed"], 1)
                    dve.wait_ge(sm["ssummed"], b + 1)
                    dve.reciprocal(sinv[:, :], ssum[:, :]).then_inc(sm["sinverted"], 1)
                    dve.wait_ge(sm["sinverted"], b + 1)
                    dve.tensor_tensor(pr[:, :, :], pr[:, :, :], spread(sinv[:, :], 64), ALU.mult).then_inc(sm["probs"], 1)
                    for t in range(2):
                        dve.wait_ge(sm["g_exped"], 2 * b + t + 1)
                        dve.tensor_reduce(gsum[:, t, :], g2[:, t, :, :], AX, ALU.add).then_inc(sm["gsummed"], 1)
                        dve.wait_ge(sm["gsummed"], 2 * b + t + 1)
                        dve.reciprocal(ginv[:, t, :], gsum[:, t, :]).then_inc(sm["ginverted"], 1)
                    for q in range(2):
                        dve.wait_ge(sm["att_made"], 2 * b + q + 1)
                        dve.tensor_tensor(att[:, 4 * q:4 * q + 4, :], SC[:, q, :].rearrange("p (i c) -> p i c", i=4),
                                          own[:, 4 * q:4 * q + 4, :], ALU.mult).then_inc(sm["att_ready"], 1)
                    first_half(b + 1)
                    dve.wait_ge(sm["final"], b + 1)
                    at = ds(b * L, L)
                    dve.tensor_tensor(X[:, at], PJ[:, 0:L], X[:, at], ALU.add).then_inc(sm["added"], 1)


def product_key_experts(nc, tag, X, XN, A, W, ident, eps):
    NH, NK, E = 8, 32, 1024
    U = 2
    NU = U * NH
    RING, W_RING = 8, 4
    with Phase(nc, tag) as ph:
        wq = ph.sb("wq", [P, 16, P])
        keys = ph.sb("keys", [P, 2, NH, NK])
        fused = ph.sb("fused", [P, 2, NH, NK])
        down, up = ph.sb("down", [P, E]), ph.sb("up", [P, 8, P])
        gam, bet = ph.sb("gam", [P, 1]), ph.sb("bet", [P, 1])
        st, mv = ph.sb("st", [P, NBLK, 6]), ph.sb("mv", [P, 2])
        col = ph.sb("col", [P, 4])
        ms = ph.sb("ms", [P, 1])
        xb = ph.sb("xb", [P, P])
        sim = ph.sb("sim", [P, U, 2, NH, NK])
        top = ph.sb("top", [P, 2, NH, 8])
        cand = ph.sb("cand", [P, NH, 64])
        best = ph.sb("best", [P, U, NH, 8])
        S, sg, w = ph.sb("S", [P, RING, E]), ph.sb("sg", [P, RING, E]), ph.sb("w", [P, W_RING, E])
        act_h = ph.sb("act_h", [P, 8, U * P])
        mix = ph.sb("mix", [P, 8, U * P])
        SIM = ph.ps("SIM", [P, 512])
        WT = ph.ps("WT", [P, U, 2, 512])
        HT = ph.ps("HT", [P, 2, 512])
        OUT = ph.ps("OUT", [P, 512])
        names = ("loaded stats moments sds invs scales negs affine fused_made fused_ready normed sim_made sim_copied "
                 "tops cands bests summed sigm weighed w_turned h_made h_on mixed out_made added passed").split()
        sm = {n: ph.sem(n) for n in names}
        loads = 16 * 6
        with nc.Block() as block:
            @block.sync
            def _(sp):
                load(sp, gam[:, :], W["gamma"].rearrange("(p c) -> p c", c=1), sm["loaded"])
                load(sp, bet[:, :], W["beta"].rearrange("(p c) -> p c", c=1), sm["loaded"])
                load(sp, wq[:, :, :], W["w_q"].rearrange("(n k) c -> k n c", k=P), sm["loaded"])
                load(sp, keys[:, :, :, :], W["keys"], sm["loaded"])
                load(sp, down[:, :], W["down"], sm["loaded"])
                load(sp, up[:, :, :], W["up"].rearrange("(n e) c -> e n c", e=P), sm["loaded"])

            @block.gpsimd
            def _(pool):
                with pool.Fori(0, NT // U) as g:
                    for k in range(NU):
                        s, h = k // NH, k % NH
                        if h == 0:
                            pool.wait_ge(sm["sim_copied"], U * g + s + 1)
                        pool.wait_ge(sm["weighed"], NU * g + k + 1)
                        a = sim[:, s, 0, h, :].rearrange("p (i o) -> p i o", o=1).broadcast_to([P, NK, NK])
                        c = sim[:, s, 1, h, :].rearrange("p (o i) -> p o i", o=1).broadcast_to([P, NK, NK])
                        pool.tensor_tensor(S[:, k % RING, :].rearrange("p (a c) -> p a c", a=NK), a, c,
                                           ALU.add).then_inc(sm["summed"], 1)

            @block.tensor
            def _(pe):
                pe.wait_ge(sm["loaded"], loads)
                for n in range(16):
                    o = pe.matmul(SIM[:, n * NK:(n + 1) * NK], wq[:, n, :], keys[:, n // NH, n % NH, :], start=True, stop=True)
                o.then_inc(sm["fused_made"], 1)
                pe.wait_ge(sm["fused_ready"], 1)

                def similarities(tile):
                    pe.wait_ge(sm["normed"], tile + 1)
                    if not isinstance(tile, int):
                        pe.wait_ge(sm["sim_copied"], tile)
                    pe.matmul(SIM[:, :], xb[:, :], fused[:, :, :, :], start=True, stop=True).then_inc(sm["sim_made"], 1)

                similarities(0)
                with pe.Fori(0, NT // U) as g:
                    for k in range(NU):
                        s, h = k // NH, k % NH
                        if h == 0:
                            similarities(U * g + s + 1)
                            pe.wait_ge(sm["h_on"], 2 * (U * g + s) + 2)
                            for n in range(8):
                                o = pe.matmul(HT[:, n // 4, n % 4 * P:(n % 4 + 1) * P], down[:, n * P:(n + 1) * P],
                                              XN[:, ds((U * g + s) * P, P)], start=True, stop=True)
                                if n % 4 == 3:
                                    o.then_inc(sm["h_made"], 1)
                            pe.wait_ge(sm["mixed"], 4 * g + 2 * s + 2)
                        pe.wait_ge(sm["weighed"], NU * g + k + 1 + RING)
                        for n in range(8):
                            o = pe.matmul(WT[:, s, n // 4, (n % 4) * P:(n % 4 + 1) * P], w[:, k % W_RING, n * P:(n + 1) * P],
                                          ident[:, :], start=h == 0 and n % 4 == 0, stop=h == NH - 1,
                                          is_transpose=True, skip_group_check=True)
                        o.then_inc(sm["w_turned"], 1)
                    pe.wait_ge(sm["mixed"], 4 * g + 8)
                    pe.wait_ge(sm["added"], g + 1)
                    for n in range(8):
                        o = pe.matmul(OUT[:, 0:U * P], up[:, n, :], mix[:, n, :], start=n == 0, stop=n == 7)
                    o.then_inc(sm["out_made"], 1)

            @block.scalar
            def _(act):
                act.wait_ge(sm["moments"], 1)
                act.activation(col[:, 0:1], mv[:, 1:2], ACT.Sqrt, bias=eps[:, 0:1]).then_inc(sm["sds"], 1)
                act.wait_ge(sm["fused_made"], 1)
                act.activation(fused[:, :, :, :], SIM[:, :].rearrange("p (a b c) -> p a b c", a=2, b=NH), ACT.Copy).then_inc(sm["fused_ready"], 1)
                act.wait_ge(sm["affine"], 1)

                def normed(tile):
                    act.activation(xb[:, :], XN[:, ds(tile * P, P)], ACT.Identity, bias=col[:, 3:4],
                                   scale=col[:, 2:3]).then_inc(sm["normed"], 1)

                def copy_similarities(tile, slot):
                    act.wait_ge(sm["sim_made"], tile + 1)
                    act.activation(sim[:, slot, :, :, :], SIM[:, :].rearrange("p (a b c) -> p a b c", a=2, b=NH),
                                   ACT.Copy).then_inc(sm["sim_copied"], 1)

                act.wait_ge(sm["fused_ready"], 1)
                normed(0)
                copy_similarities(0, 0)
                with act.Fori(0, NT // U) as g:
                    for k in range(NU):
                        s, h = k // NH, k % NH
                        if h == 0:
                            normed(U * g + s + 1)
                        if h == 4:
                            copy_similarities(U * g + s + 1, 1 - s)
                        if h == 6:
                            act.wait_ge(sm["mixed"], 4 * g + 2 * s + 2)
                            for r in range(2):
                                act.wait_ge(sm["h_made"], 2 * (U * g + s) + r + 1)
                                act.activation(act_h[:, 4 * r:4 * r + 4, s * P:(s + 1) * P],
                                               HT[:, r, :].rearrange("p (n c) -> p n c", n=4), ACT.Gelu).then_inc(sm["h_on"], 1)
                        act.wait_ge(sm["summed"], NU * g + k + 1)
                        act.wait_ge(sm["weighed"], NU * g + k + 1)
                        act.activation(sg[:, k % RING, :], S[:, k % RING, :], ACT.Sigmoid).then_inc(sm["sigm"], 1)

            @block.vector
            def _(dve):
                dve.sem_inc(sm["weighed"], RING)
                dve.sem_inc(sm["w_turned"], W_RING)
                dve.sem_inc(sm["mixed"], 4)
                dve.sem_inc(sm["h_on"], 2)
                dve.sem_inc(sm["added"], 1)
                for j in range(NBLK):
                    dve.bn_stats(st[:, j, :], XN[:, j * BLK:(j + 1) * BLK]).then_inc(sm["stats"], 1)
                dve.wait_ge(sm["stats"], NBLK)
                dve.bn_aggr(mv[:, :], st[:, :, :]).then_inc(sm["moments"], 1)
                dve.wait_ge(sm["sds"], 1)
                dve.reciprocal(col[:, 1:2], col[:, 0:1]).then_inc(sm["invs"], 1)
                dve.wait_ge(sm["invs"], 1)
                dve.wait_ge(sm["loaded"], loads)
                dve.tensor_tensor(col[:, 2:3], col[:, 1:2], gam[:, :], ALU.mult).then_inc(sm["scales"], 1)
                dve.wait_ge(sm["scales"], 1)
                dve.tensor_tensor(ms[:, :], mv[:, 0:1], col[:, 2:3], ALU.mult).then_inc(sm["negs"], 1)
                dve.wait_ge(sm["negs"], 1)
                dve.tensor_tensor(col[:, 3:4], bet[:, :], ms[:, :], ALU.subtract).then_inc(sm["affine"], 1)

                def best_of_sides(tile, slot):
                    dve.wait_ge(sm["sim_copied"], tile + 1)
                    dve.sem_inc(sm["passed"], 1)
                    for n in range(16):
                        o = dve.max(top[:, n // NH, n % NH, :], sim[:, slot, n // NH, n % NH, :])
                    o.then_inc(sm["tops"], 1)

                def best_pairs(tile, slot):
                    dve.wait_ge(sm["tops"], tile + 1)
                    a = top[:, 0, :, :].rearrange("p h (i o) -> p h i o", o=1).broadcast_to([P, NH, 8, 8])
                    c = top[:, 1, :, :].rearrange("p h (o i) -> p h o i", o=1).broadcast_to([P, NH, 8, 8])
                    dve.tensor_tensor(cand[:, :, :].rearrange("p h (i j) -> p h i j", i=8), a, c, ALU.add).then_inc(sm["cands"], 1)
                    dve.wait_ge(sm["cands"], tile + 1)
                    dve.sem_inc(sm["passed"], 1)
                    for h in range(NH):
                        o = dve.max(best[:, slot, h, :], cand[:, h, :])
                    o.then_inc(sm["bests"], 1)

                best_of_sides(0, 0)
                best_pairs(0, 0)
                with dve.Fori(0, NT // U) as g:
                    for s in range(U):
                        dve.wait_ge(sm["bests"], U * g + s + 1)
                        for h in range(NH):
                            k = s * NH + h
                            dve.wait_ge(sm["sigm"], NU * g + k + 1)
                            dve.wait_ge(sm["w_turned"], NU * g + k + 1)
                            dve.scalar_tensor_tensor(w[:, k % W_RING, :], S[:, k % RING, :], best[:, s, h, 7:8], sg[:, k % RING, :],
                                                     ALU.is_ge, ALU.mult).then_inc(sm["weighed"], 1)
                        best_of_sides(U * g + s + 1, 1 - s)
                        dve.wait_ge(sm["w_turned"], NU * g + (s + 1) * NH + W_RING)
                        dve.wait_ge(sm["h_on"], 2 * (U * g + s) + 2 + 2)
                        for q in range(2):
                            dve.tensor_tensor(mix[:, 4 * q:4 * q + 4, s * P:(s + 1) * P],
                                              WT[:, s, q, :].rearrange("p (n c) -> p n c", n=4),
                                              act_h[:, 4 * q:4 * q + 4, s * P:(s + 1) * P], ALU.mult).then_inc(sm["mixed"], 1)
                        best_pairs(U * g + s + 1, 1 - s)
                    dve.wait_ge(sm["out_made"], g + 1)
                    at = ds(g * U * P, U * P)
                    dve.scalar_tensor_tensor(X[:, at], OUT[:, 0:U * P], 0.5, X[:, at], ALU.mult, ALU.add).then_inc(sm["added"], 1)


NE, CAP = 64, 64
NPAIRS = NE // 2


def routed_experts(nc, tag, X, XN, A, W, ident, rows_dram):
    NPAIR = NE // 2
    with ExitStack() as keep:
        place = keep.enter_context(nc.sbuf_tensor(f"{tag}_place", [P, NT, NE], F32))
        vals = keep.enter_context(nc.sbuf_tensor(f"{tag}_vals", [P, NT, NPAIR, 3], F32))
        info = keep.enter_context(nc.sbuf_tensor(f"{tag}_info", [P, NPAIR, 3], F32))
        Eout = keep.enter_context(nc.sbuf_tensor(f"{tag}_Eout", [P, NPAIR, P], F32))
        route(nc, tag + "r", XN, A, W, ident, rows_dram, place, vals)
        find_slots(nc, tag + "s", A, place, vals, info)
        run_experts(nc, tag + "e", A, W, ident, rows_dram, info, Eout)
        combine(nc, tag + "c", X, XN, W, info, Eout)


def route(nc, tag, XN, A, W, ident, rows_dram, place, vals):
    with Phase(nc, tag) as ph:
        wr = ph.sb("wr", [P, NE])
        tri, ones, token = ph.sb("tri", [P, P]), ph.sb("ones", [P, P]), ph.sb("token", [P, NT])
        U = 4
        xs = ph.sb("xs", [P, U, P])
        rows = ph.sb("rows", [P, U, P])
        sc, masked, left, sel = (ph.sb(n, [P, U, NE]) for n in ("sc", "masked", "left", "sel"))
        gmax, gtop, gopen, top = (ph.sb(n, [P, U, 8]) for n in ("gmax", "gtop", "gopen", "top"))
        tsum, tclip, tinv = (ph.sb(n, [P, U]) for n in ("tsum", "tclip", "tinv"))
        wsel, wall, pos = (ph.sb(n, [P, U, NE]) for n in ("wsel", "wall", "pos"))
        before = ph.sb("before", [P, 2, NE])
        LR, CN = ph.ps("LR", [P, U, 512]), ph.ps("CN", [P, U, 512])
        names = ("loaded staged rows_made rows_copied rows_out scored gmaxed gtopped gopened masks topped lefted "
                 "selected tsums tclips tinvs wsels walls vals_made counted before_made poss places zeroed trip_done passed").split()
        sm = {n: ph.sem(n) for n in names}
        with nc.Block() as block:
            @block.sync
            def _(sp):
                for dst, src in ((wr, W["router"]), (tri, A["tri"]), (ones, A["ones"]), (token, A["token"])):
                    load(sp, dst[:, :], src, sm["loaded"])
                sp.sem_inc(sm["rows_out"], 16)
                with sp.Fori(0, NT // U) as g:
                    for s in range(U):
                        sp.wait_ge(sm["rows_copied"], U * g + s + 1)
                        sp.dma_start(rows_dram[ds((U * g + s) * P, P), :], rows[:, s, :]).then_inc(sm["rows_out"], 16)
                sp.wait_ge(sm["rows_out"], 16 * NT + 16)

            @block.tensor
            def _(pe):
                pe.wait_ge(sm["loaded"], 64)
                pe.wait_ge(sm["zeroed"], 1)
                with pe.Fori(0, NT // U) as g:
                    pe.wait_ge(sm["trip_done"], g + 1)
                    for s in range(U):
                        pe.wait_ge(sm["staged"], U * g + s + 1)
                        pe.matmul(LR[:, s, 0:NE], xs[:, s, :], wr[:, :], start=True, stop=True)
                        pe.transpose(LR[:, s, P:2 * P], xs[:, s, :], ident[:, :]).then_inc(sm["rows_made"], 1)
                    for s in range(U):
                        pe.wait_ge(sm["selected"], U * g + s + 1)
                        pe.matmul(CN[:, s, 0:NE], tri[:, :], sel[:, s, :], start=True, stop=False)
                        pe.wait_ge(sm["before_made"], U * g + s + 1)
                        pe.matmul(CN[:, s, 0:NE], ones[:, :], before[:, s % 2, :], start=False, stop=True).then_inc(sm["counted"], 1)

            @block.scalar
            def _(act):
                with act.Fori(0, NT // U) as g:
                    act.wait_ge(sm["trip_done"], g + 1)
                    act.wait_ge(sm["rows_out"], 16 * U * g + 16)
                    for s in range(U):
                        act.activation(xs[:, s, :], XN[:, ds((U * g + s) * P, P)], ACT.Copy).then_inc(sm["staged"], 1)
                    for s in range(U):
                        act.wait_ge(sm["rows_made"], U * g + s + 1)
                        act.activation(sc[:, s, :], LR[:, s, 0:NE], ACT.Sigmoid).then_inc(sm["scored"], 1)
                    for s in range(U):
                        act.activation(rows[:, s, :], LR[:, s, P:2 * P], ACT.Copy).then_inc(sm["rows_copied"], 1)

            @block.vector
            def _(dve):
                dve.sem_inc(sm["trip_done"], 1)
                dve.sem_inc(sm["before_made"], 1)
                dve.memset(before[:, :, :], 0.0).then_inc(sm["zeroed"], 1)
                dve.wait_ge(sm["zeroed"], 1)
                dve.wait_ge(sm["loaded"], 64)
                with dve.Fori(0, NT // U) as g:
                    at = lambda s: U * g + s + 1
                    grp = lambda ap: ap.rearrange("p (g e) -> p g e", g=8)
                    dve.wait_ge(sm["trip_done"], g + 1)
                    for s in range(U):
                        dve.wait_ge(sm["scored"], at(s))
                        dve.tensor_reduce(gmax[:, s, :], grp(sc[:, s, :]), AX, ALU.max).then_inc(sm["gmaxed"], 1)
                    for s in range(U):
                        dve.wait_ge(sm["gmaxed"], at(s))
                        dve.sem_inc(sm["passed"], 1)
                        dve.max(gtop[:, s, :], gmax[:, s, :]).then_inc(sm["gtopped"], 1)
                    for s in range(U):
                        dve.wait_ge(sm["gtopped"], at(s))
                        dve.tensor_scalar(gopen[:, s, :], gmax[:, s, :], gtop[:, s, 3:4], None, ALU.is_ge).then_inc(sm["gopened"], 1)
                    for s in range(U):
                        dve.wait_ge(sm["gopened"], at(s))
                        dve.tensor_tensor(grp(masked[:, s, :]), grp(sc[:, s, :]),
                                          gopen[:, s, :].rearrange("p (g o) -> p g o", o=1).broadcast_to([P, 8, 8]),
                                          ALU.mult).then_inc(sm["masks"], 1)
                    for s in range(U):
                        dve.wait_ge(sm["masks"], at(s))
                        dve.sem_inc(sm["passed"], 1)
                        dve.max(top[:, s, :], masked[:, s, :]).then_inc(sm["topped"], 1)
                    for s in range(U):
                        dve.wait_ge(sm["topped"], at(s))
                        dve.sem_inc(sm["passed"], 1)
                        dve.match_replace(left[:, s, :], top[:, s, :], masked[:, s, :], -1.0).then_inc(sm["lefted"], 1)
                    for s in range(U):
                        dve.wait_ge(sm["lefted"], at(s))
                        dve.tensor_tensor(sel[:, s, :], left[:, s, :], masked[:, s, :], ALU.not_equal).then_inc(sm["selected"], 1)
                        dve.tensor_reduce(tsum[:, s:s + 1], top[:, s, :], AX, ALU.add).then_inc(sm["tsums"], 1)
                    for s in range(U):
                        dve.wait_ge(sm["tsums"], at(s))
                        dve.tensor_scalar(tclip[:, s:s + 1], tsum[:, s:s + 1], 1e-9, None, ALU.max).then_inc(sm["tclips"], 1)
                    for s in range(U):
                        dve.wait_ge(sm["tclips"], at(s))
                        dve.reciprocal(tinv[:, s:s + 1], tclip[:, s:s + 1]).then_inc(sm["tinvs"], 1)
                    for s in range(U):
                        dve.wait_ge(sm["selected"], at(s))
                        dve.tensor_tensor(wsel[:, s, :], sel[:, s, :], masked[:, s, :], ALU.mult).then_inc(sm["wsels"], 1)
                    for s in range(U):
                        dve.wait_ge(sm["tinvs"], at(s))
                        dve.wait_ge(sm["wsels"], at(s))
                        one = vals[:, ds(U * g + s, 1), :, :].rearrange("p o n c -> p (o n) c")
                        dve.tensor_scalar(one[:, :, 1:3], wsel[:, s, :].rearrange("p (n e) -> p n e", e=2), tinv[:, s:s + 1],
                                          2.5, ALU.mult, ALU.mult).then_inc(sm["walls"], 1)
                        dve.tensor_copy(one[:, :, 0], token[:, ds(U * g + s, 1)].broadcast_to([P, NE // 2])).then_inc(sm["vals_made"], 1)
                    for s in range(U):
                        dve.wait_ge(sm["counted"], at(s))
                        dve.wait_ge(sm["before_made"], U * g + s + 1)
                        dve.tensor_tensor(before[:, (s + 1) % 2, :], before[:, s % 2, :], sel[:, s, :], ALU.add).then_inc(sm["before_made"], 1)
                        dve.tensor_scalar(pos[:, s, :], CN[:, s, 0:NE], 1.0, None, ALU.add).then_inc(sm["poss"], 1)
                    for s in range(U):
                        dve.wait_ge(sm["poss"], at(s))
                        o = dve.tensor_tensor(place[:, ds(U * g + s, 1), :].rearrange("p o e -> p (o e)"), pos[:, s, :],
                                              sel[:, s, :], ALU.mult)
                    o.then_inc(sm["trip_done"], 1)


def find_slots(nc, tag, A, place, vals, info):
    GE = 8
    NPG = GE // 2
    BF = mybir.dt.bfloat16
    NV = NT * NPAIRS * 3
    with Phase(nc, tag) as ph:
        slot1 = ph.sb("slot1", [P, GE, 64])
        R = 6
        hot = ph.sb("hot", [P, R, GE * CAP], BF)
        part = ph.sb("part", [P, NT, NPAIRS, 9], BF)
        rest1, rest2 = ph.sb("rest1", [P, NT, NPAIRS * 3]), ph.sb("rest2", [P, NT, NPAIRS * 3])
        zero = ph.sb("zero", [P, P], BF)
        pair_sum = ph.sb("pair_sum", [P, NPG, 3])
        IN = ph.ps("IN", [P, 2, 512])
        names = "loaded slots zeroed split hots used summed first_sum trip_done".split()
        sm = {n: ph.sem(n) for n in names}
        v3 = vals[:, :, :, :].rearrange("p t n c -> p (t n) c")
        p9 = part[:, :, :, :].rearrange("p t n c -> p (t n) c")
        r1, r2 = (r[:, :, :].rearrange("p t (n c) -> p (t n) c", c=3) for r in (rest1, rest2))
        with nc.Block() as block:
            @block.gpsimd
            def _(pool):
                pool.memset(zero[:, :], 0.0).then_inc(sm["zeroed"], 1)
                pool.iota(slot1[:, :, :], pattern=[[0, GE], [1, 64]], base=1, channel_multiplier=0,
                          allow_small_or_imprecise_dtypes=True).then_inc(sm["slots"], 1)

            @block.vector
            def _(dve):
                dve.sem_inc(sm["trip_done"], 1)
                dve.tensor_copy(p9[:, :, 0:3], v3).then_inc(sm["split"], 1)
                dve.wait_ge(sm["split"], 1)
                dve.tensor_tensor(r1, v3, p9[:, :, 0:3], ALU.subtract).then_inc(sm["split"], 1)
                dve.wait_ge(sm["split"], 2)
                dve.tensor_copy(p9[:, :, 3:6], r1).then_inc(sm["split"], 1)
                dve.wait_ge(sm["split"], 3)
                dve.tensor_tensor(r2, r1, p9[:, :, 3:6], ALU.subtract).then_inc(sm["split"], 1)
                dve.wait_ge(sm["split"], 4)
                dve.tensor_copy(p9[:, :, 6:9], r2).then_inc(sm["split"], 1)
                dve.wait_ge(sm["slots"], 1)
                with dve.Fori(0, NE // GE) as g:
                    for n in range(NT):
                        if n >= R:
                            dve.wait_ge(sm["used"], NT * g + n - R + 1)
                        else:
                            dve.wait_ge(sm["trip_done"], g + 1)
                        a = place[:, n, ds(g * GE, GE)].rearrange("p (e o) -> p e o", o=1).broadcast_to([P, GE, CAP])
                        dve.tensor_tensor(hot[:, n % R, :].rearrange("p (e c) -> p e c", e=GE), a, slot1[:, :, :],
                                          ALU.is_equal).then_inc(sm["hots"], 1)
                    dve.wait_ge(sm["summed"], g + 1)
                    tot = IN[:, 0, 0:9 * NPG].rearrange("p (n k c) -> p n k c", k=3, c=3)
                    dve.tensor_copy(pair_sum[:, :, :], tot[:, :, 2, :]).then_inc(sm["first_sum"], 1)
                    dve.wait_ge(sm["first_sum"], 2 * g + 1)
                    dve.tensor_tensor(pair_sum[:, :, :], tot[:, :, 1, :], pair_sum[:, :, :], ALU.add).then_inc(sm["first_sum"], 1)
                    dve.wait_ge(sm["first_sum"], 2 * g + 2)
                    dve.tensor_tensor(info[:, ds(g * NPG, NPG), :], tot[:, :, 0, :], pair_sum[:, :, :],
                                      ALU.add).then_inc(sm["trip_done"], 1)

            @block.tensor
            def _(pe):
                pe.wait_ge(sm["zeroed"], 1)
                pe.wait_ge(sm["split"], 5)
                with pe.Fori(0, NE // GE) as g:
                    pe.wait_ge(sm["trip_done"], g + 1)
                    pe.matmul(IN[:, 0, 0:9 * NPG], zero[:, :], zero[:, 0:9 * NPG], start=True, stop=True, skip_group_check=True)
                    for n in range(NT):
                        pe.wait_ge(sm["hots"], NT * g + n + 1)
                        for q in range(NPG):
                            o = pe.matmul(IN[:, 0, 9 * q:9 * q + 9], hot[:, n % R, q * P:(q + 1) * P],
                                          part[:, n, ds(g * NPG + q, 1), :].rearrange("p o c -> p (o c)"),
                                          start=False, stop=True, skip_group_check=True)
                        o.then_inc(sm["used"], 1)
                    pe.wait_ge(sm["used"], NT * g + NT)
                    pe.matmul(IN[:, 0, 0:9 * NPG], zero[:, :], zero[:, 0:9 * NPG], start=False, stop=True,
                              skip_group_check=True).then_inc(sm["summed"], 1)


def run_experts(nc, tag, A, W, ident, rows_dram, info, Eout):
    U = 4
    NPAIR = NE // 2
    with Phase(nc, tag) as ph:
        own = ph.sb("own", [P, P])
        tok = ph.sb("tok", [P, NPAIR], I32)
        ws = ph.sb("ws", [P, NPAIR])
        idx = ph.sb("idx", [P, U], I32)
        wgt, wut, wdt = ph.sb("wgt", [P, U, 2, 64]), ph.sb("wut", [P, U, 2, 64]), ph.sb("wdt", [P, U, P])
        xg, xT, gt, g2, hm = (ph.sb(n, [P, U, P]) for n in ("xg", "xT", "gt", "g2", "hm"))
        IO, GU = ph.ps("IO", [P, U, 512]), ph.ps("GU", [P, U, 512])
        names = ("loaded toks wss own_in idxs turned copied gu_made gated ups hids outs trip_done passed".split()
                 + [f"{what}{s}" for what in ("gathered", "weights") for s in range(U)])
        sm = {n: ph.sem(n) for n in names}
        gate_w = W["gate"].rearrange("(n e) h i -> n h e i", e=2)
        up_w = W["up"].rearrange("(n e) h i -> n h e i", e=2)
        down_w = W["down"].rearrange("(n e) i h -> n (e i) h", e=2)
        with nc.Block() as block:
            @block.sync
            def _(sp):
                load(sp, own[:, :], A["block64"], sm["own_in"])
                with sp.Fori(0, NPAIR // U) as g:
                    sp.wait_ge(sm["trip_done"], g + 1)
                    for s in range(U):
                        n = U * g + s
                        w = sm[f"weights{s}"]
                        load(sp, wgt[:, s, :, :], gate_w[ds(n, 1)].rearrange("o h e i -> h (o e) i"), w)
                        load(sp, wut[:, s, :, :], up_w[ds(n, 1)].rearrange("o h e i -> h (o e) i"), w)
                        load(sp, wdt[:, s, :], down_w[ds(n, 1)].rearrange("o p h -> (o p) h"), w)

            @block.gpsimd
            def _(pool):
                with pool.Fori(0, NPAIR // U) as g:
                    pool.wait_ge(sm["trip_done"], g + 1)
                    for s in range(U):
                        pool.wait_ge(sm["idxs"], U * g + s + 1)
                        pool.sem_inc(sm["passed"], 1)
                        pool.indirect_dma_start(out=xg[:, s, :], out_offset=None, in_=rows_dram[:, :],
                                                in_offset=bass.IndirectOffsetOnAxis(ap=idx[:, s:s + 1], axis=0)
                                                ).then_inc(sm[f"gathered{s}"], 16)

            @block.tensor
            def _(pe):
                with pe.Fori(0, NPAIR // U) as g:
                    for s in range(U):
                        pe.wait_ge(sm[f"gathered{s}"], 16 * g + 16)
                        pe.wait_ge(sm["trip_done"], g + 1)
                        pe.transpose(IO[:, s, 0:P], xg[:, s, :], ident[:, :]).then_inc(sm["turned"], 1)
                    for s in range(U):
                        pe.wait_ge(sm["copied"], U * g + s + 1)
                        pe.wait_ge(sm[f"weights{s}"], 48 * g + 48)
                        pe.matmul(GU[:, s, 0:P], wgt[:, s, :, :].rearrange("p e i -> p (e i)"), xT[:, s, :], start=True, stop=True)
                        pe.matmul(GU[:, s, P:2 * P], wut[:, s, :, :].rearrange("p e i -> p (e i)"), xT[:, s, :], start=True,
                                  stop=True).then_inc(sm["gu_made"], 1)
                    for s in range(U):
                        pe.wait_ge(sm["hids"], U * g + s + 1)
                        pe.matmul(IO[:, s, P:2 * P], hm[:, s, :], wdt[:, s, :], start=True, stop=True).then_inc(sm["outs"], 1)

            @block.scalar
            def _(act):
                with act.Fori(0, NPAIR // U) as g:
                    for s in range(U):
                        act.wait_ge(sm["turned"], U * g + s + 1)
                        act.wait_ge(sm["trip_done"], g + 1)
                        act.activation(xT[:, s, :], IO[:, s, 0:P], ACT.Copy).then_inc(sm["copied"], 1)
                    for s in range(U):
                        act.wait_ge(sm["gu_made"], U * g + s + 1)
                        act.activation(gt[:, s, :], GU[:, s, 0:P], ACT.Silu).then_inc(sm["gated"], 1)

            @block.vector
            def _(dve):
                dve.sem_inc(sm["trip_done"], 1)
                dve.tensor_copy(tok[:, :], info[:, :, 0]).then_inc(sm["toks"], 1)
                dve.tensor_copy(ws[0:64, :], info[0:64, :, 1])
                dve.tensor_copy(ws[64:P, :], info[64:P, :, 2]).then_inc(sm["wss"], 1)
                dve.wait_ge(sm["toks"], 1)
                dve.wait_ge(sm["wss"], 1)
                dve.wait_ge(sm["own_in"], 16)
                with dve.Fori(0, NPAIR // U) as g:
                    dve.wait_ge(sm["trip_done"], g + 1)
                    for s in range(U):
                        dve.tensor_copy(idx[:, s:s + 1], tok[:, ds(U * g + s, 1)]).then_inc(sm["idxs"], 1)
                    for s in range(U):
                        dve.wait_ge(sm["gated"], U * g + s + 1)
                        dve.tensor_tensor(g2[:, s, :], GU[:, s, P:2 * P], gt[:, s, :], ALU.mult).then_inc(sm["ups"], 1)
                    for s in range(U):
                        dve.wait_ge(sm["ups"], U * g + s + 1)
                        dve.tensor_tensor(hm[:, s, :], g2[:, s, :], own[:, :], ALU.mult).then_inc(sm["hids"], 1)
                    for s in range(U):
                        dve.wait_ge(sm["outs"], U * g + s + 1)
                        o = dve.tensor_scalar(Eout[:, ds(U * g + s, 1), :].rearrange("p o c -> p (o c)"), IO[:, s, P:2 * P],
                                              ws[:, ds(U * g + s, 1)], None, ALU.mult)
                    o.then_inc(sm["trip_done"], 1)


def combine(nc, tag, X, XN, W, info, Eout):
    NPAIR = NE // 2
    CH = 4
    NCH = NPAIR // CH
    BF = mybir.dt.bfloat16
    with Phase(nc, tag) as ph:
        lane = ph.sb("lane", [P, T])
        R = 4
        hot = ph.sb("hot", [P, R, BLK], BF)
        part = ph.sb("part", [P, 3, NPAIR, P], BF)
        rest = ph.sb("rest", [P, 2, NPAIR, P])
        sgw, suw, sdw = ph.sb("sgw", [P, 64]), ph.sb("suw", [P, 64]), ph.sb("sdw", [64, P])
        gt, hid = ph.sb("gt", [64, BLK]), ph.sb("hid", [64, BLK])
        SG, SU, OUT = ph.ps("SG", [P, 512]), ph.ps("SU", [P, 512]), ph.ps("OUT", [P, 512])
        names = ("loaded counted g_made u_made gated hids hots used out_made trip_done "
                 "part0 part1 part2 rest1 rest2").split()
        sm = {n: ph.sem(n) for n in names}

        def chunk(ap, c):
            return ap[:, c * CH:(c + 1) * CH, :].rearrange("p n c -> p (n c)")

        with nc.Block() as block:
            @block.sync
            def _(sp):
                for dst, n in ((sgw, "sgate"), (suw, "sup"), (sdw, "sdown")):
                    load(sp, dst[:, :], W[n], sm["loaded"])

            @block.gpsimd
            def _(pool):
                pool.iota(lane[:, :], pattern=[[1, T]], base=0, channel_multiplier=0,
                          allow_small_or_imprecise_dtypes=True).then_inc(sm["counted"], 1)
                for c in range(NCH + 1):
                    if c < NCH:
                        pool.wait_ge(sm["part0"], c + 1)
                        pool.tensor_tensor(chunk(rest[:, 0], c), chunk(Eout, c), chunk(part[:, 0], c), ALU.subtract).then_inc(sm["rest1"], 1)
                    if c >= 1:
                        pool.wait_ge(sm["part1"], c)
                        pool.tensor_tensor(chunk(rest[:, 1], c - 1), chunk(rest[:, 0], c - 1), chunk(part[:, 1], c - 1),
                                           ALU.subtract).then_inc(sm["rest2"], 1)

            @block.tensor
            def _(pe):
                pe.wait_ge(sm["loaded"], 48)
                with pe.Fori(0, NBLK) as g:
                    x = XN[:, ds(g * BLK, BLK)]
                    pe.wait_ge(sm["trip_done"], g + 1)
                    pe.matmul(SG[0:64, :], sgw[:, :], x, start=True, stop=True).then_inc(sm["g_made"], 1)
                    pe.matmul(SU[0:64, :], suw[:, :], x, start=True, stop=True).then_inc(sm["u_made"], 1)
                    for n in range(NPAIR):
                        pe.wait_ge(sm["hots"], NPAIR * g + n + 1)
                        if n % CH == 0:
                            pe.wait_ge(sm["part2"], n // CH + 1)
                        for k in range(3):
                            o = pe.matmul(OUT[:, :], part[:, k, n, :], hot[:, n % R, :], start=n == 0 and k == 0, stop=False)
                        o.then_inc(sm["used"], 1)
                    pe.wait_ge(sm["hids"], g + 1)
                    pe.matmul(OUT[:, :], sdw[:, :], hid[:, :], start=False, stop=True).then_inc(sm["out_made"], 1)

            @block.scalar
            def _(act):
                for c in range(NCH + 2):
                    if c < NCH:
                        act.activation(chunk(part[:, 0], c), chunk(Eout, c), ACT.Copy).then_inc(sm["part0"], 1)
                    if 0 <= c - 1 < NCH:
                        act.wait_ge(sm["rest1"], c)
                        act.activation(chunk(part[:, 1], c - 1), chunk(rest[:, 0], c - 1), ACT.Copy).then_inc(sm["part1"], 1)
                    if c >= 2:
                        act.wait_ge(sm["rest2"], c - 1)
                        act.activation(chunk(part[:, 2], c - 2), chunk(rest[:, 1], c - 2), ACT.Copy).then_inc(sm["part2"], 1)
                with act.Fori(0, NBLK) as g:
                    act.wait_ge(sm["g_made"], g + 1)
                    act.wait_ge(sm["trip_done"], g + 1)
                    act.activation(gt[:, :], SG[0:64, :], ACT.Silu).then_inc(sm["gated"], 1)

            @block.vector
            def _(dve):
                dve.sem_inc(sm["trip_done"], 1)
                dve.wait_ge(sm["counted"], 1)
                with dve.Fori(0, NBLK) as g:
                    at = ds(g * BLK, BLK)
                    for n in range(NPAIR):
                        if n >= R:
                            dve.wait_ge(sm["used"], NPAIR * g + n - R + 1)
                        else:
                            dve.wait_ge(sm["trip_done"], g + 1)
                        dve.tensor_scalar(hot[:, n % R, :], lane[:, at], info[:, n, 0:1], None, ALU.is_equal).then_inc(sm["hots"], 1)
                        if n == 4:
                            dve.wait_ge(sm["gated"], g + 1)
                            dve.wait_ge(sm["u_made"], g + 1)
                            dve.wait_ge(sm["trip_done"], g + 1)
                            dve.tensor_tensor(hid[:, :], SU[0:64, :], gt[:, :], ALU.mult).then_inc(sm["hids"], 1)
                    dve.wait_ge(sm["out_made"], g + 1)
                    dve.scalar_tensor_tensor(X[:, at], OUT[:, :], 0.5, X[:, at], ALU.mult, ALU.add).then_inc(sm["trip_done"], 1)


def build(nc, a, out):
    C = {n[2:]: v for n, v in a.items() if n.startswith("c_")}
    rows_dram = nc.dram_tensor("token_rows", (T, D), F32).ap()
    with ExitStack() as ctx:
        def sb(name, shape):
            return ctx.enter_context(nc.sbuf_tensor(name, shape, F32))

        X, XN = sb("X", [P, T]), sb("XN", [P, T + AHEAD])
        ident, ones_mean, eps = sb("ident", [P, P]), sb("ones_mean", [P, P]), sb("eps", [P, 1])
        with Phase(nc, "common") as ph:
            loaded = ph.sem("loaded")
            with nc.Block() as block:
                @block.sync
                def _(sp):
                    load(sp, ident[:, :], C["eye"], loaded)
                    load(sp, ones_mean[:, :], C["ones_mean"], loaded)
                    sp.wait_ge(loaded, 32)

                @block.vector
                def _(dve):
                    dve.memset(eps[:, :], LN_EPS)
                    dve.memset(XN[:, T:], 0.0)

        def norm(tag):
            layer_norm(nc, tag + "_norm", X, XN, ones_mean, eps)

        def pick(prefix, **names):
            return {k: a[prefix + v] for k, v in names.items()}

        def layer0_ffn(tag):
            norm(tag)
            product_key_experts(nc, tag, X, XN, C, pick("L0_ffn_", gamma="bn_gamma", beta="bn_beta", w_q="w_q",
                                                        keys="keys_p", down="down", up="up"), ident, eps)

        def layer1_ffn(tag):
            norm(tag)
            for n in range(2):
                w = {k: a["L1_ffn_" + k][n] for k in ("q", "k", "v", "q_crossed", "k_crossed", "qk_scale", "w1", "b1",
                                                      "w2", "b2", "ln_g", "ln_b")}
                w["o"] = a["L1_ffn_wo"][n].rearrange("(g p) d -> p g d", p=P)
                head_attention(nc, f"{tag}_att{n}", "win", XN, XN, C, w, ident)
                with nc.sbuf_tensor(f"{tag}_HX{n}", [P, T], F32) as HX:
                    layer_norm(nc, f"{tag}_ln{n}", XN, HX, ones_mean, eps, (w["ln_g"], w["ln_b"]))
                    gated_ffn(nc, f"{tag}_ff{n}", "gelu", XN, HX, w)
            add_half(nc, tag + "_add", X, XN)

        def layer2_ffn(tag):
            norm(tag)
            routed_experts(nc, tag, X, XN, C, pick("L2_ffn_", router="router_w", gate="gate_w", up="up_w", down="down_w",
                                                   sgate="shared_gate_w", sup="shared_up_w", sdown="shared_down_w"),
                           ident, rows_dram)

        def layer3_ffn(tag):
            norm(tag)
            gated_ffn(nc, tag, "int8", X, XN, pick("L3_ffn_", gate="w_gate", up="w_up", down="w_down"))

        enter_stream(nc, a["L0_attn_w"], X, ident)
        layer0_ffn("l0a")
        norm("l0att")
        head_attention(nc, "l0att", "rel", X, XN, C,
                       {"o": C["eye"], **pick("L0_attn_", q="Wq", k="Wk", v="Wv", r="Wr", r_crossed="Wr_crossed",
                                              u="u_bias", v_bias="v_bias")}, ident)
        layer0_ffn("l0b")
        layer1_ffn("l1a")
        norm("l1att")
        w = pick("L1_attn_", q="q", k="k", v="v", q_crossed="q_crossed", k_crossed="k_crossed", o="W_o")
        head_attention(nc, "l1att", "rope", X, XN, C, w, ident)
        layer1_ffn("l1b")
        layer2_ffn("l2a")
        norm("l2att")
        full_attention(nc, "l2att", X, XN, C, pick("L2_attn_", q="W_q", k="W_k", v="W_v", bias="bias"), ident)
        layer2_ffn("l2b")
        layer3_ffn("l3a")
        norm("l3att")
        latent_attention(nc, "l3att", X, XN, C, pick("L3_attn_", k="W_k", k_crossed="k_crossed", v="W_v", p="W_p", g="W_g",
                                                     q="latent_queries"), ident)
        layer3_ffn("l3b")
        leave_stream(nc, X, out, ident)


def laid_out(inputs):
    w = {n: np.asarray(v) for n, v in inputs.items()}
    a = {"L0_attn_w": w["L0_attn_w"]}

    def crossed(m, half):
        return m.reshape(-1, 2, half, m.shape[-1])[:, ::-1].reshape(m.shape)

    for n in ("Wq", "Wk", "Wv"):
        a["L0_attn_" + n] = w["L0_attn_" + n].T
    a["L0_attn_Wr"] = w["L0_attn_Wr"]
    a["L0_attn_Wr_crossed"] = crossed(w["L0_attn_Wr"].T, 1).T
    for n in ("u_bias", "v_bias"):
        a["L0_attn_" + n] = w["L0_attn_" + n].reshape(D, 1)
    for n in ("bn_gamma", "bn_beta", "w_q"):
        a["L0_ffn_" + n] = w["L0_ffn_" + n]
    a["L0_ffn_keys_p"] = w["L0_ffn_keys_p"].transpose(3, 2, 0, 1)
    a["L0_ffn_down"] = w["L0_ffn_down"][:1024].T
    a["L0_ffn_up"] = w["L0_ffn_up"][:1024]
    q, k, v = np.split(w["L1_attn_W_qkv"], 3, axis=0)
    a["L1_attn_q"], a["L1_attn_k"], a["L1_attn_v"] = q.T, k.T, v.T
    a["L1_attn_q_crossed"], a["L1_attn_k_crossed"] = crossed(q, 1).T, crossed(k, 1).T
    a["L1_attn_W_o"] = w["L1_attn_W_o"].T
    q, k, v = np.split(w["L1_ffn_wqkv"], 3, axis=2)
    a["L1_ffn_q"], a["L1_ffn_k"], a["L1_ffn_v"] = q, k, v
    for n, m in (("q", q), ("k", k)):
        a[f"L1_ffn_{n}_crossed"] = np.stack([crossed(x.T, 32).T for x in m])
    qs, ks = w["L1_ffn_q_scale"], w["L1_ffn_k_scale"]
    both = np.stack([qs, ks], axis=1)
    other = np.concatenate([both[:, :, 32:], both[:, :, :32]], axis=2)
    scales = np.stack([both, other], axis=1)
    a["L1_ffn_qk_scale"] = np.concatenate([scales, scales], axis=3).transpose(0, 3, 1, 2)
    for n in ("wo", "w1", "b1", "w2", "b2", "ln_g", "ln_b"):
        a["L1_ffn_" + n] = w["L1_ffn_" + n]
    for n in ("W_q", "W_k", "W_v"):
        a["L2_attn_" + n] = w["L2_attn_" + n]
    a["L2_attn_bias"] = np.stack([w["L2_attn_b_" + n] for n in "qkv"], axis=1)
    for n in ("router_w", "gate_w", "up_w", "down_w", "shared_gate_w", "shared_up_w", "shared_down_w"):
        a["L2_ffn_" + n] = w["L2_ffn_" + n]
    for n in ("W_k", "W_v", "W_p", "W_g"):
        a["L3_attn_" + n] = w["L3_attn_" + n].T
    a["L3_attn_k_crossed"] = crossed(w["L3_attn_W_k"], 1).T
    a["L3_attn_latent_queries"] = w["L3_attn_latent_queries"][0].transpose(1, 2, 0)
    for n in ("w_gate", "w_up", "w_down"):
        a["L3_ffn_" + n] = w["L3_ffn_" + n].T
    return a


def kernel(**inputs):
    import concourse.bacc as bacc
    from concourse.bass_utils import run_bass_kernel_spmd

    nc = bacc.Bacc("TRN2", target_bir_lowering=False, num_devices=1)
    arrays = {n: np.ascontiguousarray(v) for n, v in laid_out(inputs).items()}
    arrays.update({"c_" + n: v for n, v in constants().items()})
    tensors = {n: nc.dram_tensor(n, v.shape, mybir.dt.from_np(v.dtype), kind="ExternalInput").ap() for n, v in arrays.items()}
    out = nc.dram_tensor("out", (NB, L, D), F32, kind="ExternalOutput").ap()
    build(nc, tensors, out)
    r = run_bass_kernel_spmd(nc, [arrays], core_ids=[0])
    return r.results[0]["out"]
```
